# Optimizing a Trainium2 kernel written in Bass

```python
import numpy as np
import jax
import jax.numpy as jnp

def _softmax(x, axis=-1):
    return jax.nn.softmax(x, axis=axis)

def _gelu(x):
    return jax.nn.gelu(x, approximate=True)

def _silu(x):
    return jax.nn.silu(x)

def _sigmoid(x):
    return jax.nn.sigmoid(x)

def _layernorm(x, axis=-1, eps=1e-05):
    m = jnp.mean(x, axis=axis, keepdims=True)
    v = jnp.var(x, axis=axis, keepdims=True)
    return (x - m) / jnp.sqrt(v + eps)

def _scatter_add(tgt, idx, src, axis=0):
    return tgt.at[idx].add(src)

def _segment_sum(src, seg, n):
    return jax.ops.segment_sum(src, seg, n)
kernel_name = 'mk_decoder_preln_d4_seqx_r8_66ca7a'

def setup_inputs(seed: int=0):
    np.random.seed(seed)
    _w = jnp.asarray

    def _rec_inputs():
        import jax
        import jax.numpy as jnp
        _rk = jax.random.key(seed)
        x = -0.0002928 + 1 * jax.random.normal(jax.random.fold_in(_rk, 1), (1, 1024, 128), jnp.float32)
        _lenS = 1024 - jax.random.randint(jax.random.fold_in(_rk, 7), (1,), 0, max(1, 1024 // 4) + 1, jnp.int32)
        _lenS2 = 6404 - jax.random.randint(jax.random.fold_in(_rk, 8), (1,), 0, max(1, 6404 // 4) + 1, jnp.int32)
        _ctx_1024P = jax.random.normal(jax.random.fold_in(_rk, 11), (1, 16, 128), jnp.float32)
        _ctx_1024c = jax.random.dirichlet(jax.random.fold_in(_rk, 511), 0.3 * jnp.ones((16,), jnp.float32), (1, 6404))
        _ctx_1024t = jnp.einsum('bsk,bkd->bsd', _ctx_1024c, _ctx_1024P)
        _ctx_1024t = _ctx_1024t * jax.lax.rsqrt(jnp.mean(jnp.square(_ctx_1024t)) + 1e-12) * 0.953939
        ctx_1024 = 0.000227908 + 0.99994 * (_ctx_1024t + 0.3 * jax.random.normal(jax.random.fold_in(_rk, 611), (1, 6404, 128), jnp.float32))
        _validS = jnp.arange(1024)[None, :] < _lenS[:, None]
        _validS2 = jnp.arange(6404)[None, :] < _lenS2[:, None]
        _causal = jnp.tril(jnp.ones((1024, 1024), dtype=bool))
        mask_SxS_bc0 = jnp.logical_not(jnp.broadcast_to(_causal[:, :], (1024, 1024)))
        mask_BxSxS2_if1 = jnp.where(jnp.ones((1, 1024, 6404), dtype=bool), 1, 0).astype(jnp.int32)
        mask_BxS2_bk0 = jnp.logical_not(jnp.broadcast_to(_validS2[:, :], (1, 6404)))
        mask_BxS2_if0 = jnp.where(jnp.ones((1, 6404), dtype=bool), 0, 1).astype(jnp.int32)
        return (x, ctx_1024, mask_SxS_bc0, mask_BxSxS2_if1, mask_BxS2_bk0, mask_BxS2_if0)
    x, ctx_1024, mask_SxS_bc0, mask_BxSxS2_if1, mask_BxS2_bk0, mask_BxS2_if0 = _rec_inputs()

    def _L0_attn_setup():
        import jax, jax.numpy as jnp
        import numpy as np
        DIM = 128
        NUM_HEADS = 16
        NUM_KV_HEADS = 4
        HEAD_DIM = DIM // NUM_HEADS
        ROPE_BASE = 10000.0
        EPS = 1e-08
        BSZ, SEQ = (8, 128)

        def bitlinear(x, w, eps=EPS):
            alpha = jax.lax.stop_gradient(jnp.maximum(jnp.mean(jnp.abs(w)), eps))
            w_t = jnp.round(jnp.clip(w / alpha, -1.0, 1.0))
            w_q = w + jax.lax.stop_gradient(w_t * alpha - w)
            gamma = jax.lax.stop_gradient(jnp.maximum(jnp.max(jnp.abs(x), axis=-1, keepdims=True), eps) / 127.0)
            x_int = jnp.round(jnp.clip(x / gamma, -128.0, 127.0))
            x_q = x + jax.lax.stop_gradient(x_int * gamma - x)
            return x_q @ (w_q / alpha).T * alpha

        def rms_norm(x):
            eps = jnp.finfo(x.dtype).eps
            return x * jax.lax.rsqrt(jnp.mean(x * x, axis=-1, keepdims=True) + eps)

        def rope_cache(seq_len, head_dim, base):
            inv_freq = 1.0 / base ** (jnp.arange(0, head_dim, 2, dtype=jnp.float32) / head_dim)
            t = jnp.arange(seq_len, dtype=jnp.float32)
            freqs = jnp.outer(t, inv_freq)
            return (jnp.cos(freqs), jnp.sin(freqs))

        def apply_rotary(x, cos, sin):
            half = x.shape[-1] // 2
            x1, x2 = (x[..., :half], x[..., half:])
            return jnp.concatenate((x1 * cos + x2 * sin, -x1 * sin + x2 * cos), axis=-1)
        key = jax.random.key(seed)
        ks = jax.random.split(key, 6)
        x = jax.random.normal(ks[0], (BSZ, SEQ, DIM), dtype=jnp.float32)
        Wq = jax.random.normal(ks[1], (DIM, DIM), dtype=jnp.float32) * 0.02
        Wk = jax.random.normal(ks[2], (NUM_KV_HEADS * HEAD_DIM, DIM), dtype=jnp.float32) * 0.02
        Wv = jax.random.normal(ks[3], (NUM_KV_HEADS * HEAD_DIM, DIM), dtype=jnp.float32) * 0.02
        Wp = jax.random.normal(ks[4], (DIM, DIM), dtype=jnp.float32) * 0.02
        q_gain = jnp.ones((NUM_HEADS,), dtype=jnp.float32)
        return {'x': x, 'Wq': Wq, 'Wk': Wk, 'Wv': Wv, 'Wp': Wp, 'q_gain': q_gain}
    _L0_attn_all = _L0_attn_setup()
    _L0_attn_in = {k: v for k, v in _L0_attn_all.items() if k in ('Wq', 'Wk', 'Wv', 'Wp', 'q_gain')}
    del _L0_attn_all

    def _L0_xattn_setup():
        import jax, jax.numpy as jnp
        import numpy as np
        from jax import lax
        H = 16
        K1, K2 = (3, 3)
        LN_EPS = 1e-05

        def _ln(x, g, b):
            m = jnp.mean(x, axis=-1, keepdims=True)
            v = jnp.mean(jnp.square(x - m), axis=-1, keepdims=True)
            return (x - m) * lax.rsqrt(v + LN_EPS) * g + b

        def _gelu(x):
            return jax.nn.gelu(x, approximate=False)
        key = jax.random.key(seed)
        B, T, D, Th = (4, 128, 128, 32)
        C = 2 * D
        ks = jax.random.split(key, 16)

        def w(k, shape):
            fan_in = shape[0]
            return (jax.random.normal(k, shape, jnp.float32) / np.sqrt(fan_in)).astype(jnp.float32)
        inp = {'x': jax.random.normal(ks[0], (B, T, D), jnp.float32), 'historical_data': jax.random.normal(ks[1], (B, Th, D), jnp.float32), 'Wq': w(ks[2], (D, D)), 'Wk': w(ks[3], (D, D)), 'Wv': w(ks[4], (D, D)), 'hist_W': w(ks[5], (D, C)), 'hist_b': jnp.zeros((C,), jnp.float32), 'hist_ln_g': jnp.ones((C,), jnp.float32), 'hist_ln_b': jnp.zeros((C,), jnp.float32), 'ctx_W1': w(ks[6], (C, C // 4)), 'ctx_b1': jnp.zeros((C // 4,), jnp.float32), 'ctx_W2': w(ks[7], (C // 4, 1)), 'ctx_b2': jnp.zeros((1,), jnp.float32), 'kg_W1': w(ks[8], (C, D)), 'kg_b1': jnp.zeros((D,), jnp.float32), 'kg_ln_g': jnp.ones((D,), jnp.float32), 'kg_ln_b': jnp.zeros((D,), jnp.float32), 'kg_W2': w(ks[9], (D, H * K1 * K2)), 'kg_b2': jnp.zeros((H * K1 * K2,), jnp.float32), 'proj_W': w(ks[10], (D, D)), 'proj_b': jnp.zeros((D,), jnp.float32), 'causal_mask': jnp.triu(jnp.ones((T, T), bool), k=1)}
        return inp
    _L0_xattn_all = _L0_xattn_setup()
    _L0_xattn_in = {k: v for k, v in _L0_xattn_all.items() if k in ('Wq', 'Wk', 'Wv', 'hist_W', 'hist_b', 'hist_ln_g', 'hist_ln_b', 'ctx_W1', 'ctx_b1', 'ctx_W2', 'ctx_b2', 'kg_W1', 'kg_b1', 'kg_ln_g', 'kg_ln_b', 'kg_W2', 'kg_b2', 'proj_W', 'proj_b')}
    del _L0_xattn_all

    def _L0_ffn_setup():
        import jax, jax.numpy as jnp
        import numpy as np
        key = jax.random.key(seed)
        k0, k1, k2, k3 = jax.random.split(key, 4)
        B, S, D, F, E = (8, 256, 128, 256, 8)
        x = jax.random.normal(k0, (B, S, D), dtype=jnp.float32)
        Wg = jax.random.normal(k1, (D, E), dtype=jnp.float32) * 0.02
        W1 = jax.random.normal(k2, (E, D, F), dtype=jnp.float32) * 0.02
        W2 = jax.random.normal(k3, (E, F, D), dtype=jnp.float32) * 0.02
        return {'x': x, 'Wg': Wg, 'W1': W1, 'W2': W2}
    _L0_ffn_all = _L0_ffn_setup()
    _L0_ffn_in = {k: v for k, v in _L0_ffn_all.items() if k in ('Wg', 'W1', 'W2')}
    del _L0_ffn_all

    def _L1_attn_setup():
        import jax, jax.numpy as jnp
        import numpy as np
        EPS = 1e-08
        LOG_INIT = -1e+38

        def wkv_log_space(w, u, k, v, ln_a_p0, ln_a_m0, ln_b0):

            def step(carry, kv):
                ln_a_p, ln_a_m, ln_b = carry
                kt, vt = kv
                ln_v_p = jnp.log(jnp.maximum(vt, 0.0) + EPS)
                ln_v_m = jnp.log(jnp.maximum(-vt, 0.0) + EPS)
                uk = u + kt
                ln_den = jnp.logaddexp(uk, ln_b)
                wkv = jnp.exp(jnp.logaddexp(uk + ln_v_p, ln_a_p) - ln_den) - jnp.exp(jnp.logaddexp(uk + ln_v_m, ln_a_m) - ln_den)
                ln_a_p = jnp.logaddexp(ln_a_p - w, kt + ln_v_p)
                ln_a_m = jnp.logaddexp(ln_a_m - w, kt + ln_v_m)
                ln_b = jnp.logaddexp(ln_b - w, kt)
                return ((ln_a_p, ln_a_m, ln_b), wkv)
            kT = jnp.swapaxes(k, 0, 1)
            vT = jnp.swapaxes(v, 0, 1)
            _, wkv = jax.lax.scan(step, (ln_a_p0, ln_a_m0, ln_b0), (kT, vT))
            return jnp.swapaxes(wkv, 0, 1)
        key = jax.random.key(seed)
        B, T, D = (4, 512, 128)
        ks = jax.random.split(key, 10)
        s = 1.0 / np.sqrt(D)
        return {'x': jax.random.normal(ks[0], (B, T, D), jnp.float32), 'time_decay': jax.random.normal(ks[1], (D,), jnp.float32) * 0.5, 'time_first': jax.random.normal(ks[2], (D,), jnp.float32) * 0.5, 'time_mix_k': jax.random.uniform(ks[3], (1, 1, D), jnp.float32), 'time_mix_v': jax.random.uniform(ks[4], (1, 1, D), jnp.float32), 'time_mix_r': jax.random.uniform(ks[5], (1, 1, D), jnp.float32), 'W_key': jax.random.normal(ks[6], (D, D), jnp.float32) * s, 'W_value': jax.random.normal(ks[7], (D, D), jnp.float32) * s, 'W_receptance': jax.random.normal(ks[8], (D, D), jnp.float32) * s, 'W_output': jax.random.normal(ks[9], (D, D), jnp.float32) * s}
    _L1_attn_all = _L1_attn_setup()
    _L1_attn_in = {k: v for k, v in _L1_attn_all.items() if k in ('time_decay', 'time_first', 'time_mix_k', 'time_mix_v', 'time_mix_r', 'W_key', 'W_value', 'W_receptance', 'W_output')}
    del _L1_attn_all

    def _L1_xattn_setup():
        import jax, jax.numpy as jnp
        import numpy as np
        H = 16
        key = jax.random.key(seed)
        ks = jax.random.split(key, 8)
        B, T, D = (4, 256, 128)
        s = 0.02
        return {'query': jax.random.normal(ks[0], (B, T, D), jnp.float32), 'key': jax.random.normal(ks[1], (B, T, D), jnp.float32), 'value': jax.random.normal(ks[2], (B, T, D), jnp.float32), 'mask': jnp.ones((B, T, T), jnp.int32), 'Wq': jax.random.normal(ks[3], (D, D), jnp.float32) * s, 'Wk': jax.random.normal(ks[4], (D, D), jnp.float32) * s, 'Wv': jax.random.normal(ks[5], (D, D), jnp.float32) * s, 'Wo': jax.random.normal(ks[6], (D, D), jnp.float32) * s, 'bo': jnp.zeros((D,), jnp.float32)}
    _L1_xattn_all = _L1_xattn_setup()
    _L1_xattn_in = {k: v for k, v in _L1_xattn_all.items() if k in ('Wq', 'Wk', 'Wv', 'Wo', 'bo')}
    del _L1_xattn_all

    def _L1_ffn_setup():
        import jax, jax.numpy as jnp
        import numpy as np
        HIDDEN = 128
        INTER = 512
        key = jax.random.key(seed)
        k1, k2, k3, k4, k5 = jax.random.split(key, 5)
        hidden_states = jax.random.normal(k1, (4, 256, HIDDEN), dtype=jnp.float32)
        W1 = jax.random.normal(k2, (HIDDEN, INTER), dtype=jnp.float32) * (1.0 / np.sqrt(HIDDEN))
        b1 = jax.random.normal(k3, (INTER,), dtype=jnp.float32) * 0.02
        W2 = jax.random.normal(k4, (INTER, HIDDEN), dtype=jnp.float32) * (1.0 / np.sqrt(INTER))
        b2 = jax.random.normal(k5, (HIDDEN,), dtype=jnp.float32) * 0.02
        return {'hidden_states': hidden_states, 'W1': W1, 'b1': b1, 'W2': W2, 'b2': b2}
    _L1_ffn_all = _L1_ffn_setup()
    _L1_ffn_in = {k: v for k, v in _L1_ffn_all.items() if k in ('W1', 'b1', 'W2', 'b2')}
    del _L1_ffn_all

    def _L2_attn_setup():
        import jax, jax.numpy as jnp
        import numpy as np
        HEADS = 8
        BLOCK = 32
        key = jax.random.key(seed)
        ks = jax.random.split(key, 4)
        b, n, d, f = (4, 512, 128, 128)
        x = jax.random.normal(ks[0], (b, n, d), dtype=jnp.float32)
        w_qkv = jax.random.normal(ks[1], (3 * d, d), dtype=jnp.float32) * d ** (-0.5)
        w_out = jax.random.normal(ks[2], (d, d), dtype=jnp.float32) * d ** (-0.5)
        b_out = jnp.zeros((d,), dtype=jnp.float32)
        proj = jax.random.normal(ks[3], (HEADS, d // HEADS, f), dtype=jnp.float32) * (d // HEADS) ** (-0.5)
        return {'x': x, 'w_qkv': w_qkv, 'w_out': w_out, 'b_out': b_out, 'proj': proj}
    _L2_attn_all = _L2_attn_setup()
    _L2_attn_in = {k: v for k, v in _L2_attn_all.items() if k in ('w_qkv', 'w_out', 'b_out', 'proj')}
    del _L2_attn_all

    def _L2_xattn_setup():
        import jax, jax.numpy as jnp
        import numpy as np
        DIM = 128
        HEADS = 16
        HEAD_DIM = DIM // HEADS
        B, N, S = (4, 512, 64)
        key = jax.random.key(seed)
        ks = jax.random.split(key, 9)
        scale = DIM ** (-0.5)
        return {'x': jax.random.normal(ks[0], (B, N, DIM), dtype=jnp.float32), 'context': jax.random.normal(ks[1], (B, S, DIM), dtype=jnp.float32), 'context_mask': jax.random.uniform(ks[2], (B, S)) < 0.2, 'q_w': jax.random.normal(ks[3], (DIM, DIM), dtype=jnp.float32) * scale, 'q_b': jnp.zeros((DIM,), dtype=jnp.float32), 'kv_w': jax.random.normal(ks[4], (DIM, 2 * DIM), dtype=jnp.float32) * scale, 'kv_b': jnp.zeros((2 * DIM,), dtype=jnp.float32), 'proj_w': jax.random.normal(ks[5], (DIM, DIM), dtype=jnp.float32) * scale, 'proj_b': jnp.zeros((DIM,), dtype=jnp.float32)}
    _L2_xattn_all = _L2_xattn_setup()
    _L2_xattn_in = {k: v for k, v in _L2_xattn_all.items() if k in ('q_w', 'q_b', 'kv_w', 'kv_b', 'proj_w', 'proj_b')}
    del _L2_xattn_all

    def _L2_ffn_setup():
        import jax, jax.numpy as jnp
        import numpy as np
        D = 128
        I = 64
        E = 32
        K = 4
        T = 2 * 256
        C = 2 * T * K // E
        key = jax.random.key(seed)
        ks = jax.random.split(key, 9)
        bf = jnp.bfloat16
        std = 0.02
        x = jax.random.normal(ks[0], (2, 256, D), dtype=jnp.float32).astype(bf)
        gate_w = (std * jax.random.normal(ks[1], (E, D), dtype=jnp.float32)).astype(bf)
        bias = jnp.zeros((E,), jnp.float32)
        W1 = (std * jax.random.normal(ks[2], (E, D, I), dtype=jnp.float32)).astype(bf)
        W3 = (std * jax.random.normal(ks[3], (E, D, I), dtype=jnp.float32)).astype(bf)
        W2 = (std * jax.random.normal(ks[4], (E, I, D), dtype=jnp.float32)).astype(bf)
        sw1 = (std * jax.random.normal(ks[5], (I, D), dtype=jnp.float32)).astype(bf)
        sw3 = (std * jax.random.normal(ks[6], (I, D), dtype=jnp.float32)).astype(bf)
        sw2 = (std * jax.random.normal(ks[7], (D, I), dtype=jnp.float32)).astype(bf)
        return {'x': x, 'gate_w': gate_w, 'bias': bias, 'W1': W1, 'W3': W3, 'W2': W2, 'sw1': sw1, 'sw3': sw3, 'sw2': sw2}
    _L2_ffn_all = _L2_ffn_setup()
    _L2_ffn_in = {k: v for k, v in _L2_ffn_all.items() if k in ('gate_w', 'bias', 'W1', 'W3', 'W2', 'sw1', 'sw3', 'sw2')}
    del _L2_ffn_all

    def _L3_attn_setup():
        import jax, jax.numpy as jnp
        import numpy as np
        L, D, F, H = (4, 128, 256, 8)
        DH = D // H
        EPS = 1e-05

        def _layer_norm(x, scale, bias):
            mu = x.mean(-1, keepdims=True)
            var = x.var(-1, keepdims=True)
            return (x - mu) * jax.lax.rsqrt(var + EPS) * scale + bias

        def _rotate(x, cos, sin):
            x1, x2 = (x[..., 0::2], x[..., 1::2])
            r1 = x1 * cos - x2 * sin
            r2 = x1 * sin + x2 * cos
            return jnp.stack([r1, r2], axis=-1).reshape(x.shape)

        def _decay_matrix(S):
            gammas = 1.0 - jnp.exp(jnp.linspace(np.log(1 / 32), np.log(1 / 64), H)).astype(jnp.float32)
            n = jnp.arange(S)
            diff = (n[:, None] - n[None, :]).astype(jnp.float32)
            pw = jnp.exp(jnp.clip(diff, 0.0)[None] * jnp.log(gammas)[:, None, None])
            return jnp.where(diff[None] >= 0, pw, 0.0)

        def _retention(x, Wq, Wk, Wv, Wg, Wo, gn_s, gn_b, Dm, cos, sin):
            B, S, _ = x.shape
            Q = (x @ Wq).reshape(B, S, H, DH)
            K = (x @ Wk).reshape(B, S, H, DH)
            V = (x @ Wv).reshape(B, S, H, DH)
            Q = _rotate(Q, cos, sin)
            K = _rotate(K, cos, -sin)
            att = jnp.einsum('bnhd,bmhd->bhnm', Q, K) * Dm
            Y = jnp.einsum('bhnm,bmhd->bnhd', att, V)
            mu = Y.mean(-1, keepdims=True)
            var = Y.var(-1, keepdims=True)
            Y = (Y - mu) * jax.lax.rsqrt(var + EPS)
            Y = Y.reshape(B, S, D) * gn_s + gn_b
            G = jax.nn.swish(x @ Wg)
            return G * Y @ Wo
        key = jax.random.key(seed)
        ks = jax.random.split(key, 8)
        B, S = (4, 128)
        sd = 1.0 / np.sqrt(D)
        sf = 1.0 / np.sqrt(F)
        return {'X': jax.random.normal(ks[0], (B, S, D), jnp.float32), 'Wq': jax.random.normal(ks[1], (L, D, D), jnp.float32) * sd, 'Wk': jax.random.normal(ks[2], (L, D, D), jnp.float32) * sd, 'Wv': jax.random.normal(ks[3], (L, D, D), jnp.float32) * sd, 'Wg': jax.random.normal(ks[4], (L, D, D), jnp.float32) * sd, 'Wo': jax.random.normal(ks[5], (L, D, D), jnp.float32) * sd, 'W1': jax.random.normal(ks[6], (L, D, F), jnp.float32) * sd, 'W2': jax.random.normal(ks[7], (L, F, D), jnp.float32) * sf, 'ln_scale': jnp.ones((D,), jnp.float32), 'ln_bias': jnp.zeros((D,), jnp.float32), 'gn_scale': jnp.ones((L, D), jnp.float32), 'gn_bias': jnp.zeros((L, D), jnp.float32)}
    _L3_attn_all = _L3_attn_setup()
    _L3_attn_in = {k: v for k, v in _L3_attn_all.items() if k in ('Wq', 'Wk', 'Wv', 'Wg', 'Wo', 'W1', 'W2', 'ln_scale', 'ln_bias', 'gn_scale', 'gn_bias')}
    del _L3_attn_all

    def _L3_xattn_setup():
        import jax, jax.numpy as jnp
        import numpy as np
        import math
        B, M, D, H, NK = (4, 256, 128, 16, 5)
        HD = D // H

        def _gather_pad0(x, idx):
            Bx, Hx, W, hd = x.shape
            valid = (idx >= 0) & (idx < W)
            idxc = jnp.clip(idx, 0, W - 1).reshape(Bx, Hx, -1)
            g = jnp.take_along_axis(x, idxc[..., None], axis=2)
            g = g.reshape(idx.shape + (hd,))
            return g * valid[..., None].astype(x.dtype)
        key = jax.random.key(seed)
        ks = jax.random.split(key, 9)
        w = lambda k, shape: jax.random.normal(k, shape, jnp.float32) * 0.02
        return {'k': jax.random.normal(ks[0], (B, M, D), jnp.float32), 'v': jax.random.normal(ks[1], (B, M, D), jnp.float32), 'q': jax.random.normal(ks[2], (B, M, D), jnp.float32), 'mask': jnp.zeros((B, M), jnp.int32), 'Wk': w(ks[3], (D, D)), 'bk': jnp.zeros((D,), jnp.float32), 'Wv': w(ks[4], (D, D)), 'bv': jnp.zeros((D,), jnp.float32), 'Wq': w(ks[5], (D, D)), 'bq': jnp.zeros((D,), jnp.float32), 'Woff': w(ks[6], (H * NK, D)), 'boff': jnp.zeros((H * NK,), jnp.float32), 'Wo': w(ks[7], (D, D)), 'bo': jnp.zeros((D,), jnp.float32)}
    _L3_xattn_all = _L3_xattn_setup()
    _L3_xattn_in = {k: v for k, v in _L3_xattn_all.items() if k in ('Wk', 'bk', 'Wv', 'bv', 'Wq', 'bq', 'Woff', 'boff', 'Wo', 'bo')}
    del _L3_xattn_all

    def _L3_ffn_setup():
        import jax, jax.numpy as jnp
        import numpy as np
        HIDDEN = 128
        NUM_EXPERTS = 8
        TOP_K = 2
        B, S = (2, 256)
        key = jax.random.key(seed)
        k1, k2, k3, k4, k5 = jax.random.split(key, 5)
        d, dff, E = (HIDDEN, 4 * HIDDEN, NUM_EXPERTS)
        x = jax.random.normal(k1, (B, S, d), dtype=jnp.float32)
        W1 = jax.random.normal(k2, (E, d, dff), dtype=jnp.float32) * (1.0 / np.sqrt(d))
        b1 = jax.random.normal(k3, (E, dff), dtype=jnp.float32) * 0.01
        W2 = jax.random.normal(k4, (E, dff, d), dtype=jnp.float32) * (1.0 / np.sqrt(dff))
        b2 = jax.random.normal(k5, (E, d), dtype=jnp.float32) * 0.01
        return {'x': x, 'W1': W1, 'b1': b1, 'W2': W2, 'b2': b2}
    _L3_ffn_all = _L3_ffn_setup()
    _L3_ffn_in = {k: v for k, v in _L3_ffn_all.items() if k in ('W1', 'b1', 'W2', 'b2')}
    del _L3_ffn_all
    return {'x': x, 'ctx_1024': ctx_1024, 'mask_SxS_bc0': mask_SxS_bc0, 'mask_BxSxS2_if1': mask_BxSxS2_if1, 'mask_BxS2_bk0': mask_BxS2_bk0, 'mask_BxS2_if0': mask_BxS2_if0, 'L0_attn_Wq': _L0_attn_in['Wq'], 'L0_attn_Wk': _L0_attn_in['Wk'], 'L0_attn_Wv': _L0_attn_in['Wv'], 'L0_attn_Wp': _L0_attn_in['Wp'], 'L0_attn_q_gain': _L0_attn_in['q_gain'], 'L0_xattn_Wq': _L0_xattn_in['Wq'], 'L0_xattn_Wk': _L0_xattn_in['Wk'], 'L0_xattn_Wv': _L0_xattn_in['Wv'], 'L0_xattn_hist_W': _L0_xattn_in['hist_W'], 'L0_xattn_hist_b': _L0_xattn_in['hist_b'], 'L0_xattn_hist_ln_g': _L0_xattn_in['hist_ln_g'], 'L0_xattn_hist_ln_b': _L0_xattn_in['hist_ln_b'], 'L0_xattn_ctx_W1': _L0_xattn_in['ctx_W1'], 'L0_xattn_ctx_b1': _L0_xattn_in['ctx_b1'], 'L0_xattn_ctx_W2': _L0_xattn_in['ctx_W2'], 'L0_xattn_ctx_b2': _L0_xattn_in['ctx_b2'], 'L0_xattn_kg_W1': _L0_xattn_in['kg_W1'], 'L0_xattn_kg_b1': _L0_xattn_in['kg_b1'], 'L0_xattn_kg_ln_g': _L0_xattn_in['kg_ln_g'], 'L0_xattn_kg_ln_b': _L0_xattn_in['kg_ln_b'], 'L0_xattn_kg_W2': _L0_xattn_in['kg_W2'], 'L0_xattn_kg_b2': _L0_xattn_in['kg_b2'], 'L0_xattn_proj_W': _L0_xattn_in['proj_W'], 'L0_xattn_proj_b': _L0_xattn_in['proj_b'], 'L0_ffn_Wg': _L0_ffn_in['Wg'], 'L0_ffn_W1': _L0_ffn_in['W1'], 'L0_ffn_W2': _L0_ffn_in['W2'], 'L1_attn_time_decay': _L1_attn_in['time_decay'], 'L1_attn_time_first': _L1_attn_in['time_first'], 'L1_attn_time_mix_k': _L1_attn_in['time_mix_k'], 'L1_attn_time_mix_v': _L1_attn_in['time_mix_v'], 'L1_attn_time_mix_r': _L1_attn_in['time_mix_r'], 'L1_attn_W_key': _L1_attn_in['W_key'], 'L1_attn_W_value': _L1_attn_in['W_value'], 'L1_attn_W_receptance': _L1_attn_in['W_receptance'], 'L1_attn_W_output': _L1_attn_in['W_output'], 'L1_xattn_Wq': _L1_xattn_in['Wq'], 'L1_xattn_Wk': _L1_xattn_in['Wk'], 'L1_xattn_Wv': _L1_xattn_in['Wv'], 'L1_xattn_Wo': _L1_xattn_in['Wo'], 'L1_xattn_bo': _L1_xattn_in['bo'], 'L1_ffn_W1': _L1_ffn_in['W1'], 'L1_ffn_b1': _L1_ffn_in['b1'], 'L1_ffn_W2': _L1_ffn_in['W2'], 'L1_ffn_b2': _L1_ffn_in['b2'], 'L2_attn_w_qkv': _L2_attn_in['w_qkv'], 'L2_attn_w_out': _L2_attn_in['w_out'], 'L2_attn_b_out': _L2_attn_in['b_out'], 'L2_attn_proj': _L2_attn_in['proj'], 'L2_xattn_q_w': _L2_xattn_in['q_w'], 'L2_xattn_q_b': _L2_xattn_in['q_b'], 'L2_xattn_kv_w': _L2_xattn_in['kv_w'], 'L2_xattn_kv_b': _L2_xattn_in['kv_b'], 'L2_xattn_proj_w': _L2_xattn_in['proj_w'], 'L2_xattn_proj_b': _L2_xattn_in['proj_b'], 'L2_ffn_gate_w': _L2_ffn_in['gate_w'], 'L2_ffn_bias': _L2_ffn_in['bias'], 'L2_ffn_W1': _L2_ffn_in['W1'], 'L2_ffn_W3': _L2_ffn_in['W3'], 'L2_ffn_W2': _L2_ffn_in['W2'], 'L2_ffn_sw1': _L2_ffn_in['sw1'], 'L2_ffn_sw3': _L2_ffn_in['sw3'], 'L2_ffn_sw2': _L2_ffn_in['sw2'], 'L3_attn_Wq': _L3_attn_in['Wq'], 'L3_attn_Wk': _L3_attn_in['Wk'], 'L3_attn_Wv': _L3_attn_in['Wv'], 'L3_attn_Wg': _L3_attn_in['Wg'], 'L3_attn_Wo': _L3_attn_in['Wo'], 'L3_attn_W1': _L3_attn_in['W1'], 'L3_attn_W2': _L3_attn_in['W2'], 'L3_attn_ln_scale': _L3_attn_in['ln_scale'], 'L3_attn_ln_bias': _L3_attn_in['ln_bias'], 'L3_attn_gn_scale': _L3_attn_in['gn_scale'], 'L3_attn_gn_bias': _L3_attn_in['gn_bias'], 'L3_xattn_Wk': _L3_xattn_in['Wk'], 'L3_xattn_bk': _L3_xattn_in['bk'], 'L3_xattn_Wv': _L3_xattn_in['Wv'], 'L3_xattn_bv': _L3_xattn_in['bv'], 'L3_xattn_Wq': _L3_xattn_in['Wq'], 'L3_xattn_bq': _L3_xattn_in['bq'], 'L3_xattn_Woff': _L3_xattn_in['Woff'], 'L3_xattn_boff': _L3_xattn_in['boff'], 'L3_xattn_Wo': _L3_xattn_in['Wo'], 'L3_xattn_bo': _L3_xattn_in['bo'], 'L3_ffn_W1': _L3_ffn_in['W1'], 'L3_ffn_b1': _L3_ffn_in['b1'], 'L3_ffn_W2': _L3_ffn_in['W2'], 'L3_ffn_b2': _L3_ffn_in['b2']}

def reference(x, ctx_1024, mask_SxS_bc0, mask_BxSxS2_if1, mask_BxS2_bk0, mask_BxS2_if0, L0_attn_Wq, L0_attn_Wk, L0_attn_Wv, L0_attn_Wp, L0_attn_q_gain, L0_xattn_Wq, L0_xattn_Wk, L0_xattn_Wv, L0_xattn_hist_W, L0_xattn_hist_b, L0_xattn_hist_ln_g, L0_xattn_hist_ln_b, L0_xattn_ctx_W1, L0_xattn_ctx_b1, L0_xattn_ctx_W2, L0_xattn_ctx_b2, L0_xattn_kg_W1, L0_xattn_kg_b1, L0_xattn_kg_ln_g, L0_xattn_kg_ln_b, L0_xattn_kg_W2, L0_xattn_kg_b2, L0_xattn_proj_W, L0_xattn_proj_b, L0_ffn_Wg, L0_ffn_W1, L0_ffn_W2, L1_attn_time_decay, L1_attn_time_first, L1_attn_time_mix_k, L1_attn_time_mix_v, L1_attn_time_mix_r, L1_attn_W_key, L1_attn_W_value, L1_attn_W_receptance, L1_attn_W_output, L1_xattn_Wq, L1_xattn_Wk, L1_xattn_Wv, L1_xattn_Wo, L1_xattn_bo, L1_ffn_W1, L1_ffn_b1, L1_ffn_W2, L1_ffn_b2, L2_attn_w_qkv, L2_attn_w_out, L2_attn_b_out, L2_attn_proj, L2_xattn_q_w, L2_xattn_q_b, L2_xattn_kv_w, L2_xattn_kv_b, L2_xattn_proj_w, L2_xattn_proj_b, L2_ffn_gate_w, L2_ffn_bias, L2_ffn_W1, L2_ffn_W3, L2_ffn_W2, L2_ffn_sw1, L2_ffn_sw3, L2_ffn_sw2, L3_attn_Wq, L3_attn_Wk, L3_attn_Wv, L3_attn_Wg, L3_attn_Wo, L3_attn_W1, L3_attn_W2, L3_attn_ln_scale, L3_attn_ln_bias, L3_attn_gn_scale, L3_attn_gn_bias, L3_xattn_Wk, L3_xattn_bk, L3_xattn_Wv, L3_xattn_bv, L3_xattn_Wq, L3_xattn_bq, L3_xattn_Woff, L3_xattn_boff, L3_xattn_Wo, L3_xattn_bo, L3_ffn_W1, L3_ffn_b1, L3_ffn_W2, L3_ffn_b2):
    import jax
    import jax.numpy as jnp

    def _L0_attn_ref(x, Wq, Wk, Wv, Wp, q_gain):
        import jax, jax.numpy as jnp
        import numpy as np
        DIM = 128
        NUM_HEADS = 16
        NUM_KV_HEADS = 4
        HEAD_DIM = DIM // NUM_HEADS
        ROPE_BASE = 10000.0
        EPS = 1e-08
        BSZ, SEQ = (8, 128)

        def bitlinear(x, w, eps=EPS):
            alpha = jax.lax.stop_gradient(jnp.maximum(jnp.mean(jnp.abs(w)), eps))
            w_t = jnp.round(jnp.clip(w / alpha, -1.0, 1.0))
            w_q = w + jax.lax.stop_gradient(w_t * alpha - w)
            gamma = jax.lax.stop_gradient(jnp.maximum(jnp.max(jnp.abs(x), axis=-1, keepdims=True), eps) / 127.0)
            x_int = jnp.round(jnp.clip(x / gamma, -128.0, 127.0))
            x_q = x + jax.lax.stop_gradient(x_int * gamma - x)
            return x_q @ (w_q / alpha).T * alpha

        def rms_norm(x):
            eps = jnp.finfo(x.dtype).eps
            return x * jax.lax.rsqrt(jnp.mean(x * x, axis=-1, keepdims=True) + eps)

        def rope_cache(seq_len, head_dim, base):
            inv_freq = 1.0 / base ** (jnp.arange(0, head_dim, 2, dtype=jnp.float32) / head_dim)
            t = jnp.arange(seq_len, dtype=jnp.float32)
            freqs = jnp.outer(t, inv_freq)
            return (jnp.cos(freqs), jnp.sin(freqs))

        def apply_rotary(x, cos, sin):
            half = x.shape[-1] // 2
            x1, x2 = (x[..., :half], x[..., half:])
            return jnp.concatenate((x1 * cos + x2 * sin, -x1 * sin + x2 * cos), axis=-1)
        bsz, seqlen, dim = x.shape
        q = bitlinear(x, Wq).reshape(bsz, seqlen, NUM_HEADS, HEAD_DIM).transpose(0, 2, 1, 3)
        k = bitlinear(x, Wk).reshape(bsz, seqlen, NUM_KV_HEADS, HEAD_DIM).transpose(0, 2, 1, 3)
        v = bitlinear(x, Wv).reshape(bsz, seqlen, NUM_KV_HEADS, HEAD_DIM).transpose(0, 2, 1, 3)
        q = rms_norm(q)
        k = rms_norm(k)
        cos, sin = rope_cache(seqlen, HEAD_DIM, ROPE_BASE)
        q = apply_rotary(q, cos, sin)
        k = apply_rotary(k, cos, sin)
        q = q * q_gain[None, :, None, None]
        rep = NUM_HEADS // NUM_KV_HEADS
        k = jnp.repeat(k, rep, axis=1)
        v = jnp.repeat(v, rep, axis=1)
        scale = 1.0 / jnp.sqrt(jnp.float32(HEAD_DIM))
        scores = jnp.einsum('bhqd,bhkd->bhqk', q, k) * scale
        causal = jnp.tril(jnp.ones((seqlen, seqlen), dtype=bool))
        scores = jnp.where(causal, scores, jnp.finfo(scores.dtype).min)
        attn = jax.nn.softmax(scores, axis=-1)
        y = jnp.einsum('bhqk,bhkd->bhqd', attn, v)
        y = y.transpose(0, 2, 1, 3).reshape(bsz, seqlen, dim)
        return bitlinear(y, Wp)

    def _L0_xattn_ref(x, historical_data, Wq, Wk, Wv, hist_W, hist_b, hist_ln_g, hist_ln_b, ctx_W1, ctx_b1, ctx_W2, ctx_b2, kg_W1, kg_b1, kg_ln_g, kg_ln_b, kg_W2, kg_b2, proj_W, proj_b, causal_mask):
        import jax, jax.numpy as jnp
        import numpy as np
        from jax import lax
        H = 16
        K1, K2 = (3, 3)
        LN_EPS = 1e-05

        def _ln(x, g, b):
            m = jnp.mean(x, axis=-1, keepdims=True)
            v = jnp.mean(jnp.square(x - m), axis=-1, keepdims=True)
            return (x - m) * lax.rsqrt(v + LN_EPS) * g + b

        def _gelu(x):
            return jax.nn.gelu(x, approximate=False)
        B, T, D = x.shape
        hd = D // H
        scale = hd ** (-0.5)
        q = (x @ Wq).reshape(B, T, H, hd).transpose(0, 2, 1, 3)
        k = (x @ Wk).reshape(B, T, H, hd).transpose(0, 2, 1, 3)
        v = (x @ Wv).reshape(B, T, H, hd).transpose(0, 2, 1, 3)
        attn = jnp.einsum('bhqd,bhkd->bhqk', q, k) * scale
        eh = _gelu(_ln(historical_data @ hist_W + hist_b, hist_ln_g, hist_ln_b))
        aw = _gelu(eh @ ctx_W1 + ctx_b1) @ ctx_W2 + ctx_b2
        aw = jax.nn.softmax(aw, axis=1)
        cc = jnp.sum(eh * aw, axis=1)
        kp = _gelu(_ln(cc @ kg_W1 + kg_b1, kg_ln_g, kg_ln_b)) @ kg_W2 + kg_b2
        kernels = jax.nn.softmax(kp.reshape(B, H, K1 * K2), axis=-1)
        kernels = kernels.reshape(B * H, 1, K1, K2)
        mask = causal_mask[None, None]
        attn0 = jnp.where(mask, 0.0, attn).reshape(1, B * H, T, T)
        attn = lax.conv_general_dilated(attn0, kernels, window_strides=(1, 1), padding=((K1 // 2, K1 // 2), (K2 // 2, K2 // 2)), feature_group_count=B * H, dimension_numbers=('NCHW', 'OIHW', 'NCHW')).reshape(B, H, T, T)
        attn = jnp.where(mask, -jnp.inf, attn)
        p = jax.nn.softmax(attn, axis=-1)
        out = jnp.einsum('bhqk,bhkd->bhqd', p, v)
        out = out.transpose(0, 2, 1, 3).reshape(B, T, D)
        return out @ proj_W + proj_b

    def _L0_ffn_ref(x, Wg, W1, W2):
        import jax, jax.numpy as jnp
        import numpy as np
        B, S, D = x.shape
        E = Wg.shape[1]
        T = B * S
        cap = max(1, T // E)
        xt = x.reshape(T, D)
        logits = xt @ Wg
        probs = jax.nn.softmax(logits, axis=-1)
        pT = probs.T
        _, top_idx = jax.lax.top_k(pT, cap)
        sel = jnp.zeros((E, T), dtype=bool).at[jnp.arange(E)[:, None], top_idx].set(True)
        masked = jnp.where(sel, pT, -jnp.inf)
        assigned = sel.any(axis=0)
        tok2exp = jnp.where(assigned, jnp.argmax(masked, axis=0), jnp.argmax(pT, axis=0))
        weights = jnp.take_along_axis(probs, tok2exp[:, None], axis=1)[:, 0]
        out = jnp.zeros_like(xt)
        for e in range(E):
            gate = jnp.where(tok2exp == e, weights, 0.0)
            h = jax.nn.gelu(xt @ W1[e], approximate=False) @ W2[e]
            out = out + gate[:, None] * h
        return out.reshape(B, S, D)

    def _L1_attn_ref(x, time_decay, time_first, time_mix_k, time_mix_v, time_mix_r, W_key, W_value, W_receptance, W_output):
        import jax, jax.numpy as jnp
        import numpy as np
        EPS = 1e-08
        LOG_INIT = -1e+38

        def wkv_log_space(w, u, k, v, ln_a_p0, ln_a_m0, ln_b0):

            def step(carry, kv):
                ln_a_p, ln_a_m, ln_b = carry
                kt, vt = kv
                ln_v_p = jnp.log(jnp.maximum(vt, 0.0) + EPS)
                ln_v_m = jnp.log(jnp.maximum(-vt, 0.0) + EPS)
                uk = u + kt
                ln_den = jnp.logaddexp(uk, ln_b)
                wkv = jnp.exp(jnp.logaddexp(uk + ln_v_p, ln_a_p) - ln_den) - jnp.exp(jnp.logaddexp(uk + ln_v_m, ln_a_m) - ln_den)
                ln_a_p = jnp.logaddexp(ln_a_p - w, kt + ln_v_p)
                ln_a_m = jnp.logaddexp(ln_a_m - w, kt + ln_v_m)
                ln_b = jnp.logaddexp(ln_b - w, kt)
                return ((ln_a_p, ln_a_m, ln_b), wkv)
            kT = jnp.swapaxes(k, 0, 1)
            vT = jnp.swapaxes(v, 0, 1)
            _, wkv = jax.lax.scan(step, (ln_a_p0, ln_a_m0, ln_b0), (kT, vT))
            return jnp.swapaxes(wkv, 0, 1)
        B, T, D = x.shape
        last_x = jnp.concatenate([jnp.zeros((B, 1, D), x.dtype), x[:, :-1, :]], axis=1)
        k = (x * time_mix_k + last_x * (1.0 - time_mix_k)) @ W_key.T
        v = (x * time_mix_v + last_x * (1.0 - time_mix_v)) @ W_value.T
        r = (x * time_mix_r + last_x * (1.0 - time_mix_r)) @ W_receptance.T
        sr = jax.nn.sigmoid(r)
        w = jnp.exp(time_decay)
        u = time_first
        init = jnp.full((B, D), LOG_INIT, x.dtype)
        wkv = wkv_log_space(w, u, k, v, init, init, init)
        return wkv * sr @ W_output.T

    def _L1_xattn_ref(query, key, value, mask, Wq, Wk, Wv, Wo, bo):
        import jax, jax.numpy as jnp
        import numpy as np
        H = 16
        B, Tq, _ = query.shape
        Tk = key.shape[1]
        Dv = Wv.shape[0]
        Q = jnp.einsum('btd,ed->bte', query, Wq).reshape(B, Tq, H, -1).transpose(0, 2, 1, 3)
        K = jnp.einsum('btd,ed->bte', key, Wk).reshape(B, Tk, H, -1).transpose(0, 2, 1, 3)
        V = jnp.einsum('btd,ed->bte', value, Wv).reshape(B, Tk, H, -1).transpose(0, 2, 1, 3)
        d_k = K.shape[-1]
        scores = jnp.einsum('bhqd,bhkd->bhqk', Q, K) / jnp.sqrt(jnp.asarray(d_k, Q.dtype))
        scores = jnp.where(mask[:, None] == 0, jnp.asarray(-1000000000.0, scores.dtype), scores)
        attn = jax.nn.softmax(scores, axis=-1)
        Z = jnp.einsum('bhqk,bhkd->bhqd', attn, V)
        Zc = Z.transpose(0, 2, 1, 3).reshape(B, Tq, Dv)
        return jnp.einsum('btd,ed->bte', Zc, Wo) + bo

    def _L1_ffn_ref(hidden_states, W1, b1, W2, b2):
        import jax, jax.numpy as jnp
        import numpy as np
        HIDDEN = 128
        INTER = 512
        h = jax.nn.relu(jnp.einsum('bsh,hi->bsi', hidden_states, W1) + b1)
        return jnp.einsum('bsi,ih->bsh', h, W2) + b2

    def _L2_attn_ref(x, w_qkv, w_out, b_out, proj):
        import jax, jax.numpy as jnp
        import numpy as np
        HEADS = 8
        BLOCK = 32
        b, n, d = x.shape
        h = HEADS
        hd = d // h
        nb = n // BLOCK
        qkv = x @ w_qkv.T
        q, k, v = jnp.split(qkv, 3, axis=-1)

        def to_blocks(t):
            return t.reshape(b, n, h, hd).transpose(0, 2, 1, 3).reshape(b, h, nb, BLOCK, hd)
        q, k, v = (to_blocks(q), to_blocks(k), to_blocks(v))
        qp = jax.nn.elu(jnp.einsum('bhcsd,hdf->bhcsf', q, proj)) + 1.0
        kp = jax.nn.elu(jnp.einsum('bhcsd,hdf->bhcsf', k, proj)) + 1.0
        kv = jnp.einsum('bhcsf,bhcsd->bhcfd', kp, v)
        num = jnp.einsum('bhcsf,bhcfd->bhcsd', qp, kv)
        ksum = kp.sum(axis=3)
        z = 1.0 / (jnp.einsum('bhcsf,bhcf->bhcs', qp, ksum) + 1e-08)
        out = num * z[..., None]
        out = out.reshape(b, h, n, hd).transpose(0, 2, 1, 3).reshape(b, n, d)
        return out @ w_out.T + b_out

    def _L2_xattn_ref(x, context, context_mask, q_w, q_b, kv_w, kv_b, proj_w, proj_b):
        import jax, jax.numpy as jnp
        import numpy as np
        DIM = 128
        HEADS = 16
        HEAD_DIM = DIM // HEADS
        B, N, S = (4, 512, 64)
        b, n, c = x.shape
        s = context.shape[1]
        h, d = (HEADS, HEAD_DIM)
        scale = d ** (-0.5)
        q = (x @ q_w + q_b).reshape(b, n, h, d)
        kv = (context @ kv_w + kv_b).reshape(b, s, 2, h, d)
        k = kv[:, :, 0]
        v = kv[:, :, 1]
        attn = jnp.einsum('bnhd,bshd->bhns', q, k) * scale
        attn = jnp.where(context_mask[:, None, None, :], -jnp.inf, attn)
        attn = jax.nn.softmax(attn, axis=-1)
        out = jnp.einsum('bhns,bshd->bnhd', attn, v).reshape(b, n, c)
        return out @ proj_w + proj_b

    def _L2_ffn_ref(x, gate_w, bias, W1, W3, W2, sw1, sw3, sw2):
        import jax, jax.numpy as jnp
        import numpy as np
        D = 128
        I = 64
        E = 32
        K = 4
        T = 2 * 256
        C = 2 * T * K // E
        X = x.reshape(-1, D)
        logits = (X @ gate_w.T).astype(jnp.float32)
        scores = jax.nn.sigmoid(logits)
        _, idx = jax.lax.top_k(scores + bias[None, :], K)
        w = jnp.take_along_axis(scores, idx, axis=-1)
        w = w / jnp.clip(jnp.sum(w, axis=-1, keepdims=True), 1e-12, None)
        w = w.astype(x.dtype)
        eid = idx.reshape(-1)
        onehot = (eid[:, None] == jnp.arange(E)[None, :]).astype(jnp.int32)
        pos = jnp.take_along_axis(jnp.cumsum(onehot, axis=0) - 1, eid[:, None], axis=1)[:, 0]
        valid = pos < C
        posc = jnp.minimum(pos, C - 1)
        Xrep = jnp.repeat(X, K, axis=0)
        xe = jnp.zeros((E, C, D), x.dtype).at[eid, posc].add(jnp.where(valid[:, None], Xrep, jnp.zeros((), x.dtype)))
        h = jax.nn.silu(jnp.einsum('ecd,edi->eci', xe, W1)) * jnp.einsum('ecd,edi->eci', xe, W3)
        ye = jnp.einsum('eci,eid->ecd', h, W2)
        gflat = jnp.where(valid, w.reshape(-1), jnp.zeros((), x.dtype))
        yrows = ye[eid, posc] * gflat[:, None]
        out = yrows.reshape(-1, K, D).sum(axis=1)
        out = out + jax.nn.silu(X @ sw1.T) * (X @ sw3.T) @ sw2.T
        return out.reshape(x.shape)

    def _L3_attn_ref(X, Wq, Wk, Wv, Wg, Wo, W1, W2, ln_scale, ln_bias, gn_scale, gn_bias):
        import jax, jax.numpy as jnp
        import numpy as np
        L, D, F, H = (4, 128, 256, 8)
        DH = D // H
        EPS = 1e-05

        def _layer_norm(x, scale, bias):
            mu = x.mean(-1, keepdims=True)
            var = x.var(-1, keepdims=True)
            return (x - mu) * jax.lax.rsqrt(var + EPS) * scale + bias

        def _rotate(x, cos, sin):
            x1, x2 = (x[..., 0::2], x[..., 1::2])
            r1 = x1 * cos - x2 * sin
            r2 = x1 * sin + x2 * cos
            return jnp.stack([r1, r2], axis=-1).reshape(x.shape)

        def _decay_matrix(S):
            gammas = 1.0 - jnp.exp(jnp.linspace(np.log(1 / 32), np.log(1 / 64), H)).astype(jnp.float32)
            n = jnp.arange(S)
            diff = (n[:, None] - n[None, :]).astype(jnp.float32)
            pw = jnp.exp(jnp.clip(diff, 0.0)[None] * jnp.log(gammas)[:, None, None])
            return jnp.where(diff[None] >= 0, pw, 0.0)

        def _retention(x, Wq, Wk, Wv, Wg, Wo, gn_s, gn_b, Dm, cos, sin):
            B, S, _ = x.shape
            Q = (x @ Wq).reshape(B, S, H, DH)
            K = (x @ Wk).reshape(B, S, H, DH)
            V = (x @ Wv).reshape(B, S, H, DH)
            Q = _rotate(Q, cos, sin)
            K = _rotate(K, cos, -sin)
            att = jnp.einsum('bnhd,bmhd->bhnm', Q, K) * Dm
            Y = jnp.einsum('bhnm,bmhd->bnhd', att, V)
            mu = Y.mean(-1, keepdims=True)
            var = Y.var(-1, keepdims=True)
            Y = (Y - mu) * jax.lax.rsqrt(var + EPS)
            Y = Y.reshape(B, S, D) * gn_s + gn_b
            G = jax.nn.swish(x @ Wg)
            return G * Y @ Wo
        B, S, _ = X.shape
        pos = jnp.arange(S, dtype=jnp.float32)
        inv_freq = 1.0 / 10000.0 ** (jnp.arange(0, DH, 2, dtype=jnp.float32) / DH)
        ang = pos[:, None] * inv_freq[None, :]
        cos = jnp.cos(ang)[None, :, None, :]
        sin = jnp.sin(ang)[None, :, None, :]
        Dm = _decay_matrix(S)
        for i in range(L):
            Yr = _retention(_layer_norm(X, ln_scale, ln_bias), Wq[i], Wk[i], Wv[i], Wg[i], Wo[i], gn_scale[i], gn_bias[i], Dm, cos, sin) + X
            X = jax.nn.gelu(_layer_norm(Yr, ln_scale, ln_bias) @ W1[i]) @ W2[i] + Yr
        return X

    def _L3_xattn_ref(k, v, q, mask, Wk, bk, Wv, bv, Wq, bq, Woff, boff, Wo, bo):
        import jax, jax.numpy as jnp
        import numpy as np
        import math
        B, M, D, H, NK = (4, 256, 128, 16, 5)
        HD = D // H

        def _gather_pad0(x, idx):
            Bx, Hx, W, hd = x.shape
            valid = (idx >= 0) & (idx < W)
            idxc = jnp.clip(idx, 0, W - 1).reshape(Bx, Hx, -1)
            g = jnp.take_along_axis(x, idxc[..., None], axis=2)
            g = g.reshape(idx.shape + (hd,))
            return g * valid[..., None].astype(x.dtype)
        Bq, Q, _ = q.shape
        key_len = k.shape[1]
        K = jnp.einsum('bmd,ed->bme', k, Wk) + bk
        V = jnp.einsum('bmd,ed->bme', v, Wv) + bv
        Qp = jnp.einsum('bqd,ed->bqe', q, Wq) + bq
        off = jnp.einsum('bqd,ed->bqe', Qp, Woff) + boff
        off = off.reshape(Bq, Q, H, NK).transpose(0, 2, 1, 3)
        Kh = K.reshape(Bq, key_len, H, HD).transpose(0, 2, 1, 3)
        Vh = V.reshape(Bq, key_len, H, HD).transpose(0, 2, 1, 3)
        Qh = Qp.reshape(Bq, Q, H, HD).transpose(0, 2, 1, 3)
        loc = jnp.arange(Q, dtype=jnp.float32)[:, None]
        left = -NK // 2
        ref = jnp.arange(left, NK + left, dtype=jnp.float32)
        sign_lens = (1 - mask).sum(-1).astype(jnp.float32) - 1.0
        loc_x = jnp.mod(ref + off + loc, sign_lens[:, None, None, None])
        xg = loc_x / (key_len - 1) * 2.0 - 1.0
        ix = ((xg + 1.0) * key_len - 1.0) / 2.0
        x0 = jnp.floor(ix)
        dx = ix - x0
        i0 = x0.astype(jnp.int32)
        i1 = i0 + 1
        w0 = (1.0 - dx)[..., None]
        w1 = dx[..., None]
        sk = 0.5 * (w0 * _gather_pad0(Kh, i0) + w1 * _gather_pad0(Kh, i1))
        sv = 0.5 * (w0 * _gather_pad0(Vh, i0) + w1 * _gather_pad0(Vh, i1))
        scores = jnp.einsum('bhqd,bhqkd->bhqk', Qh / math.sqrt(HD), sk)
        attn = jax.nn.softmax(scores, axis=-1)
        ctx = jnp.einsum('bhqk,bhqkd->bhqd', attn, sv)
        ctx = ctx.transpose(0, 2, 1, 3).reshape(Bq, Q, H * HD)
        return jnp.einsum('bqd,ed->bqe', ctx, Wo) + bo

    def _L3_ffn_ref(x, W1, b1, W2, b2):
        import jax, jax.numpy as jnp
        import numpy as np
        HIDDEN = 128
        NUM_EXPERTS = 8
        TOP_K = 2
        B, S = (2, 256)
        Bm, Sm, d = x.shape
        E = W1.shape[0]
        x_flat = x.reshape(-1, d)
        h = jnp.mod(x_flat[:, :TOP_K].sum(axis=1).astype(jnp.int32), E)
        sel = jnp.stack([h, jnp.mod(h + 1, E)], axis=1)

        def step(acc, params):
            e, W1e, b1e, W2e, b2e = params
            w = jnp.any(sel == e, axis=1).astype(x.dtype) / TOP_K
            y = jnp.maximum(x_flat @ W1e + b1e, 0.0) @ W2e + b2e
            return (acc + w[:, None] * y, None)
        init = jnp.zeros_like(x_flat)
        out_flat, _ = jax.lax.scan(step, init, (jnp.arange(E), W1, b1, W2, b2))
        return out_flat.reshape(Bm, Sm, d)
    x = x + _L0_attn_ref(_layernorm(x, axis=-1), L0_attn_Wq, L0_attn_Wk, L0_attn_Wv, L0_attn_Wp, L0_attn_q_gain)
    x = x + _L0_xattn_ref(_layernorm(x, axis=-1), ctx_1024, L0_xattn_Wq, L0_xattn_Wk, L0_xattn_Wv, L0_xattn_hist_W, L0_xattn_hist_b, L0_xattn_hist_ln_g, L0_xattn_hist_ln_b, L0_xattn_ctx_W1, L0_xattn_ctx_b1, L0_xattn_ctx_W2, L0_xattn_ctx_b2, L0_xattn_kg_W1, L0_xattn_kg_b1, L0_xattn_kg_ln_g, L0_xattn_kg_ln_b, L0_xattn_kg_W2, L0_xattn_kg_b2, L0_xattn_proj_W, L0_xattn_proj_b, mask_SxS_bc0)
    x = x + _L0_ffn_ref(_layernorm(x, axis=-1), L0_ffn_Wg, L0_ffn_W1, L0_ffn_W2)
    x = x + _L1_attn_ref(_layernorm(x, axis=-1), L1_attn_time_decay, L1_attn_time_first, L1_attn_time_mix_k, L1_attn_time_mix_v, L1_attn_time_mix_r, L1_attn_W_key, L1_attn_W_value, L1_attn_W_receptance, L1_attn_W_output)
    x = x + _L1_xattn_ref(_layernorm(x, axis=-1), ctx_1024, ctx_1024, mask_BxSxS2_if1, L1_xattn_Wq, L1_xattn_Wk, L1_xattn_Wv, L1_xattn_Wo, L1_xattn_bo)
    x = x + _L1_ffn_ref(_layernorm(x, axis=-1), L1_ffn_W1, L1_ffn_b1, L1_ffn_W2, L1_ffn_b2)
    x = x + _L2_attn_ref(_layernorm(x, axis=-1), L2_attn_w_qkv, L2_attn_w_out, L2_attn_b_out, L2_attn_proj)
    x = x + _L2_xattn_ref(_layernorm(x, axis=-1), ctx_1024, mask_BxS2_bk0, L2_xattn_q_w, L2_xattn_q_b, L2_xattn_kv_w, L2_xattn_kv_b, L2_xattn_proj_w, L2_xattn_proj_b)
    x = x + _L2_ffn_ref(_layernorm(x, axis=-1), L2_ffn_gate_w, L2_ffn_bias, L2_ffn_W1, L2_ffn_W3, L2_ffn_W2, L2_ffn_sw1, L2_ffn_sw3, L2_ffn_sw2)
    x = x + _L3_attn_ref(_layernorm(x, axis=-1), L3_attn_Wq, L3_attn_Wk, L3_attn_Wv, L3_attn_Wg, L3_attn_Wo, L3_attn_W1, L3_attn_W2, L3_attn_ln_scale, L3_attn_ln_bias, L3_attn_gn_scale, L3_attn_gn_bias)
    x = x + _L3_xattn_ref(ctx_1024, ctx_1024, _layernorm(x, axis=-1), mask_BxS2_if0, L3_xattn_Wk, L3_xattn_bk, L3_xattn_Wv, L3_xattn_bv, L3_xattn_Wq, L3_xattn_bq, L3_xattn_Woff, L3_xattn_boff, L3_xattn_Wo, L3_xattn_bo)
    x = x + _L3_ffn_ref(_layernorm(x, axis=-1), L3_ffn_W1, L3_ffn_b1, L3_ffn_W2, L3_ffn_b2)
    return x

_drawn_inputs = setup_inputs


def setup_inputs(seed=0):
    import zlib

    import numpy as np

    out = dict(_drawn_inputs(seed))
    spreads = {'L0_attn_q_gain': (1.0, 0.6),
     'L0_xattn_hist_b': (0.0, 0.63),
     'L0_xattn_hist_ln_g': (1.0, 0.6),
     'L0_xattn_hist_ln_b': (0.0, 0.707),
     'L0_xattn_ctx_b1': (0.0, 2.0),
     'L0_xattn_kg_b1': (0.0, 0.36),
     'L0_xattn_kg_ln_g': (1.0, 0.6),
     'L0_xattn_kg_ln_b': (0.0, 0.695),
     'L0_xattn_kg_b2': (0.0, 0.709),
     'L0_xattn_proj_b': (0.0, 0.1),
     'L1_xattn_bo': (0.0, 0.1),
     'L2_attn_b_out': (0.0, 0.1),
     'L2_xattn_q_b': (0.0, 0.1),
     'L2_xattn_kv_b': (0.0, 0.1),
     'L2_xattn_proj_b': (0.0, 0.1),
     'L2_ffn_bias': (0.0, 0.8),
     'L3_attn_ln_scale': (1.0, 0.2),
     'L3_attn_ln_bias': (0.0, 0.1),
     'L3_attn_gn_scale': (1.0, 0.2),
     'L3_attn_gn_bias': (0.0, 0.1),
     'L3_xattn_bk': (0.0, 2.0),
     'L3_xattn_bv': (0.0, 0.8),
     'L3_xattn_bq': (0.0, 0.8),
     'L3_xattn_boff': (0.0, 0.8),
     'L3_xattn_bo': (0.0, 0.1)}
    factors = {'L0_attn_Wq': 7.198,
     'L0_attn_Wk': 5.189,
     'L0_attn_Wv': 2.961,
     'L0_attn_Wp': 3.348,
     'L0_xattn_ctx_W1': 6.777,
     'L0_xattn_ctx_W2': 7.824,
     'L0_ffn_Wg': 3.23,
     'L0_ffn_W1': 3.515,
     'L0_ffn_W2': 3.103,
     'L1_xattn_Wq': 8.0,
     'L1_xattn_Wk': 8.0,
     'L2_ffn_gate_w': 7.731,
     'L2_ffn_W1': 5.904,
     'L2_ffn_W3': 8.0,
     'L2_ffn_W2': 6.985,
     'L2_ffn_sw1': 4.577,
     'L2_ffn_sw3': 4.894,
     'L2_ffn_sw2': 4.092,
     'L3_xattn_Wk': 8.0,
     'L3_xattn_Wv': 5.231,
     'L3_xattn_Wq': 8.0,
     'L3_xattn_Woff': 8.0,
     'L3_xattn_Wo': 5.118,
     'L3_ffn_b1': 38.596,
     'L3_ffn_b2': 27.831}
    for name, (base, spread) in spreads.items():
        noise = np.random.default_rng([zlib.crc32(name.encode()), seed]).standard_normal(out[name].shape)
        drawn = base * np.exp(spread * noise) if base else spread * noise
        out[name] = jnp.asarray(drawn.astype(out[name].dtype))
    for name, factor in factors.items():
        out[name] = (out[name] * factor).astype(out[name].dtype)
    return out
```

```python
from contextlib import ExitStack

import concourse.bass as bass
from concourse import mybir

P = 128
T = 1024
NT = T // P
D = 128
H = 16
HD = D // H
S = 6404
KT = (S + P - 1) // P
SP = KT * P
BANK = 512
NBANK = 8

ALU = mybir.AluOpType
ACT = mybir.ActivationFunctionType
AX = mybir.AxisListType
F32 = mybir.dt.float32
BF16 = mybir.dt.bfloat16
FP8 = mybir.dt.float8e5
I32 = mybir.dt.int32
U32 = mybir.dt.uint32
ROUND = 12582912.0
BIG = 2.0 ** 30
MINUS_INF = -1.0e30


class InOrder:

    def __init__(self, eng, sem, base=0):
        self.eng, self.sem, self.base, self.n = eng, sem, base, 0

    def step(self, ins):
        ins.then_inc(self.sem, 1)
        self.n += 1
        self.eng.wait_ge(self.sem, self.base + self.n)


class Stage:

    names = {}
    used = []

    def __init__(self, nc):
        self.nc, self.ctx = nc, ExitStack()

    def __enter__(self):
        self.ctx.__enter__()
        return self

    def __exit__(self, *e):
        return self.ctx.__exit__(*e)

    def sb(self, name, shape, dt=F32):
        return self.ctx.enter_context(self.nc.sbuf_tensor(self.unique(name), shape, dt))

    def sem(self, name):
        sem = self.nc.alloc_semaphore(self.unique(name))
        Stage.used.append(sem)
        return sem

    def unique(self, name):
        Stage.names[name] = Stage.names.get(name, 0) + 1
        return f"{name}_{Stage.names[name]}"

    def block(self):
        return self.ctx.enter_context(self.nc.Block())


def give_back(nc):
    nc.all_engine_barrier()
    nc.clear_and_free_semaphores(Stage.used)
    Stage.used = []
    nc.all_engine_barrier()


def bc(ap, shape):
    while ap.ndim < len(shape):
        ap = ap.unsqueeze(ap.ndim)
    return ap.to_broadcast(list(shape))


def mid(ap, n):
    return ap.unsqueeze(1).to_broadcast([ap.shape[0], n, ap.shape[1]])


class Core:

    def __init__(self, nc, dram):
        self.nc, self.dram = nc, dram
        self.ctx = ExitStack()

    def sb(self, name, shape, dt=F32):
        return self.ctx.enter_context(self.nc.sbuf_tensor(name, shape, dt))


SWAPPED = [("L1_attn_W_key", 128), ("L1_attn_W_value", 128), ("L1_attn_W_receptance", 128), ("L1_attn_W_output", 128),
           ("L1_xattn_Wq", 128), ("L1_xattn_Wk", 128), ("L1_xattn_Wv", 128), ("L1_xattn_Wo", 128),
           ("L2_attn_w_out", 128), ("L2_ffn_gate_w", 32), ("L2_ffn_sw1", 64), ("L2_ffn_sw3", 64),
           ("L3_xattn_Wk", 128), ("L3_xattn_Wv", 128), ("L3_xattn_Wq", 128), ("L3_xattn_Woff", 80),
           ("L3_xattn_Wo", 128)]


def setup(k, need):
    nc, dr = k.nc, k.dram
    sw = [(n, r) for n, r in SWAPPED if n.split("_")[0] + "_" + n.split("_")[1] in need]
    k.wT = {n: k.sb("wT_" + n, [P, r]) for n, r in sw}
    if "L2_ffn" in need:
        k.wT["L2_ffn_sw2"] = k.sb("wT_L2_ffn_sw2", [64, D])
    with Stage(nc) as s:
        w_rows = s.sb("w_rows", [P, len(sw) + 1, D])
        wb_rows = s.sb("wb_rows", [P, 4, D], BF16)
        loaded = s.sem("loaded")
        wb_wide = s.sem("wb_wide")
        zeroed = s.sem("zeroed")
        turned = s.sem("turned")
        kept = s.sem("kept")
        pieces = []
        wide = {"L2_ffn_gate_w": 0, "L2_ffn_sw1": 1, "L2_ffn_sw3": 2}
        for i, (n, r) in enumerate(sw):
            pieces.append((w_rows[0:r, i, :], k.wT[n][:, 0:r], r))
        n_bf = 0
        if "L2_ffn" in need:
            pieces.append((w_rows[:, len(sw), 0:64], k.wT["L2_ffn_sw2"][:, :], P))
            n_bf = 4
        block = s.block()

        @block.sync
        def _(sp):
            sp.dma_start(k.x[:], dr["x"][0].rearrange("(t p) d -> p t d", p=P)).then_inc(loaded, 16)
            sp.dma_start(k.ident[:], dr["c_ident"]).then_inc(loaded, 16)
            sp.dma_start(k.iota[:], dr["c_iota"]).then_inc(loaded, 16)
            for i, (n, r) in enumerate(sw):
                dst = wb_rows[0:r, wide[n], :] if n in wide else w_rows[0:r, i, :]
                sp.dma_start(dst, dr[n]).then_inc(loaded, 16)
            if n_bf:
                sp.dma_start(wb_rows[:, 3, 0:64], dr["L2_ffn_sw2"]).then_inc(loaded, 16)
            sp.wait_ge(loaded, 16 * (3 + len(sw) + (1 if n_bf else 0)))

        n_loads = 3 + len(sw) + (1 if n_bf else 0)

        @block.vector
        def _(dve):
            nc.vector.memset(k.ones[:], 1.0).then_inc(zeroed, 1)
            dve.wait_ge(loaded, 16 * n_loads)
            nc.vector.tensor_copy(k.ident16[:], k.ident[:]).then_inc(zeroed, 1)
            nc.vector.tensor_scalar(k.lower[:], k.ident[:], LOWER, None, ALU.mult).then_inc(zeroed, 1)
            if n_bf:
                for n, i in wide.items():
                    r = dict(sw)[n]
                    j = [m for m, _ in sw].index(n)
                    nc.vector.tensor_copy(w_rows[0:r, j, :], wb_rows[0:r, i, :]).then_inc(wb_wide, 1)
                nc.vector.tensor_copy(w_rows[:, len(sw), 0:64], wb_rows[:, 3, 0:64]).then_inc(wb_wide, 1)
            for i, (src, dst, r) in enumerate(pieces):
                dve.wait_ge(turned, i + 1)
                nc.vector.tensor_copy(dst, k.ps[0:src.shape[1], i % NBANK, 0:r]).then_inc(kept, 1)

        @block.tensor
        def _(pe):
            pe.wait_ge(loaded, 16 * n_loads)
            if n_bf:
                pe.wait_ge(wb_wide, n_bf)
            for i, (src, dst, r) in enumerate(pieces):
                if i >= NBANK:
                    pe.wait_ge(kept, i - NBANK + 1)
                nc.tensor.transpose(k.ps[0:src.shape[1], i % NBANK, 0:r], src, k.ident[0:r, 0:r]).then_inc(turned, 1)


def normalise(k, affine=None, eps=1e-5, src=None):
    nc = k.nc
    x = src or k.x
    with Stage(nc) as s:
        total = s.sb("total", [P, NT])
        mean = s.sb("mean", [P, NT])
        square = s.sb("square", [P, NT, D])
        var = s.sb("var", [P, NT])
        dev = s.sb("dev", [P, NT])
        inv = s.sb("inv", [P, NT])
        order = s.sem("order")
        var_ready = s.sem("var_ready")
        dev_ready = s.sem("dev_ready")
        h_ready = s.sem("h_ready")
        turned = s.sem("turned")
        block = s.block()

        @block.vector
        def _(dve):
            o = InOrder(dve, order)
            o.step(nc.vector.tensor_reduce(total[:], x[:], AX.X, ALU.add))
            o.step(nc.vector.tensor_scalar(mean[:], total[:], 1.0 / D, None, ALU.mult))
            o.step(nc.vector.tensor_tensor(k.h[:], x[:], bc(mean[:], [P, NT, D]), ALU.subtract))
            o.step(nc.vector.tensor_tensor(square[:], k.h[:], k.h[:], ALU.mult))
            o.step(nc.vector.tensor_reduce(total[:], square[:], AX.X, ALU.add))
            nc.vector.tensor_scalar(var[:], total[:], 1.0 / D, eps, ALU.mult, ALU.add).then_inc(var_ready, 1)
            dve.wait_ge(dev_ready, 1)
            o.step(nc.vector.reciprocal(inv[:], dev[:]))
            last = nc.vector.tensor_tensor(k.h[:], k.h[:], bc(inv[:], [P, NT, D]), ALU.mult)
            if affine:
                o.step(last)
                o.step(nc.vector.tensor_tensor(k.h[:], k.h[:], mid(affine[0], NT), ALU.mult))
                last = nc.vector.tensor_tensor(k.h[:], k.h[:], mid(affine[1], NT), ALU.add)
            last.then_inc(h_ready, 1)
            dve.wait_ge(turned, 1)
            nc.vector.tensor_copy(k.hT[:, 0:BANK], k.ps[:, 0, :]).then_inc(order, 1)

        @block.scalar
        def _(act):
            act.wait_ge(var_ready, 1)
            nc.scalar.activation(dev[:], var[:], ACT.Sqrt).then_inc(dev_ready, 1)
            act.wait_ge(turned, 2)
            nc.scalar.copy(k.hT[:, BANK:T], k.ps[:, 1, :]).then_inc(dev_ready, 1)

        @block.tensor
        def _(pe):
            pe.wait_ge(h_ready, 1)
            for b in range(2):
                for j in range(4):
                    last = nc.tensor.transpose(k.ps[:, b, j * P:(j + 1) * P], k.h[:, 4 * b + j, :], k.ident[:])
                last.then_inc(turned, 1)


def load(k, pairs):
    nc = k.nc
    with Stage(nc) as t:
        loaded = t.sem("loaded")
        block = t.block()

        @block.sync
        def _(sp):
            with nc.allow_non_contiguous_dma("a few small vectors lie by partition"):
                for dst, src in pairs:
                    sp.dma_start(dst, src).then_inc(loaded, 16)
            sp.wait_ge(loaded, 16 * len(pairs))


def row(k, name, n, at=0):
    return k.dram[name][at:at + n].partition_broadcast(P)


def project(k, srcT, tiles, w, n, dst, bias=None, act=None):
    nc = k.nc
    per = BANK // n
    groups = [range(a, min(a + per, tiles)) for a in range(0, tiles, per)]
    with Stage(nc) as s:
        product = s.sem("product")
        kept = s.sem("kept")
        block = s.block()

        @block.tensor
        def _(pe):
            for g, ts in enumerate(groups):
                if g >= NBANK:
                    pe.wait_ge(kept, g - NBANK + 1)
                for j, t in enumerate(ts):
                    last = nc.tensor.matmul(k.ps[:, g % NBANK, j * n:(j + 1) * n], srcT[:, t * P:(t + 1) * P], w,
                                            start=True, stop=True)
                last.then_inc(product, 1)

        @block.vector
        def _(dve):
            for g, ts in enumerate(groups):
                dve.wait_ge(product, g + 1)
                src = k.ps[:, g % NBANK, 0:len(ts) * n].rearrange("p (t n) -> p t n", n=n)
                out = dst[:, ts[0]:ts[0] + len(ts), :]
                if bias is None:
                    nc.vector.tensor_copy(out, src).then_inc(kept, 1)
                else:
                    nc.vector.tensor_tensor(out, src, mid(bias, len(ts)), ALU.add).then_inc(kept, 1)


def turn(k, src, dstT):
    nc = k.nc
    with Stage(nc) as s:
        turned = s.sem("turned")
        kept = s.sem("kept")
        block = s.block()

        @block.tensor
        def _(pe):
            for b in range(2):
                for j in range(4):
                    last = nc.tensor.transpose(k.ps[:, b, j * P:(j + 1) * P], src[:, 4 * b + j, :], k.ident[:])
                last.then_inc(turned, 1)

        @block.vector
        def _(dve):
            for b in range(2):
                dve.wait_ge(turned, b + 1)
                nc.vector.tensor_copy(dstT[:, b * BANK:(b + 1) * BANK], k.ps[:, b, :]).then_inc(kept, 1)


def project_add(k, srcT, w, bias=None):
    nc = k.nc
    with Stage(nc) as s:
        product = s.sem("product")
        order = s.sem("order")
        block = s.block()

        @block.tensor
        def _(pe):
            for b in range(2):
                for j in range(4):
                    t = 4 * b + j
                    last = nc.tensor.matmul(k.ps[:, b, j * P:(j + 1) * P], srcT[:, t * P:(t + 1) * P], w,
                                            start=True, stop=True)
                last.then_inc(product, 1)

        @block.vector
        def _(dve):
            o = InOrder(dve, order)
            for b in range(2):
                part = k.x[:, 4 * b:4 * b + 4, :]
                dve.wait_ge(product, b + 1)
                o.step(nc.vector.tensor_tensor(part, part, k.ps[:, b, :].rearrange("p (t d) -> p t d", d=D), ALU.add))
                if bias is not None:
                    o.step(nc.vector.tensor_tensor(part, part, mid(bias, 4), ALU.add))


def experts(k, E, F, w1, w2, func, gate=None, b1=None, b2=None):
    nc = k.nc
    FC = F // P
    with Stage(nc) as s:
        hid = s.sb("hid", [P, 2, FC, T])
        up = s.sem("up")
        hid_ready = s.sem("hid_ready")
        down = s.sem("down")
        added = s.sem("added")
        block = s.block()

        @block.tensor
        def _(pe):
            def up_product(e):
                for c in range(FC):
                    n = e * FC + c
                    if n >= 2:
                        pe.wait_ge(hid_ready, n - 1)
                    for b in range(2):
                        last = nc.tensor.matmul(k.ps[:, 2 * (n % 2) + b, :], w1(e)[:, c * P:(c + 1) * P],
                                                k.hT[:, b * BANK:(b + 1) * BANK], start=True, stop=True)
                    last.then_inc(up, 1)

            def down_product(e):
                pe.wait_ge(hid_ready, FC * (e + 1))
                if e >= 2:
                    pe.wait_ge(added, NT * (e - 1))
                for t in range(NT):
                    out = k.ps[:, 4 + 2 * (e % 2) + t // 4, (t % 4) * P:(t % 4 + 1) * P]
                    if b2 is not None:
                        nc.tensor.matmul(out, k.ones[0:1, :], b2(e), start=True, stop=False)
                    for c in range(FC):
                        last = nc.tensor.matmul(out, hid[:, e % 2, c, t * P:(t + 1) * P], w2(e, c),
                                                start=(c == 0 and b2 is None), stop=(c == FC - 1))
                    if t % 4 == 3:
                        last.then_inc(down, 1)

            for e in range(E):
                up_product(e)
                if e >= 1:
                    down_product(e - 1)
            down_product(E - 1)

        @block.scalar
        def _(act):
            for n in range(E * FC):
                e, c = divmod(n, FC)
                act.wait_ge(up, n + 1)
                if e >= 2:
                    act.wait_ge(down, 2 * (e - 1))
                bias = b1(e, c) if b1 is not None else 0.0
                nc.scalar.activation(hid[:, e % 2, c, :],
                                     k.ps[:, 2 * (n % 2):2 * (n % 2) + 2, :].rearrange("p a b -> p (a b)"),
                                     func, bias=bias).then_inc(hid_ready, 1)

        @block.vector
        def _(dve):
            for e in range(E):
                for t in range(NT):
                    out = k.ps[:, 4 + 2 * (e % 2) + t // 4, (t % 4) * P:(t % 4 + 1) * P]
                    dve.wait_ge(down, 2 * e + t // 4 + 1)
                    if e >= 1:
                        dve.wait_ge(added, NT * (e - 1) + t + 1)
                    if gate is None:
                        nc.vector.tensor_tensor(k.x[:, t, :], out, k.x[:, t, :], ALU.add).then_inc(added, 1)
                    else:
                        nc.vector.scalar_tensor_tensor(out=k.x[:, t, :], in0=out, scalar=gate[:, t, e:e + 1],
                                                       in1=k.x[:, t, :], op0=ALU.mult, op1=ALU.add).then_inc(added, 1)


def relu_ffn(k):
    dr = k.dram
    F = 512
    FC = F // P
    normalise(k)
    with Stage(k.nc) as s:
        w1 = s.sb("w1", [P, F])
        w2 = s.sb("w2", [P, FC, D])
        b1 = s.sb("b1", [P, FC])
        b2 = s.sb("b2", [1, D])
        load(k, [(w1[:], dr["L1_ffn_W1"]),
                 (w2[:], dr["L1_ffn_W2"].rearrange("(c p) d -> p c d", p=P)),
                 (b1[:], dr["L1_ffn_b1"].rearrange("(c p) -> p c", p=P)),
                 (b2[:], dr["L1_ffn_b2"].rearrange("(a d) -> a d", a=1))])
        experts(k, 1, F, lambda e: w1[:], lambda e, c: w2[:, c, :], ACT.Relu,
                b1=lambda e, c: b1[:, c:c + 1], b2=lambda e: b2[:])


def hash_ffn(k):
    nc, dr = k.nc, k.dram
    E, F = 8, 512
    FC = F // P
    normalise(k)
    with Stage(nc) as s:
        gate = s.sb("gate", [P, NT, E])
        w1 = s.sb("w1", [P, E, F])
        w2 = s.sb("w2", [P, E, FC, D])
        b1 = s.sb("b1", [P, E, FC])
        b2 = s.sb("b2", [1, E, D])
        load(k, [(w1[:], dr["L3_ffn_W1"].rearrange("e d f -> d e f")),
                 (w2[:], dr["L3_ffn_W2"].rearrange("e (c p) d -> p e c d", p=P)),
                 (b1[:], dr["L3_ffn_b1"].rearrange("e (c p) -> p e c", p=P)),
                 (b2[:], dr["L3_ffn_b2"].rearrange("(a e) d -> a e d", a=1))])
        with Stage(nc) as g:
            a = g.sb("a", [P, NT])
            b = g.sb("b", [P, NT])
            c = g.sb("c", [P, NT])
            sign = g.sb("sign", [P, NT])
            eq = g.sb("eq", [P, NT, E])
            order = g.sem("order")
            block = g.block()

            @block.vector
            def _(dve):
                o = InOrder(dve, order)
                o.step(nc.vector.tensor_tensor(a[:], k.h[:, :, 0], k.h[:, :, 1], ALU.add))
                o.step(nc.vector.tensor_scalar(sign[:], a[:], 0.0, None, ALU.is_ge))
                o.step(nc.vector.tensor_scalar(sign[:], sign[:], 2.0, -1.0, ALU.mult, ALU.add))
                o.step(nc.vector.tensor_tensor(a[:], a[:], sign[:], ALU.mult))
                floor(o, nc, b, a, c)
                o.step(nc.vector.tensor_tensor(a[:], b[:], sign[:], ALU.mult))
                for first in (True, False):
                    o.step(nc.vector.tensor_scalar(sign[:], a[:], 1.0 / E, None, ALU.mult))
                    floor(o, nc, b, sign, c)
                    o.step(nc.vector.scalar_tensor_tensor(out=a[:], in0=b[:], scalar=-float(E), in1=a[:],
                                                          op0=ALU.mult, op1=ALU.add))
                    if first:
                        o.step(nc.vector.tensor_tensor(gate[:], mid(k.iota[:, 0:E], NT), bc(a[:], [P, NT, E]), ALU.is_equal))
                        o.step(nc.vector.tensor_scalar(a[:], a[:], 1.0, None, ALU.add))
                o.step(nc.vector.tensor_tensor(eq[:], mid(k.iota[:, 0:E], NT), bc(a[:], [P, NT, E]), ALU.is_equal))
                o.step(nc.vector.tensor_tensor(gate[:], gate[:], eq[:], ALU.add))
                o.step(nc.vector.tensor_scalar(gate[:], gate[:], 0.5, None, ALU.mult))
        experts(k, E, F, lambda e: w1[:, e, :], lambda e, c: w2[:, e, c, :], ACT.Relu, gate,
                b1=lambda e, c: b1[:, e, c:c + 1], b2=lambda e: b2[:, e, :])


def floor(o, nc, out, a, tmp):
    o.step(nc.vector.tensor_scalar(out[:], a[:], ROUND, -ROUND, ALU.add, ALU.add))
    o.step(nc.vector.tensor_tensor(tmp[:], out[:], a[:], ALU.is_gt))
    o.step(nc.vector.tensor_tensor(out[:], out[:], tmp[:], ALU.subtract))


def choice_ffn(k):
    nc, dr = k.nc, k.dram
    E, F = 8, 256
    FC = F // P
    CAP = T // E
    normalise(k)
    with Stage(nc) as s:
        gate = s.sb("gate", [P, NT, E])
        wg = s.sb("wg", [P, E])
        w1 = s.sb("w1", [P, E, F])
        w2 = s.sb("w2", [P, E, FC, D])
        load(k, [(wg[:], dr["L0_ffn_Wg"]),
                 (w1[:], dr["L0_ffn_W1"].rearrange("e d f -> d e f")),
                 (w2[:], dr["L0_ffn_W2"].rearrange("e (c p) d -> p e c d", p=P))])
        with Stage(nc) as g:
            probs = g.sb("probs", [P, NT, E])
            red = g.sb("red", [P, NT])
            by_expert = g.sb("by_expert", [E, 2, T])
            top8 = g.sb("top8", [E, 8])
            sel = g.sb("sel", [P, NT, E])
            cand = g.sb("cand", [P, NT, E])
            order = g.sem("order")
            logits = g.sem("logits")
            shifted = g.sem("shifted")
            powers = g.sem("powers")
            probs_ready = g.sem("probs_ready")
            turned = g.sem("turned")
            chosen = g.sem("chosen")
            back = g.sem("back")
            block = g.block()

            @block.tensor
            def _(pe):
                for t in range(NT):
                    last = nc.tensor.matmul(k.ps[:, 0, t * E:(t + 1) * E], k.hT[:, t * P:(t + 1) * P], wg[:],
                                            start=True, stop=True)
                last.then_inc(logits, 1)
                pe.wait_ge(probs_ready, 1)
                for t in range(NT):
                    last = nc.tensor.transpose(k.ps[0:E, 2 + t // 4, (t % 4) * P:(t % 4 + 1) * P], probs[:, t, :], k.ident[:])
                last.then_inc(turned, 1)
                pe.wait_ge(chosen, 1)
                for t in range(NT):
                    last = nc.tensor.transpose(k.ps[:, 1, t * E:(t + 1) * E], by_expert[:, 1, t * P:(t + 1) * P],
                                               k.ident[0:E, 0:E])
                last.then_inc(back, 1)

            @block.scalar
            def _(act):
                act.wait_ge(shifted, 1)
                nc.scalar.activation(probs[:], cand[:], ACT.Exp).then_inc(powers, 1)

            @block.vector
            def _(dve):
                o = InOrder(dve, order)
                lg = k.ps[:, 0, 0:NT * E].rearrange("p (t e) -> p t e", e=E)
                dve.wait_ge(logits, 1)
                o.step(nc.vector.tensor_reduce(red[:], lg, AX.X, ALU.max))
                nc.vector.tensor_tensor(cand[:], lg, bc(red[:], [P, NT, E]), ALU.subtract).then_inc(shifted, 1)
                dve.wait_ge(powers, 1)
                o.step(nc.vector.tensor_reduce(red[:], probs[:], AX.X, ALU.add))
                o.step(nc.vector.reciprocal(red[:], red[:]))
                nc.vector.tensor_tensor(probs[:], probs[:], bc(red[:], [P, NT, E]), ALU.mult).then_inc(probs_ready, 1)
                dve.wait_ge(turned, 1)
                o.step(nc.vector.tensor_copy(by_expert[:, 0, :], k.ps[0:E, 2:4, :].rearrange("p a b -> p (a b)")))
                for r in range(CAP // 8):
                    o.step(nc.vector.max(top8[:], by_expert[:, r % 2, :]))
                    o.step(nc.vector.match_replace(by_expert[:, (r + 1) % 2, :], top8[:], by_expert[:, r % 2, :], -1.0))
                nc.vector.tensor_scalar(by_expert[:, 1, :], by_expert[:, 0, :], 0.0, None, ALU.is_lt).then_inc(chosen, 1)
                dve.wait_ge(back, 1)
                o.step(nc.vector.tensor_copy(sel[:], k.ps[:, 1, 0:NT * E].rearrange("p (t e) -> p t e", e=E)))
                o.step(nc.vector.tensor_reduce(red[:], sel[:], AX.X, ALU.max))
                o.step(nc.vector.tensor_scalar(red[:], red[:], -1.0, 1.0, ALU.mult, ALU.add))
                o.step(nc.vector.tensor_tensor(sel[:], sel[:], bc(red[:], [P, NT, E]), ALU.max))
                o.step(nc.vector.tensor_tensor(cand[:], probs[:], sel[:], ALU.mult))
                o.step(nc.vector.scalar_tensor_tensor(out=cand[:], in0=sel[:], scalar=-1.0, in1=cand[:],
                                                      op0=ALU.add, op1=ALU.add))
                o.step(nc.vector.tensor_reduce(red[:], cand[:], AX.X, ALU.max))
                o.step(nc.vector.tensor_tensor(cand[:], cand[:], bc(red[:], [P, NT, E]), ALU.is_equal))
                o.step(nc.vector.scalar_tensor_tensor(out=cand[:], in0=cand[:], scalar=-100.0, in1=mid(k.iota[:, 0:E], NT),
                                                      op0=ALU.mult, op1=ALU.add))
                o.step(nc.vector.tensor_reduce(red[:], cand[:], AX.X, ALU.min))
                o.step(nc.vector.tensor_tensor(cand[:], cand[:], bc(red[:], [P, NT, E]), ALU.is_equal))
                o.step(nc.vector.tensor_tensor(gate[:], cand[:], probs[:], ALU.mult))
        experts(k, E, F, lambda e: w1[:, e, :], lambda e, c: w2[:, e, c, :], ACT.Gelu, gate)


def time_mix(k):
    nc, dr = k.nc, k.dram
    normalise(k)
    with Stage(nc) as outer:
        mixed = outer.sb("mixed", [P, 3, T])
        time_mix_average(k, mixed)
        project_add(k, mixed[:, 0, :], k.wT["L1_attn_W_output"][:])


def time_mix_average(k, mixed):
    nc, dr = k.nc, k.dram
    with Stage(nc) as s:
        col = s.sb("col", [P, 8])
        load(k, [(col[:, 0:1], dr["L1_attn_time_decay"].rearrange("(p a) -> p a", a=1)),
                 (col[:, 1:2], dr["L1_attn_time_first"].rearrange("(p a) -> p a", a=1))] +
                [(col[:, 2 + i:3 + i], dr["L1_attn_time_mix_" + n].rearrange("a b (p c) -> p (a b c)", c=1))
                 for i, n in enumerate("kvr")])
        rest = s.sb("rest", [P, 3])
        decay = s.sb("decay", [P, 2])
        hs = s.sb("hs", [P, T + 1])
        kvr = s.sb("kvr", [P, 3, T])
        fall = s.sb("fall", [P, T])
        m = s.sb("m", [P, T + 1])
        keep = s.sb("keep", [P, T])
        new = s.sb("new", [P, T])
        newv = s.sb("newv", [P, T])
        num = s.sb("num", [P, T + 1])
        den = s.sb("den", [P, T + 1])
        c1 = s.sb("c1", [P, T])
        c2 = s.sb("c2", [P, T])
        top = s.sb("top", [P, T])
        uk = s.sb("uk", [P, T])
        order = s.sem("order")
        mixed_ready = s.sem("mixed_ready")
        product = s.sem("product")
        w_ready = s.sem("w_ready")
        to_power = s.sem("to_power")
        powers = s.sem("powers")
        block = s.block()

        @block.tensor
        def _(pe):
            for i, n in enumerate(("key", "value", "receptance")):
                pe.wait_ge(mixed_ready, i + 1)
                for b in range(2):
                    last = nc.tensor.matmul(k.ps[:, 2 * i + b, :], k.wT["L1_attn_W_" + n][:],
                                            mixed[:, i, b * BANK:(b + 1) * BANK], start=True, stop=True)
                last.then_inc(product, 1)

        @block.scalar
        def _(act):
            nc.scalar.activation(decay[:, 0:1], col[:, 0:1], ACT.Exp).then_inc(w_ready, 1)
            act.wait_ge(to_power, 1)
            nc.scalar.activation(keep[:], keep[:], ACT.Exp).then_inc(powers, 1)
            nc.scalar.activation(new[:], new[:], ACT.Exp).then_inc(powers, 1)
            act.wait_ge(to_power, 2)
            nc.scalar.activation(c1[:], c1[:], ACT.Exp).then_inc(powers, 1)
            nc.scalar.activation(c2[:], c2[:], ACT.Exp).then_inc(powers, 1)
            act.wait_ge(product, 3)
            nc.scalar.activation(kvr[:, 2, :], k.ps[:, 4:6, :].rearrange("p a b -> p (a b)"), ACT.Sigmoid).then_inc(powers, 1)

        @block.vector
        def _(dve):
            o = InOrder(dve, order)
            o.step(nc.vector.memset(hs[:, 0:1], 0.0))
            o.step(nc.vector.memset(m[:, 0:1], -1.0e38))
            o.step(nc.vector.memset(num[:, 0:1], 0.0))
            o.step(nc.vector.memset(den[:, 0:1], 0.0))
            o.step(nc.vector.tensor_copy(hs[:, 1:T + 1], k.hT[:]))
            o.step(nc.vector.tensor_scalar(rest[:], col[:, 2:5], -1.0, 1.0, ALU.mult, ALU.add))
            for i in range(3):
                o.step(nc.vector.tensor_scalar(mixed[:, i, :], hs[:, 0:T], rest[:, i:i + 1], None, ALU.mult))
                nc.vector.scalar_tensor_tensor(out=mixed[:, i, :], in0=k.hT[:], scalar=col[:, 2 + i:3 + i],
                                               in1=mixed[:, i, :], op0=ALU.mult, op1=ALU.add).then_inc(mixed_ready, 1)
            dve.wait_ge(w_ready, 1)
            o.step(nc.vector.tensor_scalar(decay[:, 1:2], decay[:, 0:1], -1.0, None, ALU.mult))
            o.step(nc.vector.memset(fall[:], 0.0))
            o.step(nc.vector.tensor_scalar(fall[:], fall[:], decay[:, 1:2], None, ALU.add))
            for i in range(2):
                dve.wait_ge(product, i + 1)
                o.step(nc.vector.tensor_copy(kvr[:, i, :], k.ps[:, 2 * i:2 * i + 2, :].rearrange("p a b -> p (a b)")))
            kk, vv = kvr[:, 0, :], kvr[:, 1, :]
            o.step(nc.vector.tensor_tensor_scan(m[:, 1:T + 1], fall[:], kk, -1.0e38, ALU.add, ALU.max))
            o.step(nc.vector.scalar_tensor_tensor(out=keep[:], in0=m[:, 0:T], scalar=decay[:, 1:2], in1=m[:, 1:T + 1],
                                                  op0=ALU.add, op1=ALU.subtract))
            nc.vector.tensor_tensor(new[:], kk, m[:, 1:T + 1], ALU.subtract).then_inc(to_power, 1)
            o.step(nc.vector.tensor_scalar(uk[:], kk, col[:, 1:2], None, ALU.add))
            o.step(nc.vector.tensor_tensor(top[:], uk[:], m[:, 0:T], ALU.max))
            o.step(nc.vector.tensor_tensor(c1[:], m[:, 0:T], top[:], ALU.subtract))
            nc.vector.tensor_tensor(c2[:], uk[:], top[:], ALU.subtract).then_inc(to_power, 1)
            dve.wait_ge(powers, 2)
            o.step(nc.vector.tensor_tensor(newv[:], new[:], vv, ALU.mult))
            o.step(nc.vector.tensor_tensor_scan(den[:, 1:T + 1], keep[:], new[:], 0.0, ALU.mult, ALU.add))
            o.step(nc.vector.tensor_tensor_scan(num[:, 1:T + 1], keep[:], newv[:], 0.0, ALU.mult, ALU.add))
            dve.wait_ge(powers, 4)
            o.step(nc.vector.tensor_tensor(num[:, 0:T], num[:, 0:T], c1[:], ALU.mult))
            o.step(nc.vector.tensor_tensor(den[:, 0:T], den[:, 0:T], c1[:], ALU.mult))
            o.step(nc.vector.tensor_tensor(newv[:], c2[:], vv, ALU.mult))
            o.step(nc.vector.tensor_tensor(num[:, 0:T], num[:, 0:T], newv[:], ALU.add))
            o.step(nc.vector.tensor_tensor(den[:, 0:T], den[:, 0:T], c2[:], ALU.add))
            o.step(nc.vector.reciprocal(den[:, 0:T], den[:, 0:T]))
            o.step(nc.vector.tensor_tensor(num[:, 0:T], num[:, 0:T], den[:, 0:T], ALU.mult))
            dve.wait_ge(powers, 5)
            o.step(nc.vector.tensor_tensor(mixed[:, 0, :], num[:, 0:T], kvr[:, 2, :], ALU.mult))


def linear_attention(k):
    nc, dr = k.nc, k.dram
    HH, HW = 8, 16
    normalise(k)
    with Stage(nc) as s:
        wrows = s.sb("wrows", [HW, 2 * HH, D])
        proj = s.sb("proj", [HW, HH, D])
        vrows = s.sb("vrows", [P, D])
        vT = s.sb("vT", [P, D])
        same = s.sb("same", [P, P])
        b_out = s.sb("b_out", [P, D])
        load(k, [(wrows[:], dr["L2_attn_w_qkv"][0:2 * D].rearrange("(h j) i -> j h i", j=HW)),
                 (vrows[:], dr["L2_attn_w_qkv"][2 * D:3 * D]),
                 (proj[:], dr["L2_attn_proj"].rearrange("h j f -> j h f")),
                 (same[:], dr["c_same32"]), (b_out[:], row(k, "L2_attn_b_out", D))])
        folded = s.sb("folded", [P, 2 * HH, D])
        with Stage(nc) as g:
            product = g.sem("product")
            kept = g.sem("kept")
            block = g.block()

            @block.tensor
            def _(pe):
                for i in range(2 * HH):
                    last = nc.tensor.matmul(k.ps[:, i // 4, (i % 4) * P:(i % 4 + 1) * P], wrows[:, i, :],
                                            proj[:, i % HH, :], start=True, stop=True)
                    if i % 4 == 3:
                        last.then_inc(product, 1)
                nc.tensor.transpose(k.ps[:, 4, 0:P], vrows[:], k.ident[:]).then_inc(product, 1)

            @block.vector
            def _(dve):
                for b in range(4):
                    dve.wait_ge(product, b + 1)
                    nc.vector.tensor_copy(folded[:, 4 * b:4 * b + 4, :],
                                          k.ps[:, b, :].rearrange("p (i f) -> p i f", f=D)).then_inc(kept, 1)
                dve.wait_ge(product, 5)
                nc.vector.tensor_copy(vT[:], k.ps[:, 4, 0:P]).then_inc(kept, 1)
        v = s.sb("v", [P, NT, D])
        project(k, k.hT, NT, vT[:], D, v)
        out = s.sb("out", [P, NT, D])
        outT = s.sb("outT", [P, T])
        with Stage(nc) as g:
            v1 = g.sb("v1", [P, NT, HH, HW + 1])
            low = g.sb("low", [P, 2 * T])
            feat = g.sb("feat", [P, 2 * T])
            prod = g.sb("prod", [P, NT, P])
            z = g.sb("z", [P, NT])
            order = g.sem("order")
            qk = g.sem("qk")
            low_ready = g.sem("low_ready")
            powers = g.sem("powers")
            feat_ready = g.sem("feat_ready")
            scores = g.sem("scores")
            prod_ready = g.sem("prod_ready")
            sums = g.sem("sums")
            done = g.sem("done")
            block = g.block()

            @block.tensor
            def _(pe):
                for h in range(HH):
                    if h >= 1:
                        pe.wait_ge(feat_ready, h)
                    for i in range(2):
                        for b in range(2):
                            last = nc.tensor.matmul(k.ps[:, 2 * i + b, :], folded[:, i * HH + h, :],
                                                    k.hT[:, b * BANK:(b + 1) * BANK], start=True, stop=True)
                    last.then_inc(qk, 1)
                    pe.wait_ge(feat_ready, h + 1)
                    if h >= 1:
                        pe.wait_ge(prod_ready, h)
                    for t in range(NT):
                        last = nc.tensor.matmul(k.ps[:, 4 + t // 4, (t % 4) * P:(t % 4 + 1) * P],
                                                feat[:, T + t * P:T + (t + 1) * P], feat[:, t * P:(t + 1) * P],
                                                start=True, stop=True)
                    last.then_inc(scores, 1)
                    pe.wait_ge(prod_ready, h + 1)
                    if h >= 1:
                        pe.wait_ge(done, h)
                    for t in range(NT):
                        last = nc.tensor.matmul(k.ps[:, 6, t * 32:t * 32 + HW + 1], prod[:, t, :], v1[:, t, h, :],
                                                start=True, stop=True)
                    last.then_inc(sums, 1)

            @block.scalar
            def _(act):
                for h in range(HH):
                    act.wait_ge(low_ready, h + 1)
                    nc.scalar.activation(low[:], low[:], ACT.Exp).then_inc(powers, 1)

            @block.vector
            def _(dve):
                o = InOrder(dve, order)
                o.step(nc.vector.memset(v1[:], 1.0))
                o.step(nc.vector.tensor_copy(v1[:, :, :, 0:HW], v[:].rearrange("p t (h d) -> p t h d", h=HH)))
                for h in range(HH):
                    both = k.ps[:, 0:4, :].rearrange("p a b -> p (a b)")
                    dve.wait_ge(qk, h + 1)
                    nc.vector.tensor_scalar(low[:], both, 0.0, None, ALU.min).then_inc(low_ready, 1)
                    dve.wait_ge(powers, h + 1)
                    if h >= 1:
                        dve.wait_ge(scores, h)
                    nc.vector.scalar_tensor_tensor(out=feat[:], in0=both, scalar=0.0, in1=low[:],
                                                   op0=ALU.max, op1=ALU.add).then_inc(feat_ready, 1)
                    dve.wait_ge(scores, h + 1)
                    if h >= 1:
                        dve.wait_ge(sums, h)
                    for b in range(2):
                        last = nc.vector.tensor_tensor(prod[:, 4 * b:4 * b + 4, :],
                                                       k.ps[:, 4 + b, :].rearrange("p (t n) -> p t n", n=P),
                                                       mid(same[:], 4), ALU.mult)
                        if b == 0:
                            o.step(last)
                    last.then_inc(prod_ready, 1)
                    dve.wait_ge(sums, h + 1)
                    acc = k.ps[:, 6, 0:NT * 32].rearrange("p (t n) -> p t n", n=32)
                    o.step(nc.vector.tensor_scalar(z[:], acc[:, :, HW], 1e-8, None, ALU.add))
                    o.step(nc.vector.reciprocal(z[:], z[:]))
                    nc.vector.tensor_tensor(out[:, :, h * HW:(h + 1) * HW], acc[:, :, 0:HW], bc(z[:], [P, NT, HW]),
                                            ALU.mult).then_inc(done, 1)
                    dve.wait_ge(done, h + 1)
        turn(k, out, outT)
        project_add(k, outT, k.wT["L2_attn_w_out"][:], b_out[:])


def retention(k):
    nc, dr = k.nc, k.dram
    L, F, HH, HW = 4, 256, 8, 16
    normalise(k)
    with Stage(nc) as s:
        X = s.sb("X", [P, NT, D])
        table = s.sb("table", [P, 2, NT, 8])
        within = s.sb("within", [P, HH, P])
        powers_in = s.sb("powers_in", [P, 2, HH])
        blocks = s.sb("blocks", [P, P + 1])
        head_of = s.sb("head_of", [P, HH])
        ln = s.sb("ln", [P, 2, D])
        load(k, [(table[:], dr["c_rot16"]), (within[:], dr["c_within"]), (powers_in[:], dr["c_powers"]),
                 (blocks[:], dr["c_blocks"]), (head_of[:], dr["c_head_of"]),
                 (ln[:, 0, :], row(k, "L3_attn_ln_scale", D)), (ln[:, 1, :], row(k, "L3_attn_ln_bias", D))])
        with Stage(nc) as g:
            done = g.sem("done")
            block = g.block()

            @block.vector
            def _(dve):
                nc.vector.tensor_copy(X[:], k.h[:]).then_inc(done, 1)
        outer, k.x = k.x, X
        for i in range(L):
            normalise(k, (ln[:, 0, :], ln[:, 1, :]))
            retention_layer(k, i, table, within, powers_in, blocks, head_of)
            normalise(k, (ln[:, 0, :], ln[:, 1, :]))
            with Stage(nc) as g:
                w1 = g.sb("w1", [P, F])
                w2 = g.sb("w2", [P, F // P, D])
                load(k, [(w1[:], dr["L3_attn_W1"][i]), (w2[:], dr["L3_attn_W2"][i].rearrange("(c p) d -> p c d", p=P))])
                experts(k, 1, F, lambda e: w1[:], lambda e, c: w2[:, c, :], ACT.Gelu_apprx_tanh)
        k.x = outer
        with Stage(nc) as g:
            done = g.sem("done")
            block = g.block()

            @block.vector
            def _(dve):
                nc.vector.tensor_tensor(k.x[:], k.x[:], X[:], ALU.add).then_inc(done, 1)


def retention_layer(k, i, table, within, powers_in, blocks, head_of):
    nc, dr = k.nc, k.dram
    HH, HW = 8, 16
    with Stage(nc) as s:
        w = s.sb("w", [P, 4, D])
        wo = s.sb("wo", [P, D])
        gn = s.sb("gn", [P, 2, D])
        load(k, [(w[:, j, :], dr["L3_attn_W" + n][i]) for j, n in enumerate("qkvg")] +
                [(wo[:], dr["L3_attn_Wo"][i]),
                 (gn[:, 0, :], dr["L3_attn_gn_scale"][i].partition_broadcast(P)),
                 (gn[:, 1, :], dr["L3_attn_gn_bias"][i].partition_broadcast(P))])
        qkvg = s.sb("qkvg", [P, NT, 4 * D])
        project(k, k.hT, NT, w[:].rearrange("p a b -> p (a b)"), 4 * D, qkvg)
        rot = s.sb("rot", [P, 4, NT, D])
        out = s.sb("out", [P, NT, D])
        with Stage(nc) as g:
            t1 = g.sb("t1", [P, NT, 8 * 8])
            t2 = g.sb("t2", [P, NT, 8 * 8])
            turnedT = g.sb("turnedT", [P, 3, T])
            wide_q = g.sb("wide_q", [P, NT, HH, P])
            state = g.sb("state", [P, NT, D])
            prod = g.sb("prod", [P, 2, HH, P])
            kv = g.sb("kv", [P, NT, D])
            order = g.sem("order")
            rot_ready = g.sem("rot_ready")
            turned = g.sem("turned")
            turned_kept = g.sem("turned_kept")
            kv_product = g.sem("kv_product")
            state_ready = g.sem("state_ready")
            scores = g.sem("scores")
            prod_ready = g.sem("prod_ready")
            sums = g.sem("sums")
            taken = g.sem("taken")
            block = g.block()

            def half(ap, odd):
                return ap.rearrange("p t (h f two) -> p t h f two", h=HH, two=2)[:, :, :, :, odd]

            def four(ap):
                return ap[:].rearrange("p t (h f) -> p t h f", h=HH)

            @block.vector
            def _(dve):
                o = InOrder(dve, order)
                cos, sin = (table[:, a].unsqueeze(2).to_broadcast([P, NT, HH, 8]) for a in range(2))
                for j in range(2):
                    src = qkvg[:, :, j * D:(j + 1) * D]
                    x1, x2 = half(src, 0), half(src, 1)
                    o.step(nc.vector.tensor_tensor(four(t1), x1, cos, ALU.mult))
                    o.step(nc.vector.tensor_tensor(four(t2), x2, sin, ALU.mult))
                    o.step(nc.vector.tensor_tensor(half(rot[:, j], 0), four(t1), four(t2), ALU.subtract if j == 0 else ALU.add))
                    o.step(nc.vector.tensor_tensor(four(t1), x1, sin, ALU.mult))
                    o.step(nc.vector.tensor_tensor(four(t2), x2, cos, ALU.mult))
                    if j == 0:
                        o.step(nc.vector.tensor_tensor(half(rot[:, j], 1), four(t1), four(t2), ALU.add))
                    else:
                        o.step(nc.vector.tensor_tensor(half(rot[:, j], 1), four(t2), four(t1), ALU.subtract))
                for j in range(2):
                    wide = powers_in[:, j, :].unsqueeze(1).unsqueeze(3).to_broadcast([P, NT, HH, HW])
                    o.step(nc.vector.tensor_tensor(rot[:, 2 + j].rearrange("p t (h d) -> p t h d", h=HH),
                                                   rot[:, j].rearrange("p t (h d) -> p t h d", h=HH), wide, ALU.mult))
                nc.vector.memset(state[:, 0, :], 0.0).then_inc(rot_ready, 1)
                for a in range(3):
                    dve.wait_ge(turned, a + 1)
                    nc.vector.tensor_copy(turnedT[:, a, :], k.ps[:, 2 * a:2 * a + 2, :].rearrange("p a b -> p (a b)")).then_inc(turned_kept, 1)
                dve.wait_ge(turned_kept, 3)
                for h in range(HH):
                    nc.vector.tensor_scalar(wide_q[:, :, h, :], turnedT[:, 0, :].rearrange("p (t n) -> p t n", n=P),
                                            head_of[:, h:h + 1], None, ALU.mult).then_inc(turned_kept, 1)
                dve.wait_ge(kv_product, 1)
                for b in range(2):
                    o.step(nc.vector.tensor_tensor(kv[:, 4 * b:4 * b + 4, :],
                                                   k.ps[:, 6 + b, :].rearrange("p (t n) -> p t n", n=P),
                                                   mid(blocks[:, 0:P], 4), ALU.mult))
                for t in range(1, NT):
                    nc.vector.scalar_tensor_tensor(out=state[:, t, :], in0=state[:, t - 1, :], scalar=blocks[:, P:P + 1],
                                                   in1=kv[:, t - 1, :], op0=ALU.mult, op1=ALU.add).then_inc(state_ready, 1)
                    dve.wait_ge(state_ready, t)
                for t in range(NT):
                    dve.wait_ge(scores, t + 1)
                    if t >= 2:
                        dve.wait_ge(sums, t - 1)
                    nc.vector.tensor_tensor(prod[:, t % 2], k.ps[:, 2 * (t % 2):2 * (t % 2) + 2, :].rearrange("p a (h n) -> p (a h) n", n=P),
                                            within[:], ALU.mult).then_inc(prod_ready, 1)
                for b in range(2):
                    dve.wait_ge(sums, 4 * b + 4)
                    nc.vector.tensor_copy(out[:, 4 * b:4 * b + 4, :],
                                          k.ps[:, 4 + b, :].rearrange("p (t n) -> p t n", n=P)).then_inc(taken, 1)

            @block.tensor
            def _(pe):
                pe.wait_ge(rot_ready, 1)
                for a in range(3):
                    for t in range(NT):
                        last = nc.tensor.transpose(k.ps[:, 2 * a + t // 4, (t % 4) * P:(t % 4 + 1) * P], rot[:, a, t, :], k.ident[:])
                    last.then_inc(turned, 1)
                for t in range(NT):
                    last = nc.tensor.matmul(k.ps[:, 6 + t // 4, (t % 4) * P:(t % 4 + 1) * P], rot[:, 3, t, :],
                                            qkvg[:, t, 2 * D:3 * D], start=True, stop=True)
                last.then_inc(kv_product, 1)
                pe.wait_ge(turned_kept, 3 + HH)
                pe.wait_ge(state_ready, NT - 1)

                def weigh(t):
                    if t >= 2:
                        pe.wait_ge(prod_ready, t - 1)
                    for b in range(2):
                        last = nc.tensor.matmul(k.ps[:, 2 * (t % 2) + b, :], turnedT[:, 1, t * P:(t + 1) * P],
                                                wide_q[:, t, 4 * b:4 * b + 4, :], start=True, stop=True)
                    last.then_inc(scores, 1)

                def add_up(t):
                    acc = k.ps[:, 4 + t // 4, (t % 4) * P:(t % 4 + 1) * P]
                    nc.tensor.matmul(acc, turnedT[:, 2, t * P:(t + 1) * P], state[:, t, :], start=True, stop=False,
                                     skip_group_check=True)
                    pe.wait_ge(prod_ready, t + 1)
                    for h in range(HH):
                        last = nc.tensor.matmul(acc[:, h * HW:(h + 1) * HW], prod[:, t % 2, h, :],
                                                qkvg[:, t, 2 * D + h * HW:2 * D + (h + 1) * HW],
                                                start=False, stop=True, skip_group_check=True)
                    last.then_inc(sums, 1)

                for t in range(NT):
                    weigh(t)
                    if t >= 1:
                        add_up(t - 1)
                add_up(NT - 1)
        with Stage(nc) as g:
            red = g.sb("red", [P, NT * HH])
            sq = g.sb("sq", [P, NT * HH, HW])
            var = g.sb("var", [P, NT * HH])
            silu = g.sb("silu", [P, NT, D])
            order = g.sem("order")
            var_ready = g.sem("var_ready")
            roots = g.sem("roots")
            gated = g.sem("gated")
            block = g.block()
            y = out[:].rearrange("p t (h d) -> p (t h) d", d=HW)

            @block.scalar
            def _(act):
                nc.scalar.activation(silu[:], qkvg[:, :, 3 * D:4 * D], ACT.Silu).then_inc(gated, 1)
                act.wait_ge(var_ready, 1)
                nc.scalar.activation(var[:], var[:], ACT.Sqrt).then_inc(roots, 1)

            @block.vector
            def _(dve):
                o = InOrder(dve, order)
                o.step(nc.vector.tensor_reduce(red[:], y, AX.X, ALU.add))
                o.step(nc.vector.tensor_scalar(red[:], red[:], 1.0 / HW, None, ALU.mult))
                o.step(nc.vector.tensor_tensor(y, y, bc(red[:], [P, NT * HH, HW]), ALU.subtract))
                o.step(nc.vector.tensor_tensor(sq[:], y, y, ALU.mult))
                o.step(nc.vector.tensor_reduce(red[:], sq[:], AX.X, ALU.add))
                nc.vector.tensor_scalar(var[:], red[:], 1.0 / HW, 1e-5, ALU.mult, ALU.add).then_inc(var_ready, 1)
                dve.wait_ge(roots, 1)
                o.step(nc.vector.reciprocal(red[:], var[:]))
                o.step(nc.vector.tensor_tensor(y, y, bc(red[:], [P, NT * HH, HW]), ALU.mult))
                o.step(nc.vector.tensor_tensor(out[:], out[:], mid(gn[:, 0, :], NT), ALU.mult))
                o.step(nc.vector.tensor_tensor(out[:], out[:], mid(gn[:, 1, :], NT), ALU.add))
                dve.wait_ge(gated, 1)
                o.step(nc.vector.tensor_tensor(out[:], out[:], silu[:], ALU.mult))
        outT = s.sb("outT", [P, T])
        turn(k, out, outT)
        project_add(k, outT, wo[:])


def routed_ffn(k):
    nc, dr = k.nc, k.dram
    E, F, TOP = 32, 64, 4
    PLACES = 2 * (2 * 256) * TOP // E
    PAIRS = E // 2
    normalise(k)
    with Stage(nc) as s:
        gateT = s.sb("gateT", [E, T])
        spread = s.sb("spread", [E, PAIRS, P])
        wa = s.sb("wa", [P, E, F])
        wb = s.sb("wb", [P, E, F])
        wc = s.sb("wc", [P, PAIRS, D])
        with Stage(nc) as g:
            raw = g.sb("raw", [P, 3, E * F], BF16)
            before = g.sb("before", [P, P])
            bias = g.sb("bias", [P, E])
            load(k, [(raw[:, 0, :].rearrange("p (e f) -> p e f", e=E), dr["L2_ffn_W1"].rearrange("e d f -> d e f")),
                     (raw[:, 1, :].rearrange("p (e f) -> p e f", e=E), dr["L2_ffn_W3"].rearrange("e d f -> d e f")),
                     (raw[:, 2, :].rearrange("p (e d) -> p e d", d=D), dr["L2_ffn_W2"].rearrange("(q b) i d -> (b i) q d", b=2)),
                     (before[:], dr["c_before"]), (bias[:], row(k, "L2_ffn_bias", E)), (spread[:], dr["c_spread"])])
            scores = g.sb("scores", [P, NT, E])
            keys = g.sb("keys", [P, NT, E])
            top8 = g.sb("top8", [P, NT, 8])
            place = g.sb("place", [P, NT, 8], U32)
            placef = g.sb("placef", [P, NT, 8])
            sel = g.sb("sel", [P, NT, E])
            eq = g.sb("eq", [P, NT, E])
            red = g.sb("red", [P, NT])
            order = g.sem("order")
            wide = g.sem("wide")
            logits = g.sem("logits")
            sig = g.sem("sig")
            sel_ready = g.sem("sel_ready")
            counts = g.sem("counts")
            gate_ready = g.sem("gate_ready")
            turned = g.sem("turned")
            block = g.block()

            @block.gpsimd
            def _(pool):
                nc.gpsimd.tensor_copy(wa[:].rearrange("p e f -> p (e f)"), raw[:, 0, :]).then_inc(wide, 1)
                nc.gpsimd.tensor_copy(wb[:].rearrange("p e f -> p (e f)"), raw[:, 1, :]).then_inc(wide, 1)
                nc.gpsimd.tensor_copy(wc[:].rearrange("p e f -> p (e f)"), raw[:, 2, :]).then_inc(wide, 1)

            @block.tensor
            def _(pe):
                for t in range(NT):
                    last = nc.tensor.matmul(k.ps[:, 0, t * E:(t + 1) * E], k.hT[:, t * P:(t + 1) * P],
                                            k.wT["L2_ffn_gate_w"][:], start=True, stop=True)
                last.then_inc(logits, 1)
                pe.wait_ge(sel_ready, 1)
                nc.tensor.matmul(k.ps[:, 1, 0:NT * E], before[:], sel[:].rearrange("p t e -> p (t e)"), start=True,
                                 stop=False, skip_group_check=True)
                for a in range(1, NT):
                    last = nc.tensor.matmul(k.ps[:, 1, a * E:NT * E], k.ones[:],
                                            sel[:, 0:NT - a, :].rearrange("p t e -> p (t e)"), start=False,
                                            stop=(a == NT - 1), skip_group_check=True)
                last.then_inc(counts, 1)
                pe.wait_ge(gate_ready, 1)
                for t in range(NT):
                    last = nc.tensor.transpose(k.ps[0:E, 2 + t // 4, (t % 4) * P:(t % 4 + 1) * P], sel[:, t, :], k.ident[:])
                last.then_inc(turned, 1)

            @block.scalar
            def _(act):
                act.wait_ge(logits, 1)
                nc.scalar.activation(scores[:].rearrange("p t e -> p (t e)"), k.ps[:, 0, 0:NT * E], ACT.Sigmoid).then_inc(sig, 1)

            @block.vector
            def _(dve):
                o = InOrder(dve, order)
                dve.wait_ge(sig, 1)
                o.step(nc.vector.tensor_tensor(keys[:], scores[:], mid(bias[:], NT), ALU.add))
                for t in range(NT):
                    o.step(nc.vector.max(top8[:, t, :], keys[:, t, :]))
                    o.step(nc.vector.max_index(place[:, t, :], top8[:, t, :], keys[:, t, :]))
                o.step(nc.vector.tensor_copy(placef[:], place[:]))
                for j in range(TOP):
                    dst = sel if j == 0 else eq
                    o.step(nc.vector.tensor_tensor(dst[:], mid(k.iota[:, 0:E], NT), bc(placef[:, :, j], [P, NT, E]), ALU.is_equal))
                    if j:
                        last = nc.vector.tensor_tensor(sel[:], sel[:], eq[:], ALU.add)
                        if j < TOP - 1:
                            o.step(last)
                last.then_inc(sel_ready, 1)
                dve.wait_ge(sel_ready, 1)
                o.step(nc.vector.tensor_tensor(scores[:], scores[:], sel[:], ALU.mult))
                o.step(nc.vector.tensor_reduce(red[:], scores[:], AX.X, ALU.add))
                o.step(nc.vector.tensor_scalar(red[:], red[:], 1e-12, None, ALU.max))
                o.step(nc.vector.reciprocal(red[:], red[:]))
                o.step(nc.vector.tensor_tensor(scores[:], scores[:], bc(red[:], [P, NT, E]), ALU.mult))
                dve.wait_ge(counts, 1)
                o.step(nc.vector.tensor_scalar(eq[:].rearrange("p t e -> p (t e)"), k.ps[:, 1, 0:NT * E], float(PLACES), None, ALU.is_lt))
                nc.vector.tensor_tensor(sel[:], scores[:], eq[:], ALU.mult).then_inc(gate_ready, 1)
                dve.wait_ge(turned, 1)
                o.step(nc.vector.tensor_copy(gateT[:], k.ps[0:E, 2:4, :].rearrange("p a b -> p (a b)")))
        with Stage(nc) as g:
            act_a = g.sb("act_a", [P, 2, T])
            hid = g.sb("hid", [P, 2, T])
            order = g.sem("order")
            up = g.sem("up")
            silu = g.sem("silu")
            product = g.sem("product")
            hid_ready = g.sem("hid_ready")
            used = g.sem("used")
            block = g.block()
            flat = [k.ps[:, 2 * a:2 * a + 2, :].rearrange("p a b -> p (a b)") for a in range(3)]

            @block.tensor
            def _(pe):
                def up_products(q):
                    if q >= 1:
                        pe.wait_ge(hid_ready, q)
                    m = P if q < PAIRS else F
                    for b in range(2):
                        ht = k.hT[:, b * BANK:(b + 1) * BANK]
                        a1 = wa[:, 2 * q:2 * q + 2, :] if q < PAIRS else k.wT["L2_ffn_sw1"][:]
                        a3 = wb[:, 2 * q:2 * q + 2, :] if q < PAIRS else k.wT["L2_ffn_sw3"][:]
                        nc.tensor.matmul(k.ps[0:m, b, :], a1, ht, start=True, stop=True)
                        last = nc.tensor.matmul(k.ps[0:m, 2 + b, :], a3, ht, start=True, stop=True)
                        if q < PAIRS:
                            last = nc.tensor.matmul(k.ps[:, 4 + b, :], spread[:, q, :], gateT[:, b * BANK:(b + 1) * BANK],
                                                    start=True, stop=True)
                    last.then_inc(up, 1)

                def down_product(q):
                    pe.wait_ge(hid_ready, q + 1)
                    for t in range(NT):
                        m = P if q < PAIRS else F
                        w = wc[:, q, :] if q < PAIRS else k.wT["L2_ffn_sw2"][:]
                        last = nc.tensor.matmul(k.ps[:, 6 + t // 4, (t % 4) * P:(t % 4 + 1) * P],
                                                hid[0:m, q % 2, t * P:(t + 1) * P], w, start=(q == 0 and t % 4 == 0), stop=(q == PAIRS),
                                                skip_group_check=True)
                    last.then_inc(used, 1)

                for q in range(PAIRS + 1):
                    up_products(q)
                    if q >= 1:
                        down_product(q - 1)
                down_product(PAIRS)

            @block.scalar
            def _(act):
                for q in range(PAIRS + 1):
                    m = P if q < PAIRS else F
                    act.wait_ge(up, q + 1)
                    if q >= 2:
                        act.wait_ge(hid_ready, q - 1)
                    nc.scalar.activation(act_a[0:m, q % 2, :], flat[0][0:m], ACT.Silu).then_inc(silu, 1)

            @block.vector
            def _(dve):
                for q in range(PAIRS + 1):
                    m = P if q < PAIRS else F
                    dve.wait_ge(silu, q + 1)
                    dve.wait_ge(up, q + 1)
                    if q >= 2:
                        dve.wait_ge(used, q - 1)
                    one = nc.vector.tensor_tensor(hid[0:m, q % 2, :], flat[1][0:m], act_a[0:m, q % 2, :], ALU.mult)
                    if q < PAIRS:
                        one.then_inc(product, 1)
                        dve.wait_ge(product, q + 1)
                        one = nc.vector.tensor_tensor(hid[:, q % 2, :], flat[2], hid[:, q % 2, :], ALU.mult)
                    one.then_inc(hid_ready, 1)
                o = InOrder(dve, order)
                for b in range(2):
                    part = k.x[:, 4 * b:4 * b + 4, :]
                    dve.wait_ge(used, PAIRS + 1)
                    o.step(nc.vector.tensor_tensor(part, part, k.ps[:, 6 + b, :].rearrange("p (t d) -> p t d", d=D), ALU.add))


PARTS = 6
ONE = PARTS * HD
SHIFT = ONE + 1
ROWS = SHIFT + 3
SLOT = 64
LOW8 = -57344.0
LOWER = 2.0 ** 14
BYTE8 = 251.0
STEP8 = 2.0 ** -8
PAIRS = H // 2


def attend(k, tiles, q, keys, values, out, key_mask=None, mask8=None):
    nc = k.nc
    n_keys = tiles * P
    kgroups = [range(a, min(a + 8, tiles)) for a in range(0, tiles, 8)]
    chunks = [(a, min(a + BANK, n_keys)) for a in range(0, n_keys, BANK)]
    NC, NG = len(chunks), len(kgroups)
    prepare = ([("keys", g) for g in range(NG)] + [("queries", 0)] +
               [("chunk", a, t, c) for a in range(2) for t in range(NT) for c in range(NC)] + [("queries", 1)])
    G = len(prepare)
    STEPS = 6 + (4 if mask8 is not None else 0)

    def before(p, a, b):
        if isinstance(p, int) and p == 0:
            return a
        return 2 * a + (p - 1) * (a + b)

    def phases(eng, phase, straight=False):
        phase(0, 0)
        if straight:
            for p in range(1, PAIRS):
                phase(p, p % 2)
            return
        with eng.Fori(0, PAIRS // 2 - 1) as i:
            phase(2 * i + 1, 1)
            phase(2 * i + 2, 0)
        phase(PAIRS - 1, 1)

    with Stage(nc) as s:
        kstack = s.sb("kstack", [P, tiles, 2, SLOT], BF16)
        qstack = s.sb("qstack", [P, 2, NT, 2, SLOT], BF16)
        kturned = s.sb("kturned", [P, 2, n_keys], BF16)
        qturned = s.sb("qturned", [P, 2, T], BF16)
        vstack = s.sb("vstack", [P, 2, tiles, 2, HD + 1])
        left = s.sb("left", [P, max(tiles, NT), 2, HD])
        probs = s.sb("probs", [P, 4, T])
        maxima = s.sb("maxima", [P, 2 * NT, NC])
        shift = s.sb("shift", [P, 2 * NT])
        shift_left = s.sb("shift_left", [P, 2 * NT])
        empty = s.sb("empty", [P, 2, 2 * NT])
        sums = s.sb("sums", [P, BANK])
        inverse = s.sb("inverse", [P, 2 * NT])
        junk = s.sb("junk", [P, 4, BANK], BF16)
        cleared = s.sem("cleared")
        pool_order = s.sem("pool_order")
        stacks_ready = s.sem("stacks_ready")
        values_ready = s.sem("values_ready")
        ring_filled = s.sem("ring_filled")
        ring_free = s.sem("ring_free")
        dve_order = s.sem("dve_order")
        shift_ready = s.sem("shift_ready")
        scores_filled = s.sem("scores_filled")
        probs_ready = s.sem("probs_ready")
        unit_done = s.sem("unit_done")
        sums_taken = s.sem("sums_taken")
        block = s.block()

        def ring(j):
            return 5 + j % 3

        def score_buffer(n):
            return k.ps[:, 2 * (n % 2):2 * (n % 2) + 2, :].rearrange("p a b -> p (a b)")

        @block.gpsimd
        def _(pool):
            nc.gpsimd.memset(kstack[:], 0.0).then_inc(cleared, 1)
            nc.gpsimd.memset(qstack[:], 0.0).then_inc(cleared, 1)
            nc.gpsimd.memset(vstack[:], 1.0).then_inc(cleared, 1)
            nc.gpsimd.memset(sums[:], 0.0).then_inc(cleared, 1)
            pool.wait_ge(cleared, 4)
            nc.gpsimd.memset(kstack[:, :, :, SHIFT:ROWS], 1.0).then_inc(cleared, 1)
            nc.gpsimd.memset(qstack[:, :, :, :, ONE:ONE + 1], 1.0).then_inc(cleared, 1)
            n_clear = 6
            if key_mask is not None:
                nc.gpsimd.tensor_copy(kstack[:, :, :, ONE], bc(key_mask, [P, tiles, 2])).then_inc(cleared, 1)
                n_clear = 7
            pool.wait_ge(cleared, n_clear)

            def split(o, src, stack, first, second, third, last_step=None):
                rest = left[:, 0:src.shape[1]]

                def slot(i):
                    return stack[:, :, :, i * HD:(i + 1) * HD]
                o.step(nc.gpsimd.tensor_copy(slot(first[0]), src))
                o.step(nc.gpsimd.tensor_tensor(rest, src, slot(first[0]), ALU.subtract))
                o.step(nc.gpsimd.tensor_copy(slot(second[0]), rest))
                o.step(nc.gpsimd.tensor_tensor(rest, rest, slot(second[0]), ALU.subtract))
                o.step(nc.gpsimd.tensor_copy(slot(third[0]), rest))
                copies = [(slot(i), slot(part[0])) for part in (first, second, third) for i in part[1:]]
                for dst, src2 in copies[:-1]:
                    o.step(nc.gpsimd.tensor_copy(dst, src2))
                return copies[-1]

            per_pair = 2 * 8 - 1

            def stacks(pp, par):
                o = InOrder(pool, pool_order, pp * per_pair)
                src = keys[:, :, bass.ds(16 * pp, 16)].rearrange("p t (a d) -> p t a d", a=2)
                dst, last = split(o, src, kstack, (0, 1, 2), (3, 4), (5,))
                o.step(nc.gpsimd.tensor_copy(dst, last))
                src = q[:, :, bass.ds(16 * pp, 16)].rearrange("p t (a d) -> p t a d", a=2)
                dst, last = split(o, src, qstack[:, par], (0, 3, 5), (1, 4), (2,))
                nc.gpsimd.tensor_copy(dst, last).then_inc(stacks_ready, 1)
                pool.wait_ge(stacks_ready, pp + 1)

            def value_stack(pp, par):
                src = values[:, :, bass.ds(16 * pp, 16)].rearrange("p t (a d) -> p t a d", a=2)
                nc.gpsimd.tensor_copy(vstack[:, par, :, :, 0:HD], src).then_inc(values_ready, 1)

            value_stack(0, 0)
            stacks(0, 0)
            value_stack(1, 1)
            pool.wait_ge(ring_filled, NG)
            stacks(1, 1)
            pool.wait_ge(unit_done, tiles)
            value_stack(2, 0)
            pool.wait_ge(ring_filled, G + NG)
            stacks(2, 0)

            def later(pp, par):
                pool.wait_ge(ring_filled, before(pp - 2, G, 1) + 1 + NG)
                stacks(pp, par)
                pool.wait_ge(unit_done, (pp - 1) * tiles)
                value_stack(pp, par)

            for pp in range(3, PAIRS):
                later(pp, pp % 2)

        @block.tensor
        def _(pe):
            def ring_item(item, pp, par, base, j):
                bank = ring(j)
                pe.wait_ge(ring_free, base + max(j - 2, 0)) if not (isinstance(base, int) and base + max(j - 2, 0) == 0) else None
                turned = k.ps[:, bank, :].bitcast(BF16)
                if item[0] == "keys":
                    if item[1] == 0:
                        pe.wait_ge(stacks_ready, pp + 1)
                    for m, t in enumerate(kgroups[item[1]]):
                        last = nc.tensor.transpose(turned[:, m * P:(m + 1) * P],
                                                   kstack[:, t].rearrange("p a r -> p (a r)"), k.ident16[:])
                elif item[0] == "queries":
                    if item[1] == 1:
                        pe.wait_ge(shift_ready, pp + 1)
                    for t in range(NT):
                        last = nc.tensor.transpose(turned[:, t * P:(t + 1) * P],
                                                   qstack[:, par, t].rearrange("p a r -> p (a r)"), k.ident16[:])
                elif item[0] == "chunk":
                    _, a, t, c = item
                    if (a, t, c) == (0, 0, 0):
                        pe.wait_ge(ring_free, base + j)
                    lo, hi = chunks[c]
                    rows = slice(a * SLOT, a * SLOT + SHIFT)
                    last = nc.tensor.matmul(k.ps[:, bank, 0:hi - lo], qturned[rows, par, t * P:(t + 1) * P],
                                            kturned[rows, par, lo:hi], start=True, stop=True)
                else:
                    pe.wait_ge(sums_taken, 4 * (pp + 1))
                    for m in range(4):
                        last = nc.tensor.transpose(k.ps[:, bank, m * P:(m + 1) * P], sums[:, m * P:(m + 1) * P], k.ident[:])
                last.then_inc(ring_filled, 1)

            def scores(p, par, n):
                t, a = divmod(n, 2)
                if n >= 2 or not (isinstance(p, int) and p == 0):
                    pe.wait_ge(probs_ready, 2 * tiles * p + n - 1)
                rows = slice(a * SLOT, a * SLOT + ROWS)
                for b in range(2):
                    last = nc.tensor.matmul(k.ps[:, 2 * (n % 2) + b, :], kturned[rows, par, t * P:(t + 1) * P],
                                            qturned[rows, par, b * BANK:(b + 1) * BANK], start=True,
                                            stop=(mask8 is None), skip_group_check=True)
                    if mask8 is not None:
                        for m in range(4):
                            last = nc.tensor.matmul(k.ps[:, 2 * (n % 2) + b, m * P:(m + 1) * P],
                                                    mask8[:, 4 * b + m, t * P:(t + 1) * P], k.lower[:],
                                                    start=False, stop=True, skip_group_check=True)
                last.then_inc(scores_filled, 1)

            def weigh(p, par, t):
                if t == 0:
                    pe.wait_ge(values_ready, p + 1)
                    if not (isinstance(p, int) and p == 0):
                        pe.wait_ge(sums_taken, 4 * p)
                pe.wait_ge(probs_ready, 2 * tiles * p + 2 * t + 2)
                for a in range(2):
                    for b in range(2):
                        at = 32 * (2 * a + b)
                        last = nc.tensor.matmul(k.ps[at:at + HD + 1, 4, :], vstack[:, par, t, a, :],
                                                probs[:, (2 * tiles * par + 2 * t + a) % 4, b * BANK:(b + 1) * BANK],
                                                start=(t == 0), stop=(t == tiles - 1), skip_group_check=True)
                last.then_inc(unit_done, 1)

            for j, item in enumerate(prepare):
                ring_item(item, 0, 0, 0, j)

            def phase(p, par):
                base = before(p, G, 1)
                alone = isinstance(p, int)
                items = [] if alone and p == 0 else [(("sums",), p - 1, 1 - par)]
                if not (alone and p == PAIRS - 1):
                    items += [(item, p + 1, 1 - par) for item in prepare]
                pe.wait_ge(ring_free, base)
                scores(p, par, 0)
                scores(p, par, 1)
                at = 0
                for t in range(tiles):
                    upto = len(items) * (t + 1) // tiles
                    for j in range(at, upto):
                        ring_item(items[j][0], items[j][1], items[j][2], base, j)
                    at = upto
                    if t + 1 < tiles:
                        scores(p, par, 2 * t + 2)
                        scores(p, par, 2 * t + 3)
                    weigh(p, par, t)

            phases(pe, phase)
            ring_item(("sums",), PAIRS - 1, 1, before(PAIRS - 1, G, 1) + 1, 0)

        @block.scalar
        def _(act):
            def phase(p, par):
                first = isinstance(p, int) and p == 0
                for n in range(2 * tiles):
                    act.wait_ge(scores_filled, 2 * tiles * p + n + 1)
                    if n >= 4 or not first:
                        act.wait_ge(unit_done, tiles * p + n // 2 - 1)
                    nc.scalar.activation(probs[:, (2 * tiles * par + n) % 4, :], score_buffer(n), ACT.Exp,
                                         scale=(1.0 if mask8 is None else 1.0 / STEP8)).then_inc(probs_ready, 1)
                act.wait_ge(unit_done, tiles * (p + 1))
                if not first:
                    act.wait_ge(ring_filled, before(p, G, 1) + 1)
                for j in range(4):
                    nc.scalar.copy(sums[32 * j:32 * j + HD + 1, :], k.ps[32 * j:32 * j + HD + 1, 4, :]).then_inc(sums_taken, 1)

            phases(act, phase)

        @block.vector
        def _(dve):
            def ring_item(o, item, pp, par, base, j):
                bank = ring(j)
                dve.wait_ge(ring_filled, base + j + 1)
                turned = k.ps[:, bank, :].bitcast(BF16)
                if item[0] == "keys":
                    ts = kgroups[item[1]]
                    last = nc.vector.tensor_copy(kturned[:, par, ts[0] * P:(ts[-1] + 1) * P], turned[:, 0:len(ts) * P])
                elif item[0] == "queries":
                    last = nc.vector.tensor_copy(qturned[:, par, :], turned)
                elif item[0] == "chunk":
                    _, a, t, c = item
                    lo, hi = chunks[c]
                    dst = maxima[:, a * NT + t, c:c + 1]
                    if mask8 is None:
                        last = nc.vector.tensor_reduce(dst, k.ps[:, bank, 0:hi - lo], AX.X, ALU.max)
                    else:
                        if j >= 4:
                            dve.wait_ge(ring_free, base + j - 3)
                        last = nc.vector.tensor_tensor_reduce(junk[:, j % 4, 0:hi - lo], k.ps[:, bank, 0:hi - lo],
                                                              mask8[:, t, lo:hi].bitcast(mybir.dt.uint8), 1.0, -3.0e38,
                                                              ALU.subtract, ALU.max, dst)
                else:
                    acc = k.ps[:, bank, :].rearrange("p (m a b r) -> p a b m r", m=4, a=2, b=2)
                    inv = inverse[:].rearrange("p (a b m) -> p a b m", a=2, b=2)
                    o.step(nc.vector.reciprocal(inv, acc[:, :, :, :, HD]))
                    for a in range(2):
                        last = nc.vector.tensor_tensor(out[:, :, bass.ds(16 * pp + 8 * a, 8)].rearrange("p (b m) d -> p b m d", b=2),
                                                       acc[:, a, :, :, 0:HD], bc(inv[:, a], [P, 2, 4, HD]), ALU.mult)
                        if a == 0:
                            o.step(last)
                last.then_inc(ring_free, 1)
                if item == prepare[-2]:
                    dve.wait_ge(ring_free, base + j + 1)
                    place_shift(o, par)

            def place_shift(o, par):
                o.step(nc.vector.tensor_reduce(shift[:], maxima[:], AX.X, ALU.max, negate=True))
                if mask8 is not None:
                    o.step(nc.vector.tensor_scalar(empty[:, 0], shift[:], BYTE8 / 2, None, ALU.is_gt))
                    o.step(nc.vector.tensor_scalar(empty[:, 1], empty[:, 0], -1.0, 1.0, ALU.mult, ALU.add))
                    o.step(nc.vector.tensor_tensor(shift[:], shift[:], empty[:, 1], ALU.mult))
                    o.step(nc.vector.scalar_tensor_tensor(out=shift[:], in0=empty[:, 0], scalar=-LOW8 * LOWER, in1=shift[:],
                                                          op0=ALU.mult, op1=ALU.add))
                parts = [qstack[:, par, :, :, SHIFT + i].rearrange("p t a -> p a t") for i in range(3)]
                whole = shift[:].rearrange("p (a t) -> p a t", a=2)
                rest = shift_left[:].rearrange("p (a t) -> p a t", a=2)
                o.step(nc.vector.tensor_copy(parts[0], whole))
                o.step(nc.vector.tensor_tensor(rest, whole, parts[0], ALU.subtract))
                o.step(nc.vector.tensor_copy(parts[1], rest))
                o.step(nc.vector.tensor_tensor(rest, rest, parts[1], ALU.subtract))
                nc.vector.tensor_copy(parts[2], rest).then_inc(shift_ready, 1)

            PREP = STEPS - 1
            o = InOrder(dve, dve_order)
            for j, item in enumerate(prepare):
                ring_item(o, item, 0, 0, 0, j)
            assert o.n == PREP, o.n

            def phase(p, par):
                base = before(p, G, 1)
                o = InOrder(dve, dve_order, before(p, PREP, 2))
                alone = isinstance(p, int)
                items = [] if alone and p == 0 else [(("sums",), p - 1, 1 - par)]
                if not (alone and p == PAIRS - 1):
                    items += [(item, p + 1, 1 - par) for item in prepare]
                for j, (item, pp, pr) in enumerate(items):
                    ring_item(o, item, pp, pr, base, j)

            phases(dve, phase, mask8 is not None)
            p = PAIRS - 1
            ring_item(InOrder(dve, dve_order, before(p, PREP, 2) + 2), ("sums",), p, 1, before(p, G, 1) + 1, 0)


def context_turned(k, s):
    nc = k.nc
    ctxT = s.sb("ctxT", [P, SP])
    full, rest = S // P, S % P
    groups = [range(a, min(a + 4, KT)) for a in range(0, KT, 4)]
    with Stage(nc) as g:
        rows = g.sb("rows", [P, KT, D])
        loaded = [g.sem(f"loaded{i}") for i in range(5)]
        zeroed = g.sem("zeroed")
        turned = g.sem("turned")
        kept = g.sem("kept")
        block = g.block()
        cuts = [0, 16, 32, full]

        @block.sync
        def _(sp):
            sp.wait_ge(zeroed, 1)
            sp.dma_start(rows[0:rest, full, :], k.dram["ctx_1024"][0, full * P:S]).then_inc(loaded[3], 16)
            for i in range(3):
                sp.dma_start(rows[:, cuts[i]:cuts[i + 1], :],
                             k.dram["ctx_1024"][0, cuts[i] * P:cuts[i + 1] * P].rearrange("(t p) d -> p t d", p=P)).then_inc(loaded[i], 16)

        @block.tensor
        def _(pe):
            for i, ts in enumerate(groups):
                for c in range(3):
                    if ts[0] == cuts[c]:
                        pe.wait_ge(loaded[c], 16)
                if ts[-1] == KT - 1:
                    pe.wait_ge(loaded[3], 16)
                if i >= NBANK:
                    pe.wait_ge(kept, i - NBANK + 1)
                for j, t in enumerate(ts):
                    last = nc.tensor.transpose(k.ps[:, i % NBANK, j * P:(j + 1) * P], rows[:, t, :], k.ident[:])
                last.then_inc(turned, 1)

        @block.vector
        def _(dve):
            nc.vector.memset(rows[:, full, :], 0.0).then_inc(zeroed, 1)
            for i, ts in enumerate(groups):
                dve.wait_ge(turned, i + 1)
                nc.vector.tensor_copy(ctxT[:, ts[0] * P:(ts[-1] + 1) * P], k.ps[:, i % NBANK, 0:len(ts) * P]).then_inc(kept, 1)
    return ctxT


def clear(k, aps):
    nc = k.nc
    with Stage(nc) as s:
        done = s.sem("done")
        block = s.block()

        @block.vector
        def _(dve):
            for ap in aps:
                nc.vector.memset(ap, 0).then_inc(done, 1)


def scale_by(k, ap, factor):
    nc = k.nc
    with Stage(nc) as s:
        done = s.sem("done")
        block = s.block()

        @block.vector
        def _(dve):
            nc.vector.tensor_scalar(ap, ap, factor, None, ALU.mult).then_inc(done, 1)


def masked_attention(k):
    nc, dr = k.nc, k.dram
    normalise(k)
    with Stage(nc) as s:
        q = k.h
        out = k.hT[:].rearrange("p (t d) -> p t d", t=NT)
        outT = k.h[:].rearrange("p t d -> p (t d)")
        bo = s.sb("bo", [P, D])
        ends = s.sb("ends", [P, KT])
        mask8 = s.sb("mask8", [P, NT, SP], FP8)
        project(k, k.hT, NT, k.wT["L1_xattn_Wq"][:], D, q)
        scale_by(k, q[:], HD ** -0.5 * STEP8)
        load(k, [(bo[:], row(k, "L1_xattn_bo", D)), (ends[:], dr["c_ends"])])
        with Stage(nc) as g:
            raw = g.sb("raw", [P, 2, S], I32)
            loaded = [g.sem(f"loaded{i}") for i in range(2)]
            kept = g.sem("kept")
            block = g.block()

            @block.sync
            def _(sp):
                for t in range(NT):
                    if t >= 2:
                        sp.wait_ge(kept, t)
                    sp.dma_start(raw[:, t % 2, :], dr["mask_BxSxS2_if1"][0, t * P:(t + 1) * P]).then_inc(loaded[t % 2], 16)

            @block.vector
            def _(dve):
                nc.vector.memset(mask8[:, :, S:SP], 0.0).then_inc(kept, 1)
                for t in range(NT):
                    dve.wait_ge(loaded[t % 2], 16 * (t // 2 + 1))
                    nc.vector.tensor_scalar(mask8[:, t, 0:S].bitcast(mybir.dt.uint8), raw[:, t % 2, :], 0.0, BYTE8,
                                            ALU.is_equal, ALU.mult).then_inc(kept, 1)
        keys = s.sb("keys", [P, KT, D])
        values = s.sb("values", [P, KT, D])
        with Stage(nc) as g:
            ctxT = context_turned(k, g)
            project(k, ctxT, KT, k.wT["L1_xattn_Wk"][:], D, keys)
            project(k, ctxT, KT, k.wT["L1_xattn_Wv"][:], D, values)
        attend(k, KT, q, keys, values, out, ends[:], mask8)
        turn(k, out, outT)
        project_add(k, outT, k.wT["L1_xattn_Wo"][:], bo[:])


def cross_attention(k):
    nc, dr = k.nc, k.dram
    normalise(k)
    with Stage(nc) as s:
        q = s.sb("q", [P, NT, D])
        out = s.sb("out", [P, NT, D])
        wq = s.sb("wq", [P, D])
        wkv = s.sb("wkv", [P, 2 * D])
        wo = s.sb("wo", [P, D])
        bias = s.sb("bias", [P, 4, D])
        ends = s.sb("ends", [P, KT])
        maskb = s.sb("maskb", [P, KT], mybir.dt.uint8)
        full, rest = S // P, S % P
        load(k, [(wq[:], dr["L2_xattn_q_w"]), (wkv[:], dr["L2_xattn_kv_w"]), (wo[:], dr["L2_xattn_proj_w"]),
                 (bias[:, 0, :], row(k, "L2_xattn_q_b", D)), (bias[:, 1, :], row(k, "L2_xattn_kv_b", D)),
                 (bias[:, 2, :], row(k, "L2_xattn_kv_b", D, D)), (bias[:, 3, :], row(k, "L2_xattn_proj_b", D)),
                 (ends[:], dr["c_ends"])])
        clear(k, [maskb[:, full:full + 1]])
        load(k, [(maskb[:, 0:full], dr["mask_BxS2_bk0"][0, 0:full * P].rearrange("(t p) -> p t", p=P)),
                 (maskb[0:rest, full:full + 1], dr["mask_BxS2_bk0"][0, full * P:S].rearrange("(p a) -> p a", a=1))])
        with Stage(nc) as g:
            done = g.sem("done")
            block = g.block()

            @block.vector
            def _(dve):
                nc.vector.scalar_tensor_tensor(out=ends[:], in0=maskb[:], scalar=MINUS_INF, in1=ends[:],
                                               op0=ALU.mult, op1=ALU.min).then_inc(done, 1)
        project(k, k.hT, NT, wq[:], D, q, bias[:, 0, :])
        scale_by(k, q[:], HD ** -0.5)
        keys = s.sb("keys", [P, KT, D])
        values = s.sb("values", [P, KT, D])
        with Stage(nc) as g:
            ctxT = context_turned(k, g)
            project(k, ctxT, KT, wkv[:, 0:D], D, keys, bias[:, 1, :])
            project(k, ctxT, KT, wkv[:, D:2 * D], D, values, bias[:, 2, :])
        attend(k, KT, q, keys, values, out, ends[:])
        turn(k, out, k.hT)
        project_add(k, k.hT, wo[:], bias[:, 3, :])


def quantise(k, src, dstT, scale):
    nc = k.nc
    with Stage(nc) as s:
        inv = s.sb("inv", [P, NT])
        whole = s.sb("whole", [P, NT, D])
        order = s.sem("order")
        rounded = s.sem("rounded")
        turned = s.sem("turned")
        kept = s.sem("kept")
        block = s.block()

        @block.vector
        def _(dve):
            o = InOrder(dve, order)
            o.step(nc.vector.tensor_reduce(scale[:], src[:], AX.X, ALU.max, apply_absolute_value=True))
            o.step(nc.vector.tensor_scalar(scale[:], scale[:], 1e-8, 1.0 / 127.0, ALU.max, ALU.mult))
            o.step(nc.vector.reciprocal(inv[:], scale[:]))
            o.step(nc.vector.tensor_tensor(whole[:], src[:], bc(inv[:], [P, NT, D]), ALU.mult))
            o.step(nc.vector.tensor_scalar(whole[:], whole[:], 127.0, -128.0, ALU.min, ALU.max))
            nc.vector.tensor_scalar(whole[:], whole[:], ROUND, -ROUND, ALU.add, ALU.add).then_inc(rounded, 1)
            for b in range(2):
                dve.wait_ge(turned, b + 1)
                nc.vector.tensor_copy(dstT[:, b * BANK:(b + 1) * BANK], k.ps[:, b, :]).then_inc(kept, 1)

        @block.tensor
        def _(pe):
            pe.wait_ge(rounded, 1)
            for b in range(2):
                for j in range(4):
                    last = nc.tensor.transpose(k.ps[:, b, j * P:(j + 1) * P], whole[:, 4 * b + j, :], k.ident[:])
                last.then_inc(turned, 1)


def ternary_attention(k):
    nc, dr = k.nc, k.dram
    KVH = 4
    KVD = KVH * HD
    N = D + 2 * KVD
    names = [("Wq", D), ("Wk", KVD), ("Wv", KVD), ("Wp", D)]
    normalise(k)
    with Stage(nc) as s:
        wT = s.sb("wT", [P, N + D], BF16)
        alpha = s.sb("alpha", [P, 4])
        scale = s.sb("scale", [P, NT])
        gain = s.sb("gain", [P, H])
        table = s.sb("table", [P, 2, NT, HD // 2])
        mask8 = s.sb("mask8", [P, NT, T], FP8)
        intT = s.sb("intT", [P, T], BF16)
        q = s.sb("q", [P, NT, D])
        keys = s.sb("keys", [P, NT, D])
        values = s.sb("values", [P, NT, D])
        out = s.sb("out", [P, NT, D])
        with Stage(nc) as g:
            rows = g.sb("rows", [P, 4, D])
            later = g.sb("later", [P, P])
            total = g.sb("total", [P, 4])
            inv = g.sb("inv", [P, 4])
            loaded = g.sem("loaded")
            order = g.sem("order")
            summed = g.sem("summed")
            spread = g.sem("spread")
            rounded = g.sem("rounded")
            turned = g.sem("turned")
            kept = g.sem("kept")
            block = g.block()

            @block.sync
            def _(sp):
                for i, (n, r) in enumerate(names):
                    sp.dma_start(rows[0:r, i, :], dr["L0_attn_" + n]).then_inc(loaded, 16)
                sp.dma_start(gain[:], row(k, "L0_attn_q_gain", H)).then_inc(loaded, 16)
                sp.dma_start(table[:], dr["c_rot8"]).then_inc(loaded, 16)
                sp.dma_start(later[:], dr["c_before"]).then_inc(loaded, 16)

            @block.vector
            def _(dve):
                o = InOrder(dve, order)
                o.step(nc.vector.memset(total[:], 0.0))
                dve.wait_ge(loaded, 16 * 7)
                bytes8 = mask8[:].bitcast(mybir.dt.uint8)
                for t in range(NT):
                    if t:
                        o.step(nc.vector.memset(bytes8[:, t, 0:t * P], 0))
                    o.step(nc.vector.tensor_scalar(bytes8[:, t, t * P:(t + 1) * P], later[:], BYTE8, None, ALU.mult))
                    if t < NT - 1:
                        o.step(nc.vector.memset(bytes8[:, t, (t + 1) * P:], int(BYTE8)))
                for i, (n, r) in enumerate(names):
                    last = nc.vector.tensor_reduce(total[0:r, i:i + 1], rows[0:r, i, :], AX.X, ALU.add, apply_absolute_value=True)
                    if i < 3:
                        o.step(last)
                last.then_inc(summed, 1)
                dve.wait_ge(spread, 1)
                for i, (n, r) in enumerate(names):
                    o.step(nc.vector.tensor_scalar(alpha[:, i:i + 1], k.ps[:, 0, i:i + 1], 1.0 / (r * D), 1e-8, ALU.mult, ALU.max))
                o.step(nc.vector.reciprocal(inv[:], alpha[:]))
                for i, (n, r) in enumerate(names):
                    w = rows[0:r, i, :]
                    o.step(nc.vector.tensor_scalar(w, w, inv[0:r, i:i + 1], 1.0, ALU.mult, ALU.min))
                    o.step(nc.vector.tensor_scalar(w, w, -1.0, ROUND, ALU.max, ALU.add))
                    last = nc.vector.tensor_scalar(w, w, -ROUND, None, ALU.add)
                    if i < 3:
                        o.step(last)
                last.then_inc(rounded, 1)
                dve.wait_ge(turned, 1)
                nc.vector.tensor_copy(wT[:], k.ps[:, 1, 0:N + D]).then_inc(kept, 1)

            @block.tensor
            def _(pe):
                pe.wait_ge(summed, 1)
                nc.tensor.matmul(k.ps[:, 0, 0:4], k.ones[:], total[:], start=True, stop=True).then_inc(spread, 1)
                pe.wait_ge(rounded, 1)
                at = 0
                for i, (n, r) in enumerate(names):
                    last = nc.tensor.transpose(k.ps[:, 1, at:at + r], rows[0:r, i, :], k.ident[0:r, 0:r])
                    at += r
                last.then_inc(turned, 1)
        quantise(k, k.h, intT, scale)
        with Stage(nc) as g:
            small = g.sb("small", [P, NT, 2 * KVD])
            square = g.sb("square", [P, NT, D + KVD])
            var = g.sb("var", [P, NT, H + KVH])
            turn1 = g.sb("turn1", [P, NT, D + KVD])
            t1 = g.sb("t1", [P, NT, H, HD // 2])
            t2 = g.sb("t2", [P, NT, H, HD // 2])
            order = g.sem("order")
            product = g.sem("product")
            var_ready = g.sem("var_ready")
            roots = g.sem("roots")
            block = g.block()

            @block.tensor
            def _(pe):
                for t in range(NT):
                    last = nc.tensor.matmul(k.ps[:, t // 2, (t % 2) * 256:(t % 2) * 256 + N], intT[:, t * P:(t + 1) * P],
                                            wT[:, 0:N], start=True, stop=True)
                last.then_inc(product, 1)

            @block.scalar
            def _(act):
                act.wait_ge(var_ready, 1)
                nc.scalar.activation(var[:], var[:], ACT.Sqrt).then_inc(roots, 1)

            @block.vector
            def _(dve):
                o = InOrder(dve, order)
                dve.wait_ge(product, 1)
                acc = k.ps[:, 0:4, :].rearrange("p b (j n) -> p (b j) n", j=2)
                o.step(nc.vector.tensor_tensor(q[:], acc[:, :, 0:D], bc(scale[:], [P, NT, D]), ALU.mult))
                o.step(nc.vector.tensor_tensor(small[:], acc[:, :, D:N], bc(scale[:], [P, NT, 2 * KVD]), ALU.mult))
                o.step(nc.vector.tensor_scalar(q[:], q[:], alpha[:, 0:1], None, ALU.mult))
                for i in range(2):
                    part = small[:, :, i * KVD:(i + 1) * KVD]
                    o.step(nc.vector.tensor_scalar(part, part, alpha[:, 1 + i:2 + i], None, ALU.mult))
                o.step(nc.vector.tensor_tensor(square[:, :, 0:D], q[:], q[:], ALU.mult))
                kk = small[:, :, 0:KVD]
                o.step(nc.vector.tensor_tensor(square[:, :, D:D + KVD], kk, kk, ALU.mult))
                o.step(nc.vector.tensor_reduce(var[:], square[:].rearrange("p t (h d) -> p t h d", d=HD), AX.X, ALU.add))
                nc.vector.tensor_scalar(var[:], var[:], 1.0 / HD, 1.1920929e-07, ALU.mult, ALU.add).then_inc(var_ready, 1)
                dve.wait_ge(roots, 1)
                o.step(nc.vector.reciprocal(var[:], var[:]))
                o.step(nc.vector.tensor_tensor(var[:, :, 0:H], var[:, :, 0:H], mid(gain[:], NT), ALU.mult))
                o.step(nc.vector.tensor_scalar(var[:, :, 0:H], var[:, :, 0:H], HD ** -0.5 * STEP8, None, ALU.mult))
                for src, heads, at, fac in ((q[:], H, 0, var[:, :, 0:H]), (kk, KVH, D, var[:, :, H:H + KVH])):
                    src4 = src.rearrange("p t (h d) -> p t h d", d=HD)
                    dst4 = turn1[:, :, at:at + heads * HD].rearrange("p t (h d) -> p t h d", d=HD)
                    half = HD // 2
                    cos, sin = (table[:, a].unsqueeze(2).to_broadcast([P, NT, heads, half]) for a in range(2))
                    x1, x2 = src4[:, :, :, 0:half], src4[:, :, :, half:HD]
                    u1, u2 = t1[:, :, 0:heads], t2[:, :, 0:heads]
                    o.step(nc.vector.tensor_tensor(u1, x1, cos, ALU.mult))
                    o.step(nc.vector.tensor_tensor(u2, x2, sin, ALU.mult))
                    o.step(nc.vector.tensor_tensor(dst4[:, :, :, 0:half], u1, u2, ALU.add))
                    o.step(nc.vector.tensor_tensor(u1, x1, sin, ALU.mult))
                    o.step(nc.vector.tensor_tensor(u2, x2, cos, ALU.mult))
                    o.step(nc.vector.tensor_tensor(dst4[:, :, :, half:HD], u2, u1, ALU.subtract))
                    o.step(nc.vector.tensor_tensor(dst4, dst4, fac.unsqueeze(3).to_broadcast([P, NT, heads, HD]), ALU.mult))
                o.step(nc.vector.tensor_copy(q[:], turn1[:, :, 0:D]))
                rep = H // KVH
                for h in range(KVH):
                    for dst, src in ((keys, turn1[:, :, D + h * HD:D + (h + 1) * HD]),
                                     (values, small[:, :, KVD + h * HD:KVD + (h + 1) * HD])):
                        o.step(nc.vector.tensor_copy(dst[:, :, h * rep * HD:(h + 1) * rep * HD].rearrange("p t (r d) -> p t r d", d=HD),
                                                     src.unsqueeze(2).to_broadcast([P, NT, rep, HD])))
        attend(k, NT, q, keys, values, out, None, mask8)
        quantise(k, out, intT, scale)
        with Stage(nc) as g:
            order = g.sem("order")
            product = g.sem("product")
            block = g.block()

            @block.tensor
            def _(pe):
                for t in range(NT):
                    last = nc.tensor.matmul(k.ps[:, t // 4, (t % 4) * P:(t % 4 + 1) * P], intT[:, t * P:(t + 1) * P],
                                            wT[:, N:N + D], start=True, stop=True)
                last.then_inc(product, 1)

            @block.vector
            def _(dve):
                o = InOrder(dve, order)
                dve.wait_ge(product, 1)
                acc = k.ps[:, 0:2, :].rearrange("p b (j n) -> p (b j) n", j=4)
                o.step(nc.vector.tensor_tensor(out[:], acc, bc(scale[:], [P, NT, D]), ALU.mult))
                o.step(nc.vector.tensor_scalar(out[:], out[:], alpha[:, 3:4], None, ALU.mult))
                o.step(nc.vector.tensor_tensor(k.x[:], k.x[:], out[:], ALU.add))


def context_kernels(k, kern):
    nc, dr = k.nc, k.dram
    C, F = 2 * D, 64
    n = "L0_xattn_"
    with Stage(nc) as s:
        hist_w = s.sb("hist_w", [P, C])
        rows = s.sb("rows", [P, 3, C])
        w1 = s.sb("w1", [P, 2, F])
        b1 = s.sb("b1", [F, 1])
        w2 = s.sb("w2", [F, 1])
        b2 = s.sb("b2", [P, 1])
        kw1 = s.sb("kw1", [P, 2, D])
        kw2 = s.sb("kw2", [P, 9 * H])
        kb = s.sb("kb", [1, 3, D])
        kb2 = s.sb("kb2", [1, 9 * H])
        ends = s.sb("ends", [P, KT])
        load(k, [(hist_w[:], dr[n + "hist_W"]), (rows[:, 0, :], row(k, n + "hist_b", C)),
                 (rows[:, 1, :], row(k, n + "hist_ln_g", C)), (rows[:, 2, :], row(k, n + "hist_ln_b", C)),
                 (w1[:], dr[n + "ctx_W1"].rearrange("(c p) f -> p c f", p=P)),
                 (b1[:], dr[n + "ctx_b1"].rearrange("(p a) -> p a", a=1)), (w2[:], dr[n + "ctx_W2"]),
                 (b2[:], row(k, n + "ctx_b2", 1)), (kw1[:], dr[n + "kg_W1"].rearrange("(c p) f -> p c f", p=P)),
                 (kw2[:], dr[n + "kg_W2"])] +
                [(kb[:, i, :], dr[n + m].rearrange("(a d) -> a d", a=1)) for i, m in enumerate(("kg_b1", "kg_ln_g", "kg_ln_b"))] +
                [(kb2[:], dr[n + "kg_b2"].rearrange("(a d) -> a d", a=1)), (ends[:], dr["c_ends"])])
        eh = s.sb("eh", [P, KT, C])
        with Stage(nc) as g:
            ctxT = context_turned(k, g)
            project(k, ctxT, KT, hist_w[:], C, eh, rows[:, 0, :])
        with Stage(nc) as g:
            square = g.sb("square", [P, KT, C])
            red = g.sb("red", [P, KT])
            var = g.sb("var", [P, KT])
            order = g.sem("order")
            var_ready = g.sem("var_ready")
            roots = g.sem("roots")
            centred = g.sem("centred")
            squared = g.sem("squared")
            block = g.block()
            full = [P, KT, C]

            @block.vector
            def _(dve):
                o = InOrder(dve, order)
                o.step(nc.vector.tensor_reduce(red[:], eh[:], AX.X, ALU.add))
                o.step(nc.vector.tensor_scalar(red[:], red[:], 1.0 / C, None, ALU.mult))
                nc.vector.tensor_tensor(eh[:], eh[:], bc(red[:], full), ALU.subtract).then_inc(centred, 1)
                dve.wait_ge(squared, 1)
                o.step(nc.vector.tensor_reduce(red[:], square[:], AX.X, ALU.add))
                nc.vector.tensor_scalar(var[:], red[:], 1.0 / C, 1e-5, ALU.mult, ALU.add).then_inc(var_ready, 1)
                dve.wait_ge(roots, 1)
                o.step(nc.vector.reciprocal(red[:], var[:]))
                o.step(nc.vector.tensor_tensor(eh[:], eh[:], bc(red[:], full), ALU.mult))
                o.step(nc.vector.tensor_tensor(eh[:], eh[:], mid(rows[:, 1, :], KT), ALU.mult))
                nc.vector.tensor_tensor(eh[:], eh[:], mid(rows[:, 2, :], KT), ALU.add).then_inc(centred, 1)

            @block.scalar
            def _(act):
                act.wait_ge(centred, 1)
                nc.scalar.activation(square[:], eh[:], ACT.Square).then_inc(squared, 1)
                act.wait_ge(var_ready, 1)
                nc.scalar.activation(var[:], var[:], ACT.Sqrt).then_inc(roots, 1)
                act.wait_ge(centred, 2)
                nc.scalar.activation(eh[:], eh[:], ACT.Gelu).then_inc(squared, 1)
        weight = s.sb("weight", [P, KT])
        with Stage(nc) as g:
            ehT = g.sb("ehT", [P, 2, SP])
            hid = g.sb("hid", [F, SP])
            turned = g.sem("turned")
            turned_kept = g.sem("turned_kept")
            up = g.sem("up")
            hid_ready = g.sem("hid_ready")
            down = g.sem("down")
            order = g.sem("order")
            chunks = [(a, min(a + BANK, SP)) for a in range(0, SP, BANK)]
            groups = [(c, range(a, min(a + 4, KT))) for c in range(2) for a in range(0, KT, 4)]
            block = g.block()

            @block.tensor
            def _(pe):
                for i, (c, ts) in enumerate(groups):
                    if i >= 4:
                        pe.wait_ge(turned_kept, i - 3)
                    for j, t in enumerate(ts):
                        last = nc.tensor.transpose(k.ps[:, i % 4, j * P:(j + 1) * P], eh[:, t, c * P:(c + 1) * P], k.ident[:])
                    last.then_inc(turned, 1)
                pe.wait_ge(turned_kept, len(groups))
                for i, (lo, hi) in enumerate(chunks):
                    if i >= 3:
                        pe.wait_ge(hid_ready, i - 2)
                    for c in range(2):
                        last = nc.tensor.matmul(k.ps[0:F, 4 + i % 3, 0:hi - lo], w1[:, c, :], ehT[:, c, lo:hi],
                                                start=(c == 0), stop=(c == 1))
                    last.then_inc(up, 1)
                pe.wait_ge(hid_ready, len(chunks))
                for t in range(KT):
                    last = nc.tensor.matmul(k.ps[:, 7, t:t + 1], hid[:, t * P:(t + 1) * P], w2[:], start=True, stop=True)
                last.then_inc(down, 1)

            @block.scalar
            def _(act):
                for i, (lo, hi) in enumerate(chunks):
                    act.wait_ge(up, i + 1)
                    nc.scalar.activation(hid[:, lo:hi], k.ps[0:F, 4 + i % 3, 0:hi - lo], ACT.Gelu, bias=b1[:, 0:1]).then_inc(hid_ready, 1)

            @block.vector
            def _(dve):
                for i, (c, ts) in enumerate(groups):
                    dve.wait_ge(turned, i + 1)
                    nc.vector.tensor_copy(ehT[:, c, ts[0] * P:(ts[-1] + 1) * P], k.ps[:, i % 4, 0:len(ts) * P]).then_inc(turned_kept, 1)
                o = InOrder(dve, order)
                dve.wait_ge(down, 1)
                o.step(nc.vector.tensor_scalar(weight[:], k.ps[:, 7, 0:KT], b2[:, 0:1], None, ALU.add))
                o.step(nc.vector.tensor_tensor(weight[:], weight[:], ends[:], ALU.add))
        with Stage(nc) as g:
            top = g.sb("top", [P, 4])
            lane = g.sb("lane", [1, 2])
            acc = g.sb("acc", [P, 1])
            cc = g.sb("cc", [1, C])
            ccT = g.sb("ccT", [P, 2])
            z = g.sb("z", [1, D])
            zz = g.sb("zz", [1, D])
            st = g.sb("st", [1, 8])
            zT = g.sb("zT", [P, 1])
            ker = g.sb("ker", [1, 9 * H])
            red = g.sb("red", [1, H])
            order = g.sem("order")
            to_pe = g.sem("to_pe")
            from_pe = g.sem("from_pe")
            to_act = g.sem("to_act")
            from_act = g.sem("from_act")
            block = g.block()

            @block.vector
            def _(dve):
                o = InOrder(dve, order)
                nc.vector.tensor_reduce(top[:, 0:1], weight[:], AX.X, ALU.max).then_inc(to_pe, 1)
                dve.wait_ge(from_pe, 1)
                nc.vector.tensor_reduce(lane[:, 0:1], k.ps[0:1, 0, 0:P], AX.X, ALU.max, negate=True).then_inc(to_pe, 1)
                dve.wait_ge(from_pe, 2)
                nc.vector.tensor_copy(top[:, 1:2], k.ps[:, 1, 0:1]).then_inc(to_act, 1)
                dve.wait_ge(from_pe, 3)
                o.step(nc.vector.reciprocal(lane[:, 1:2], k.ps[0:1, 2, C:C + 1]))
                nc.vector.tensor_scalar(cc[:], k.ps[0:1, 2, 0:C], lane[:, 1:2], None, ALU.mult).then_inc(to_pe, 1)
                dve.wait_ge(from_pe, 4)
                nc.vector.tensor_copy(ccT[:], k.ps[:, 3, 0:2]).then_inc(to_pe, 1)
                dve.wait_ge(from_pe, 5)
                o.step(nc.vector.tensor_tensor(z[:], k.ps[0:1, 4, 0:D], kb[:, 0, :], ALU.add))
                o.step(nc.vector.tensor_reduce(st[:, 0:1], z[:], AX.X, ALU.add))
                o.step(nc.vector.tensor_scalar(st[:, 1:2], st[:, 0:1], 1.0 / D, None, ALU.mult))
                o.step(nc.vector.tensor_scalar(z[:], z[:], st[:, 1:2], None, ALU.subtract))
                o.step(nc.vector.tensor_tensor(zz[:], z[:], z[:], ALU.mult))
                o.step(nc.vector.tensor_reduce(st[:, 2:3], zz[:], AX.X, ALU.add))
                nc.vector.tensor_scalar(st[:, 3:4], st[:, 2:3], 1.0 / D, 1e-5, ALU.mult, ALU.add).then_inc(to_act, 1)
                dve.wait_ge(from_act, 2)
                o.step(nc.vector.reciprocal(st[:, 5:6], st[:, 4:5]))
                o.step(nc.vector.tensor_scalar(z[:], z[:], st[:, 5:6], None, ALU.mult))
                o.step(nc.vector.tensor_tensor(z[:], z[:], kb[:, 1, :], ALU.mult))
                nc.vector.tensor_tensor(z[:], z[:], kb[:, 2, :], ALU.add).then_inc(to_act, 1)
                dve.wait_ge(from_pe, 6)
                nc.vector.tensor_copy(zT[:], k.ps[:, 5, 0:1]).then_inc(to_pe, 1)
                dve.wait_ge(from_pe, 7)
                o.step(nc.vector.tensor_tensor(ker[:], k.ps[0:1, 6, 0:9 * H], kb2[:], ALU.add))
                by_head = ker[:].rearrange("p (h j) -> p h j", h=H)
                o.step(nc.vector.tensor_reduce(red[:], by_head, AX.X, ALU.max))
                nc.vector.tensor_tensor(by_head, by_head, bc(red[:], [1, H, 9]), ALU.subtract).then_inc(to_act, 1)
                dve.wait_ge(from_act, 4)
                o.step(nc.vector.tensor_reduce(red[:], by_head, AX.X, ALU.add))
                o.step(nc.vector.reciprocal(red[:], red[:]))
                nc.vector.tensor_tensor(by_head, by_head, bc(red[:], [1, H, 9]), ALU.mult).then_inc(to_pe, 1)
                dve.wait_ge(from_pe, 8)
                nc.vector.tensor_copy(kern[:], k.ps[:, 7, 0:9 * H]).then_inc(to_act, 1)

            @block.scalar
            def _(act):
                act.wait_ge(to_act, 1)
                nc.scalar.activation(weight[:], weight[:], ACT.Exp, bias=top[:, 1:2], accum_out=top[:, 2:3]).then_inc(from_act, 1)
                act.wait_ge(to_act, 2)
                nc.scalar.activation(st[:, 4:5], st[:, 3:4], ACT.Sqrt).then_inc(from_act, 1)
                act.wait_ge(to_act, 3)
                nc.scalar.activation(z[:], z[:], ACT.Gelu).then_inc(from_act, 1)
                act.wait_ge(to_act, 4)
                nc.scalar.activation(ker[:], ker[:], ACT.Exp).then_inc(from_act, 1)

            @block.tensor
            def _(pe):
                pe.wait_ge(to_pe, 1)
                nc.tensor.transpose(k.ps[0:1, 0, 0:P], top[:, 0:1], k.ident[:]).then_inc(from_pe, 1)
                pe.wait_ge(to_pe, 2)
                nc.tensor.matmul(k.ps[:, 1, 0:1], k.ones[0:1, :], lane[:, 0:1], start=True, stop=True).then_inc(from_pe, 1)
                pe.wait_ge(from_act, 1)
                for t in range(KT):
                    nc.tensor.matmul(k.ps[0:1, 2, 0:C], weight[:, t:t + 1], eh[:, t, :], start=(t == 0), stop=(t == KT - 1))
                nc.tensor.matmul(k.ps[0:1, 2, C:C + 1], top[:, 2:3], k.ones[:, 0:1], start=True, stop=True).then_inc(from_pe, 1)
                pe.wait_ge(to_pe, 3)
                for c in range(2):
                    last = nc.tensor.transpose(k.ps[:, 3, c:c + 1], cc[:, c * P:(c + 1) * P], k.ident[0:1, 0:1])
                last.then_inc(from_pe, 1)
                pe.wait_ge(to_pe, 4)
                for c in range(2):
                    last = nc.tensor.matmul(k.ps[0:1, 4, 0:D], ccT[:, c:c + 1], kw1[:, c, :], start=(c == 0), stop=(c == 1))
                last.then_inc(from_pe, 1)
                pe.wait_ge(from_act, 3)
                nc.tensor.transpose(k.ps[:, 5, 0:1], z[:], k.ident[0:1, 0:1]).then_inc(from_pe, 1)
                pe.wait_ge(to_pe, 5)
                nc.tensor.matmul(k.ps[0:1, 6, 0:9 * H], zT[:], kw2[:], start=True, stop=True).then_inc(from_pe, 1)
                pe.wait_ge(to_pe, 6)
                nc.tensor.matmul(k.ps[:, 7, 0:9 * H], k.ones[0:1, :], ker[:], start=True, stop=True).then_inc(from_pe, 1)


def convolved_attention(k):
    nc, dr = k.nc, k.dram
    WIN = P - 2
    NW = (T + WIN - 1) // WIN
    last_out = T - (NW - 1) * WIN
    n = "L0_xattn_"
    normalise(k)
    with Stage(nc) as s:
        kern = s.sb("kern", [P, 9 * H])
        context_kernels(k, kern)
        w = s.sb("w", [P, 4, D])
        proj_b = s.sb("proj_b", [P, D])
        shifts = s.sb("shifts", [P, 3, WIN])
        head8 = s.sb("head8", [P, H])
        keep8 = s.sb("keep8", [P, NW, T], mybir.dt.uint8)
        lose8 = s.sb("lose8", [WIN, NW, T], mybir.dt.uint8)
        keep = s.sb("keep", [P, NW, T], BF16)
        lose = s.sb("lose", [WIN, NW, T], BF16)
        load(k, [(w[:, i, :], dr[n + m]) for i, m in enumerate(("Wq", "Wk", "Wv", "proj_W"))] +
                [(proj_b[:], row(k, n + "proj_b", D)), (shifts[:], dr["c_shifts"]), (head8[:], dr["c_head8"])])
        clear(k, [keep8[:, 0, :], keep8[:, NW - 1, :], lose8[:, NW - 1, :]])
        mask = dr["mask_SxS_bc0"]
        inner = mask[WIN - 1:WIN - 1 + (NW - 2) * WIN]
        loads = [(keep8[1:P, 0, :], mask[0:P - 1]), (keep8[0:last_out + 1, NW - 1, :], mask[T - last_out - 1:T]),
                 (lose8[0:last_out, NW - 1, :], mask[T - last_out:T]),
                 (lose8[:, 0:NW - 1, :], mask[0:(NW - 1) * WIN].rearrange("(w p) n -> p w n", p=WIN))]
        loads += [(keep8[:, i, :], mask[i * WIN - 1:i * WIN - 1 + P]) for i in range(1, NW - 1)]
        load(k, loads)
        qz = s.sb("qz", [P, NW * WIN + 2])
        kT = s.sb("kT", [P, T])
        v = s.sb("v", [P, NT, D])
        out = s.sb("out", [WIN, NW, D])
        project(k, k.hT, NT, w[:, 2, :], D, v)
        with Stage(nc) as g:
            product = g.sem("product")
            kept = g.sem("kept")
            block = g.block()

            @block.tensor
            def _(pe):
                for i in range(2):
                    for b in range(2):
                        last = nc.tensor.matmul(k.ps[:, 2 * i + b, :], w[:, i, :], k.hT[:, b * BANK:(b + 1) * BANK],
                                                start=True, stop=True)
                    last.then_inc(product, 1)

            @block.vector
            def _(dve):
                nc.vector.memset(qz[:, 0:1], 0.0).then_inc(kept, 1)
                nc.vector.memset(qz[:, T + 1:NW * WIN + 2], 0.0).then_inc(kept, 1)
                dve.wait_ge(product, 1)
                nc.vector.tensor_scalar(qz[:, 1:T + 1], k.ps[:, 0:2, :].rearrange("p a b -> p (a b)"), HD ** -0.5, None,
                                        ALU.mult).then_inc(kept, 1)
                dve.wait_ge(product, 2)
                nc.vector.tensor_copy(kT[:], k.ps[:, 2:4, :].rearrange("p a b -> p (a b)")).then_inc(kept, 1)
                nc.vector.tensor_scalar(keep[:], keep8[:], -1.0, 1.0, ALU.mult, ALU.add).then_inc(kept, 1)
                nc.vector.tensor_scalar(lose[:], lose8[:], MINUS_INF, None, ALU.mult).then_inc(kept, 1)
        planes(k, qz, kT, v, kern, shifts, head8, keep, lose, out, WIN, NW)
        outT = s.sb("outT", [P, T])
        with Stage(nc) as g:
            turned = g.sem("turned")
            kept = g.sem("kept")
            block = g.block()

            @block.tensor
            def _(pe):
                for i in range(NW):
                    no = WIN if i < NW - 1 else last_out
                    last = nc.tensor.transpose(k.ps[:, i // 4, (i % 4) * P:(i % 4) * P + no], out[0:no, i, :], k.ident[0:no, 0:no])
                last.then_inc(turned, 1)

            @block.vector
            def _(dve):
                dve.wait_ge(turned, 1)
                for i in range(NW):
                    no = WIN if i < NW - 1 else last_out
                    nc.vector.tensor_copy(outT[:, i * WIN:i * WIN + no], k.ps[:, i // 4, (i % 4) * P:(i % 4) * P + no]).then_inc(kept, 1)
        project_add(k, outT, w[:, 3, :], proj_b[:])


def planes(k, qz, kT, v, kern, shifts, head8, keep, lose, out, WIN, NW):
    nc = k.nc
    with Stage(nc) as s:
        qh = s.sb("qh", [P, 2, NW * WIN + 2])
        bands = s.sb("bands", [P, 2, 3, WIN])
        plane = s.sb("plane", [P, 3, T + 2])
        power = s.sb("power", [WIN, 3, T])
        top = s.sb("top", [WIN, 3, 2])
        total = s.sb("total", [WIN, 3, 2])
        powerT = s.sb("powerT", [P, 3, NT, P])
        cleared = s.sem("cleared")
        order = s.sem("order")
        head_order = s.sem("head_order")
        head_ready = s.sem("head_ready")
        scores = s.sem("scores")
        masked = s.sem("masked")
        mixed = s.sem("mixed")
        mixed_kept = s.sem("mixed_kept")
        top_ready = s.sem("top_ready")
        powers = s.sem("powers")
        turned = s.sem("turned")
        turned_kept = s.sem("turned_kept")
        sums = s.sem("sums")
        done = s.sem("done")
        block = s.block()

        def rows(w):
            return P, WIN

        def two(b):
            return k.ps[:, b:b + 2, :].rearrange("p a b -> p (a b)")

        def heads(eng, head, straight=False):
            if straight:
                for h in range(H):
                    head(h, h % 2)
                return
            head(0, 0)
            head(1, 1)
            with eng.Fori(1, H // 2 - 1) as i:
                head(2 * i, 0)
                head(2 * i + 1, 1)
            head(H - 2, 0)
            head(H - 1, 1)

        def back(h, w, n):
            return (w - n) % NW, -1 if w < n else 0, not (isinstance(h, int) and h == 0 and w < n)

        @block.tensor
        def _(pe):
            def score(h, par, w, u):
                nr, no = rows(w)
                if w == 0:
                    pe.wait_ge(head_ready, h + 1)
                if not (isinstance(u, int) and u == 0):
                    pe.wait_ge(masked, u)
                for b in range(2):
                    last = nc.tensor.matmul(k.ps[0:nr, b, :], qh[:, par, w * WIN:w * WIN + nr], kT[:, b * BANK:(b + 1) * BANK],
                                            start=True, stop=True)
                last.then_inc(scores, 1)

            def mix(par, w, u):
                nr, no = rows(w)
                pe.wait_ge(masked, u + 1)
                if not (isinstance(u, int) and u == 0):
                    pe.wait_ge(mixed_kept, u)
                for b in range(2):
                    for c in range(3):
                        last = nc.tensor.matmul(k.ps[0:no, 2 + b, :], bands[0:nr, par, c, 0:no],
                                                plane[0:nr, w % 3, b * BANK + c:b * BANK + c + BANK],
                                                start=(c == 0), stop=(c == 2))
                last.then_inc(mixed, 1)

            def turn_powers(w, u):
                nr, no = rows(w)
                pe.wait_ge(powers, u + 1)
                if not (isinstance(u, int) and u == 0):
                    pe.wait_ge(turned_kept, u)
                for t in range(NT):
                    last = nc.tensor.transpose(k.ps[:, 4 + t // 4, (t % 4) * P:(t % 4) * P + no],
                                               power[0:no, w % 3, t * P:(t + 1) * P], k.ident[0:no, 0:no])
                last.then_inc(turned, 1)

            def weigh(h, w, u):
                nr, no = rows(w)
                pe.wait_ge(turned_kept, u + 1)
                if not (isinstance(u, int) and u == 0):
                    pe.wait_ge(done, u)
                for t in range(NT):
                    last = nc.tensor.matmul(k.ps[0:no, 6, 0:HD], powerT[:, w % 3, t, 0:no], v[:, t, bass.ds(h * HD, HD)],
                                            start=(t == 0), stop=(t == NT - 1))
                last.then_inc(sums, 1)

            score(0, 0, 0, 0)

            def head(h, par):
                for w in range(NW):
                    u = h * NW + w
                    if w < NW - 1:
                        score(h, par, w + 1, u + 1)
                    elif not (isinstance(h, int) and h == H - 1):
                        score(h + 1, 1 - par, 0, u + 1)
                    mix(par, w, u)
                    pw, dh, there = back(h, w, 1)
                    if there:
                        turn_powers(pw, u - 1)
                    pw, dh, there = back(h, w, 2)
                    if there:
                        weigh(h + dh, pw, u - 2)

            heads(pe, head)
            U = H * NW
            turn_powers(NW - 1, U - 1)
            weigh(H - 1, NW - 2, U - 2)
            weigh(H - 1, NW - 1, U - 1)

        @block.scalar
        def _(act):
            def head(h, par):
                for w in range(NW):
                    u = h * NW + w
                    nr, no = rows(w)
                    act.wait_ge(top_ready, u + 1)
                    nc.scalar.activation(power[0:no, w % 3, :], power[0:no, w % 3, :], ACT.Exp, bias=top[0:no, w % 3, 1:2],
                                         accum_out=total[0:no, w % 3, 0:1]).then_inc(powers, 1)

            heads(act, head)

        @block.vector
        def _(dve):
            def prepare(h, par):
                o = InOrder(dve, head_order, h * 9)
                o.step(nc.vector.tensor_scalar(qh[:, par, :], qz[:], head8[:, bass.ds(h, 1)], None, ALU.mult))
                for a in range(3):
                    for c in range(3):
                        weight = kern[:, bass.ds(9 * h + 3 * a + c, 1)]
                        if a == 0:
                            ins = nc.vector.tensor_scalar(bands[:, par, c, :], shifts[:, a, :], weight, None, ALU.mult)
                        else:
                            ins = nc.vector.scalar_tensor_tensor(out=bands[:, par, c, :], in0=shifts[:, a, :], scalar=weight,
                                                                 in1=bands[:, par, c, :], op0=ALU.mult, op1=ALU.add)
                        if (a, c) == (2, 2):
                            ins.then_inc(head_ready, 1)
                        else:
                            o.step(ins)

            def mask_out(w, u):
                nr, no = rows(w)
                dve.wait_ge(mixed, u + 1)
                if not (isinstance(u, int) and u < 3):
                    dve.wait_ge(turned, u - 2)
                nc.vector.tensor_tensor_reduce(power[0:no, w % 3, :], two(2)[0:no], lose[0:no, w, :], 1.0, -3.0e38,
                                               ALU.add, ALU.max, top[0:no, w % 3, 0:1]).then_inc(mixed_kept, 1)
                dve.wait_ge(mixed_kept, u + 1)
                nc.vector.tensor_scalar(top[0:no, w % 3, 1:2], top[0:no, w % 3, 0:1], -1.0, None, ALU.mult).then_inc(top_ready, 1)

            def keep_turned(w, u):
                nr, no = rows(w)
                dve.wait_ge(turned, u + 1)
                if not (isinstance(u, int) and u < 3):
                    dve.wait_ge(sums, u - 2)
                nc.vector.tensor_copy(powerT[:, w % 3, :, 0:no], two(4).rearrange("p (t n) -> p t n", n=P)[:, :, 0:no]).then_inc(turned_kept, 1)

            def finish(h, w, u):
                nr, no = rows(w)
                dve.wait_ge(sums, u + 1)
                nc.vector.reciprocal(total[0:no, w % 3, 1:2], total[0:no, w % 3, 0:1]).then_inc(order, 1)
                dve.wait_ge(order, u + 1)
                nc.vector.tensor_scalar(out[0:no, w, bass.ds(h * HD, HD)], k.ps[0:no, 6, 0:HD], total[0:no, w % 3, 1:2], None,
                                        ALU.mult).then_inc(done, 1)

            nc.vector.memset(plane[:, :, 0:1], 0.0).then_inc(cleared, 1)
            nc.vector.memset(plane[:, :, T + 1:T + 2], 0.0).then_inc(cleared, 1)
            dve.wait_ge(cleared, 2)
            prepare(0, 0)

            def head(h, par):
                for w in range(NW):
                    u = h * NW + w
                    nr, no = rows(w)
                    dve.wait_ge(scores, u + 1)
                    if not (isinstance(u, int) and u < 3):
                        dve.wait_ge(mixed, u - 2)
                    nc.vector.tensor_tensor(plane[0:nr, w % 3, 1:T + 1], two(0)[0:nr], keep[0:nr, w, :], ALU.mult).then_inc(masked, 1)
                    pw, dh, there = back(h, w, 1)
                    if there:
                        mask_out(pw, u - 1)
                    if w == 4 and not (isinstance(h, int) and h == H - 1):
                        prepare(h + 1, 1 - par)
                    pw, dh, there = back(h, w, 2)
                    if there:
                        keep_turned(pw, u - 2)
                    pw, dh, there = back(h, w, 3)
                    if there:
                        finish(h + dh, pw, u - 3)

            heads(dve, head, straight=True)
            U = H * NW
            mask_out(NW - 1, U - 1)
            for n in (2, 1):
                keep_turned(NW - n, U - n)
            for n in (3, 2, 1):
                finish(H - 1, NW - n, U - n)


def deformable_attention(k):
    nc, dr = k.nc, k.dram
    NK = 5
    HK = H * NK
    LINE = 4 * HD
    n = "L3_xattn_"
    normalise(k)
    table = k.table_dram
    with Stage(nc) as s:
        qp = s.sb("qp", [P, NT, D])
        index = s.sb("index", [P, NT, HK], U32)
        frac = s.sb("frac", [P, 2, NT, HK])
        bo = s.sb("bo", [P, D])
        load(k, [(bo[:], row(k, n + "bo", D))])
        with Stage(nc) as g:
            bias = g.sb("bias", [P, 2, D])
            wkv = g.sb("wkv", [P, 2 * D])
            zero = g.sb("zero", [1, H * LINE])
            lines = g.sb("lines", [P, 3, H, 2, 2, HD])
            ctxz = g.sb("ctxz", [P, SP + P])
            load(k, [(bias[:, 0, :], row(k, n + "bk", D)), (bias[:, 1, :], row(k, n + "bv", D))])
            with Stage(nc) as f:
                ctxT = context_turned(k, f)
                with Stage(nc) as e:
                    done = e.sem("done")
                    block = e.block()

                    @block.vector
                    def _(dve):
                        nc.vector.memset(ctxz[:, 0:2], 0.0).then_inc(done, 1)
                        nc.vector.memset(ctxz[:, S + 2:SP + P], 0.0).then_inc(done, 1)
                        nc.vector.memset(zero[:], 0.0).then_inc(done, 1)
                        nc.vector.tensor_copy(wkv[:, 0:D], k.wT[n + "Wk"][:]).then_inc(done, 1)
                        nc.vector.tensor_copy(wkv[:, D:2 * D], k.wT[n + "Wv"][:]).then_inc(done, 1)
                        nc.vector.tensor_copy(ctxz[:, 2:S + 2], ctxT[:, 0:S]).then_inc(done, 1)
            with Stage(nc) as f:
                product = f.sem("product")
                line_ready = f.sem("line_ready")
                stored = [f.sem(f"stored{i}") for i in range(3)]
                block = f.block()

                @block.tensor
                def _(pe):
                    for t in range(KT):
                        if t >= 4:
                            pe.wait_ge(line_ready, 2 * (t - 3))
                        for nb in range(2):
                            last = nc.tensor.matmul(k.ps[:, 2 * (t % 4) + nb, 0:2 * D], ctxz[:, t * P + nb:t * P + nb + P], wkv[:],
                                                    start=True, stop=True)
                        last.then_inc(product, 1)

                @block.vector
                def _(dve):
                    both = bias[:].rearrange("p c (h d) -> p h c d", h=H)
                    for t in range(KT):
                        dve.wait_ge(product, t + 1)
                        if t >= 3:
                            dve.wait_ge(stored[t % 3], 16 * (t // 3))
                        for nb in range(2):
                            src = k.ps[:, 2 * (t % 4) + nb, 0:2 * D].rearrange("p (c h d) -> p h c d", c=2, h=H)
                            nc.vector.tensor_tensor(lines[:, t % 3, :, nb], src, both, ALU.add).then_inc(line_ready, 1)

                @block.sync
                def _(sp):
                    for t in range(KT):
                        sp.wait_ge(line_ready, 2 * t + 2)
                        sp.dma_start(table[t * P:(t + 1) * P, :],
                                     lines[:, t % 3].rearrange("p h a c d -> p (h a c d)")).then_inc(stored[t % 3], 16)
                    for i in range(3):
                        sp.wait_ge(stored[i], 16 * ((KT - i + 2) // 3))
                    half = zero[:, 0:H * LINE // 2].rearrange("p (h r) -> p h r", h=H)
                    def part(r, a):
                        return table[r:r + 1, :].rearrange("p (h a r) -> p h a r", h=H, a=2)[:, :, a, :]
                    for dst, src in ((table[0:1, :], zero[:]), (table[S + 2:S + 3, :], zero[:]), (part(1, 0), half), (part(S + 1, 1), half)):
                        sp.dma_start(dst, src).then_inc(stored[0], 16)
                    sp.wait_ge(stored[0], 16 * ((KT + 2) // 3 + 4))
        with Stage(nc) as g:
            bq = g.sb("bq", [P, D])
            boff = g.sb("boff", [P, HK])
            where = g.sb("where", [P, NT, HK])
            head_row = g.sb("head_row", [P, HK])
            mask = g.sb("mask", [P, KT], I32)
            qpT = g.sb("qpT", [P, T])
            pos = g.sb("pos", [P, NT, HK])
            a = g.sb("a", [P, NT, HK])
            b = g.sb("b", [P, NT, HK])
            c = g.sb("c", [P, NT, HK])
            full, rest = S // P, S % P
            load(k, [(bq[:], row(k, n + "bq", D)), (boff[:], row(k, n + "boff", HK)), (where[:], dr["c_where"]),
                     (head_row[:], dr["c_head_row"]), (mask[:, full:full + 1], dr["c_one32"])])
            load(k, [(mask[:, 0:full], dr["mask_BxS2_if0"][0, 0:full * P].rearrange("(t p) -> p t", p=P)),
                     (mask[0:rest, full:full + 1], dr["mask_BxS2_if0"][0, full * P:S].rearrange("(p a) -> p a", a=1))])
            project(k, k.hT, NT, k.wT[n + "Wq"][:], D, qp, bq[:])
            turn(k, qp, qpT)
            project(k, qpT, NT, k.wT[n + "Woff"][:], HK, pos, boff[:])
            with Stage(nc) as f:
                free = f.sb("free", [P, KT])
                few = f.sb("few", [P, 4])
                order = f.sem("order")
                counted = f.sem("counted")
                spread = f.sem("spread")
                block = f.block()

                @block.tensor
                def _(pe):
                    pe.wait_ge(counted, 1)
                    nc.tensor.matmul(k.ps[:, 0, 0:1], k.ones[:], few[:, 0:1], start=True, stop=True).then_inc(spread, 1)

                @block.vector
                def _(dve):
                    o = InOrder(dve, order)
                    o.step(nc.vector.tensor_scalar(free[:], mask[:], -1.0, 1.0, ALU.mult, ALU.add))
                    nc.vector.tensor_reduce(few[:, 0:1], free[:], AX.X, ALU.add).then_inc(counted, 1)
                    dve.wait_ge(spread, 1)
                    o.step(nc.vector.tensor_scalar(few[:, 1:2], k.ps[:, 0, 0:1], -1.0, None, ALU.add))
                    o.step(nc.vector.reciprocal(few[:, 2:3], few[:, 1:2]))
                    o.step(nc.vector.tensor_scalar(few[:, 3:4], few[:, 1:2], -1.0, None, ALU.mult))
                    o.step(nc.vector.tensor_tensor(pos[:], pos[:], where[:], ALU.add))
                    o.step(nc.vector.tensor_scalar(a[:], pos[:], few[:, 2:3], None, ALU.mult))
                    floor(o, nc, b, a, c)
                    o.step(nc.vector.scalar_tensor_tensor(out=pos[:], in0=b[:], scalar=few[:, 3:4], in1=pos[:], op0=ALU.mult, op1=ALU.add))
                    o.step(nc.vector.tensor_scalar(a[:], pos[:], few[:, 1:2], 0.0, ALU.mult, ALU.is_lt))
                    o.step(nc.vector.scalar_tensor_tensor(out=pos[:], in0=a[:], scalar=few[:, 1:2], in1=pos[:], op0=ALU.mult, op1=ALU.add))
                    o.step(nc.vector.tensor_scalar(pos[:], pos[:], 1.0 / (S - 1), 2.0, ALU.mult, ALU.mult))
                    o.step(nc.vector.tensor_scalar(pos[:], pos[:], -1.0, 1.0, ALU.add, ALU.add))
                    o.step(nc.vector.tensor_scalar(pos[:], pos[:], float(S), -1.0, ALU.mult, ALU.add))
                    o.step(nc.vector.tensor_scalar(pos[:], pos[:], 0.5, None, ALU.mult))
                    floor(o, nc, b, pos, c)
                    o.step(nc.vector.tensor_tensor(frac[:, 1], pos[:], b[:], ALU.subtract))
                    o.step(nc.vector.tensor_scalar(frac[:, 0], frac[:, 1], -1.0, 1.0, ALU.mult, ALU.add))
                    o.step(nc.vector.tensor_scalar(b[:], b[:], -2.0, float(S), ALU.max, ALU.min))
                    o.step(nc.vector.tensor_scalar(b[:], b[:], 2.0, float(H), ALU.add, ALU.mult))
                    o.step(nc.vector.tensor_tensor(b[:], b[:], mid(head_row[:], NT), ALU.add))
                    o.step(nc.vector.tensor_copy(index[:], b[:]))
        sampled_attention(k, qp, index, frac, table, NK, LINE)
        turn(k, qp, k.hT)
        project_add(k, k.hT, k.wT[n + "Wo"][:], bo[:])


def sampled_attention(k, qp, index, frac, table, NK, LINE):
    nc = k.nc
    HK = H * NK
    lines_of = table.rearrange("r (h c) -> (r h) c", h=H)
    with Stage(nc) as s:
        line = s.sb("line", [P, 2, HK, LINE])
        near = s.sb("near", [P, HK, 2 * HD])
        far = s.sb("far", [P, HK, 2 * HD])
        prod = s.sb("prod", [P, HK, HD])
        score = s.sb("score", [P, HK])
        red = s.sb("red", [P, H])
        gathered = [s.sem(f"gathered{i}") for i in range(2)]
        order = s.sem("order")
        used = s.sem("used")
        shifted = s.sem("shifted")
        powers = s.sem("powers")
        done = s.sem("done")
        block = s.block()

        @block.gpsimd
        def _(pool):
            for t in range(NT):
                if t >= 2:
                    pool.wait_ge(used, t - 1)
                for j in range(HK):
                    nc.gpsimd.indirect_dma_start(line[:, t % 2, j, :], None, lines_of,
                                                 bass.IndirectOffsetOnAxis(ap=index[:, t, j:j + 1], axis=0)).then_inc(gathered[t % 2], 16)

        @block.scalar
        def _(act):
            for t in range(NT):
                act.wait_ge(shifted, t + 1)
                nc.scalar.activation(score[:], score[:], ACT.Exp).then_inc(powers, 1)

        @block.vector
        def _(dve):
            o = InOrder(dve, order)
            by_head = score[:].rearrange("p (h j) -> p h j", h=H)
            for t in range(NT):
                dve.wait_ge(gathered[t % 2], 16 * HK * (t // 2 + 1))
                full = [P, HK, 2 * HD]
                o.step(nc.vector.tensor_tensor(near[:], line[:, t % 2, :, 0:2 * HD], bc(frac[:, 0, t, :], full), ALU.mult))
                nc.vector.tensor_tensor(far[:], line[:, t % 2, :, 2 * HD:LINE], bc(frac[:, 1, t, :], full), ALU.mult).then_inc(used, 1)
                dve.wait_ge(used, t + 1)
                o.step(nc.vector.tensor_tensor(near[:], near[:], far[:], ALU.add))
                q = qp[:, t, :].rearrange("p (h d) -> p h d", h=H).unsqueeze(2).to_broadcast([P, H, NK, HD])
                o.step(nc.vector.tensor_tensor(prod[:].rearrange("p (h j) d -> p h j d", h=H),
                                               near[:, :, 0:HD].rearrange("p (h j) d -> p h j d", h=H), q, ALU.mult))
                o.step(nc.vector.tensor_reduce(score[:], prod[:], AX.X, ALU.add))
                o.step(nc.vector.tensor_scalar(score[:], score[:], 0.5 * HD ** -0.5, None, ALU.mult))
                o.step(nc.vector.tensor_reduce(red[:], by_head, AX.X, ALU.max))
                nc.vector.tensor_tensor(by_head, by_head, bc(red[:], [P, H, NK]), ALU.subtract).then_inc(shifted, 1)
                dve.wait_ge(powers, t + 1)
                o.step(nc.vector.tensor_reduce(red[:], by_head, AX.X, ALU.add))
                o.step(nc.vector.reciprocal(red[:], red[:]))
                o.step(nc.vector.tensor_scalar(red[:], red[:], 0.5, None, ALU.mult))
                o.step(nc.vector.tensor_tensor(by_head, by_head, bc(red[:], [P, H, NK]), ALU.mult))
                o.step(nc.vector.tensor_tensor(prod[:], near[:, :, HD:2 * HD], bc(score[:], [P, HK, HD]), ALU.mult))
                o.step(nc.vector.tensor_reduce(qp[:, t, :].rearrange("p (h d) -> p h d", h=H),
                                               prod[:].rearrange("p (h j) d -> p h d j", h=H), AX.X, ALU.add))


SUBLAYERS = ["L0_attn", "L0_xattn", "L0_ffn", "L1_attn", "L1_xattn", "L1_ffn",
             "L2_attn", "L2_xattn", "L2_ffn", "L3_attn", "L3_xattn", "L3_ffn"]


def build(nc, dram, out, need=SUBLAYERS):
    k = Core(nc, dram)
    Stage.names = {}
    with k.ctx:
        k.x = k.sb("x_sb", [P, NT, D])
        k.h = k.sb("h", [P, NT, D])
        k.hT = k.sb("hT", [P, T])
        k.ident = k.sb("ident", [P, P])
        k.ident16 = k.sb("ident16", [P, P], BF16)
        k.lower = k.sb("lower", [P, P], BF16)
        k.iota = k.sb("iota", [P, P])
        k.ones = k.sb("ones", [P, P])
        k.ps = k.ctx.enter_context(nc.psum_tensor("ps", [P, NBANK, BANK], F32))
        k.table_dram = nc.dram_tensor("table", (SP, H * 4 * HD), F32, kind="Internal").ap()
        setup(k, need)
        give_back(nc)
        for n in SUBLAYERS:
            if n in need:
                DO[n](k)
                give_back(nc)
        with Stage(nc) as s:
            stored = s.sem("stored")
            block = s.block()

            @block.sync
            def _(sp):
                sp.dma_start(out[0].rearrange("(t p) d -> p t d", p=P), k.x[:]).then_inc(stored, 16)
                sp.wait_ge(stored, 16)


DO = {"L0_attn": ternary_attention, "L0_xattn": convolved_attention, "L3_xattn": deformable_attention, "L1_xattn": masked_attention, "L2_xattn": cross_attention,
      "L0_ffn": choice_ffn, "L1_attn": time_mix, "L1_ffn": relu_ffn, "L2_attn": linear_attention,
      "L2_ffn": routed_ffn, "L3_attn": retention, "L3_ffn": hash_ffn}


def constants():
    import numpy as np
    f = np.float32
    c = {"c_ident": np.eye(P, dtype=f)}
    c["c_iota"] = np.tile(np.arange(P, dtype=f), (P, 1))
    i = np.arange(P)
    c["c_same32"] = (i[:, None] // 32 == i[None, :] // 32).astype(f)
    c["c_before"] = (i[:, None] < i[None, :]).astype(f)
    c["c_spread"] = (np.arange(32)[:, None, None] == 2 * np.arange(16)[None, :, None] + i[None, None, :] // 64).astype(f)
    pos = np.arange(T, dtype=f)

    def rotation(width):
        inv = (1.0 / f(10000.0) ** (np.arange(0, width, 2, dtype=f) / f(width))).astype(f)
        ang = pos[:, None] * inv[None, :]
        both = np.stack([np.cos(ang), np.sin(ang)]).astype(f)
        return np.ascontiguousarray(both.reshape(2, NT, P, width // 2).transpose(2, 0, 1, 3))

    c["c_rot16"] = rotation(16)
    c["c_rot8"] = rotation(HD)
    gammas = (1.0 - np.exp(np.linspace(np.log(1 / 32), np.log(1 / 64), 8)).astype(f)).astype(np.float64)
    diff = i[None, None, :] - i[:, None, None]
    c["c_within"] = np.where(diff >= 0, gammas[None, :, None] ** np.maximum(diff, 0), 0.0).astype(f)
    c["c_powers"] = np.stack([gammas[None, :] ** (i[:, None] + 1), gammas[None, :] ** (127 - i[:, None])], 1).astype(f)
    blocks = (i[:, None] // 16 == i[None, :] // 16).astype(f)
    c["c_blocks"] = np.concatenate([blocks, (gammas[i // 16] ** 128)[:, None].astype(f)], 1)
    c["c_head_of"] = (i[:, None] // 16 == np.arange(8)[None, :]).astype(f)
    c["c_head8"] = (i[:, None] // 8 == np.arange(16)[None, :]).astype(f)
    c["c_ends"] = np.where(np.arange(KT)[None, :] * P + i[:, None] < S, 0.0, MINUS_INF).astype(f)
    c["c_shifts"] = (i[:, None, None] == np.arange(P - 2)[None, None, :] + np.arange(3)[None, :, None]).astype(f)
    c["c_one32"] = np.ones((P, 1), np.int32)
    where = (np.arange(NT)[None, :, None] * P + i[:, None, None] + np.tile(np.arange(-3, 2), H)[None, None, :]).astype(f)
    c["c_where"] = where
    c["c_head_row"] = np.tile(np.repeat(np.arange(H), 5).astype(f), (P, 1))
    return c


def kernel(**inputs):
    import numpy as np
    import concourse.bacc as bacc
    from concourse.bass_utils import run_bass_kernel_spmd

    nc = bacc.Bacc("TRN2", target_bir_lowering=False, num_devices=1)
    arrays = {n: np.ascontiguousarray(a) for n, a in inputs.items()}
    arrays.update(constants())
    dram = {n: nc.dram_tensor("in_" + n, a.shape, mybir.dt.from_np(a.dtype), kind="ExternalInput").ap()
            for n, a in arrays.items()}
    out = nc.dram_tensor("out", (1, T, D), F32, kind="ExternalOutput").ap()
    build(nc, dram, out)
    r = run_bass_kernel_spmd(nc, [{"in_" + n: a for n, a in arrays.items()}], core_ids=[0])
    return r.results[0]["out"]
```

```python
from contextlib import ExitStack

import concourse.bass as bass
from concourse import mybir

P = 128
T = 1024
NT = T // P
D = 128
H = 16
HD = D // H
S = 6404
KT = (S + P - 1) // P
SP = KT * P
BANK = 512
NBANK = 8

ALU = mybir.AluOpType
ACT = mybir.ActivationFunctionType
AX = mybir.AxisListType
F32 = mybir.dt.float32
BF16 = mybir.dt.bfloat16
FP8 = mybir.dt.float8e5
I32 = mybir.dt.int32
U32 = mybir.dt.uint32
ROUND = 12582912.0
BIG = 2.0 ** 30
MINUS_INF = -1.0e30


class InOrder:

    def __init__(self, eng, sem, base=0):
        self.eng, self.sem, self.base, self.n = eng, sem, base, 0

    def step(self, ins):
        ins.then_inc(self.sem, 1)
        self.n += 1
        self.eng.wait_ge(self.sem, self.base + self.n)


class Stage:

    names = {}
    used = []

    def __init__(self, nc):
        self.nc, self.ctx = nc, ExitStack()

    def __enter__(self):
        self.ctx.__enter__()
        return self

    def __exit__(self, *e):
        return self.ctx.__exit__(*e)

    def sb(self, name, shape, dt=F32):
        return self.ctx.enter_context(self.nc.sbuf_tensor(self.unique(name), shape, dt))

    def sem(self, name):
        sem = self.nc.alloc_semaphore(self.unique(name))
        Stage.used.append(sem)
        return sem

    def unique(self, name):
        Stage.names[name] = Stage.names.get(name, 0) + 1
        return f"{name}_{Stage.names[name]}"

    def block(self):
        return self.ctx.enter_context(self.nc.Block())


def give_back(nc):
    nc.all_engine_barrier()
    nc.clear_and_free_semaphores(Stage.used)
    Stage.used = []
    nc.all_engine_barrier()


def bc(ap, shape):
    while ap.ndim < len(shape):
        ap = ap.unsqueeze(ap.ndim)
    return ap.to_broadcast(list(shape))


def mid(ap, n):
    return ap.unsqueeze(1).to_broadcast([ap.shape[0], n, ap.shape[1]])


class Core:

    def __init__(self, nc, dram):
        self.nc, self.dram = nc, dram
        self.ctx = ExitStack()

    def sb(self, name, shape, dt=F32):
        return self.ctx.enter_context(self.nc.sbuf_tensor(name, shape, dt))


SWAPPED = [("L1_attn_W_key", 128), ("L1_attn_W_value", 128), ("L1_attn_W_receptance", 128), ("L1_attn_W_output", 128),
           ("L1_xattn_Wq", 128), ("L1_xattn_Wk", 128), ("L1_xattn_Wv", 128), ("L1_xattn_Wo", 128),
           ("L2_attn_w_out", 128), ("L2_ffn_gate_w", 32), ("L2_ffn_sw1", 64), ("L2_ffn_sw3", 64),
           ("L3_xattn_Wk", 128), ("L3_xattn_Wv", 128), ("L3_xattn_Wq", 128), ("L3_xattn_Woff", 80),
           ("L3_xattn_Wo", 128)]


def setup(k, need):
    nc, dr = k.nc, k.dram
    sw = [(n, r) for n, r in SWAPPED if n.split("_")[0] + "_" + n.split("_")[1] in need]
    k.wT = {n: k.sb("wT_" + n, [P, r]) for n, r in sw}
    if "L2_ffn" in need:
        k.wT["L2_ffn_sw2"] = k.sb("wT_L2_ffn_sw2", [64, D])
    with Stage(nc) as s:
        w_rows = s.sb("w_rows", [P, len(sw) + 1, D])
        wb_rows = s.sb("wb_rows", [P, 4, D], BF16)
        loaded = s.sem("loaded")
        wb_wide = s.sem("wb_wide")
        zeroed = s.sem("zeroed")
        turned = s.sem("turned")
        kept = s.sem("kept")
        pieces = []
        wide = {"L2_ffn_gate_w": 0, "L2_ffn_sw1": 1, "L2_ffn_sw3": 2}
        for i, (n, r) in enumerate(sw):
            pieces.append((w_rows[0:r, i, :], k.wT[n][:, 0:r], r))
        n_bf = 0
        if "L2_ffn" in need:
            pieces.append((w_rows[:, len(sw), 0:64], k.wT["L2_ffn_sw2"][:, :], P))
            n_bf = 4
        block = s.block()

        @block.sync
        def _(sp):
            sp.dma_start(k.x[:], dr["x"][0].rearrange("(t p) d -> p t d", p=P)).then_inc(loaded, 16)
            sp.dma_start(k.ident[:], dr["c_ident"]).then_inc(loaded, 16)
            sp.dma_start(k.iota[:], dr["c_iota"]).then_inc(loaded, 16)
            for i, (n, r) in enumerate(sw):
                dst = wb_rows[0:r, wide[n], :] if n in wide else w_rows[0:r, i, :]
                sp.dma_start(dst, dr[n]).then_inc(loaded, 16)
            if n_bf:
                sp.dma_start(wb_rows[:, 3, 0:64], dr["L2_ffn_sw2"]).then_inc(loaded, 16)
            sp.wait_ge(loaded, 16 * (3 + len(sw) + (1 if n_bf else 0)))

        n_loads = 3 + len(sw) + (1 if n_bf else 0)

        @block.vector
        def _(dve):
            nc.vector.memset(k.ones[:], 1.0).then_inc(zeroed, 1)
            dve.wait_ge(loaded, 16 * n_loads)
            nc.vector.tensor_copy(k.ident16[:], k.ident[:]).then_inc(zeroed, 1)
            nc.vector.tensor_scalar(k.lower[:], k.ident[:], LOWER, None, ALU.mult).then_inc(zeroed, 1)
            if n_bf:
                for n, i in wide.items():
                    r = dict(sw)[n]
                    j = [m for m, _ in sw].index(n)
                    nc.vector.tensor_copy(w_rows[0:r, j, :], wb_rows[0:r, i, :]).then_inc(wb_wide, 1)
                nc.vector.tensor_copy(w_rows[:, len(sw), 0:64], wb_rows[:, 3, 0:64]).then_inc(wb_wide, 1)
            for i, (src, dst, r) in enumerate(pieces):
                dve.wait_ge(turned, i + 1)
                nc.vector.tensor_copy(dst, k.ps[0:src.shape[1], i % NBANK, 0:r]).then_inc(kept, 1)

        @block.tensor
        def _(pe):
            pe.wait_ge(loaded, 16 * n_loads)
            if n_bf:
                pe.wait_ge(wb_wide, n_bf)
            for i, (src, dst, r) in enumerate(pieces):
                if i >= NBANK:
                    pe.wait_ge(kept, i - NBANK + 1)
                nc.tensor.transpose(k.ps[0:src.shape[1], i % NBANK, 0:r], src, k.ident[0:r, 0:r]).then_inc(turned, 1)


def normalise(k, affine=None, eps=1e-5, src=None, loads=()):
    nc = k.nc
    x = src or k.x
    with Stage(nc) as s:
        total = s.sb("total", [P, NT])
        mean = s.sb("mean", [P, NT])
        square = s.sb("square", [P, NT, D])
        var = s.sb("var", [P, NT])
        dev = s.sb("dev", [P, NT])
        inv = s.sb("inv", [P, NT])
        order = s.sem("order")
        var_ready = s.sem("var_ready")
        dev_ready = s.sem("dev_ready")
        h_ready = s.sem("h_ready")
        turned = s.sem("turned")
        loaded = s.sem("loaded")
        block = s.block()

        @block.sync
        def _(sp):
            with nc.allow_non_contiguous_dma("a few small vectors lie by partition"):
                for dst, dram in loads:
                    sp.dma_start(dst, dram).then_inc(loaded, 16)
            if loads:
                sp.wait_ge(loaded, 16 * len(loads))

        @block.vector
        def _(dve):
            o = InOrder(dve, order)
            o.step(nc.vector.tensor_reduce(total[:], x[:], AX.X, ALU.add))
            o.step(nc.vector.tensor_scalar(mean[:], total[:], 1.0 / D, None, ALU.mult))
            o.step(nc.vector.tensor_tensor(k.h[:], x[:], bc(mean[:], [P, NT, D]), ALU.subtract))
            o.step(nc.vector.tensor_tensor(square[:], k.h[:], k.h[:], ALU.mult))
            o.step(nc.vector.tensor_reduce(total[:], square[:], AX.X, ALU.add))
            nc.vector.tensor_scalar(var[:], total[:], 1.0 / D, eps, ALU.mult, ALU.add).then_inc(var_ready, 1)
            dve.wait_ge(dev_ready, 1)
            o.step(nc.vector.reciprocal(inv[:], dev[:]))
            last = nc.vector.tensor_tensor(k.h[:], k.h[:], bc(inv[:], [P, NT, D]), ALU.mult)
            if affine:
                o.step(last)
                o.step(nc.vector.tensor_tensor(k.h[:], k.h[:], mid(affine[0], NT), ALU.mult))
                last = nc.vector.tensor_tensor(k.h[:], k.h[:], mid(affine[1], NT), ALU.add)
            last.then_inc(h_ready, 1)
            dve.wait_ge(turned, 1)
            nc.vector.tensor_copy(k.hT[:, 0:BANK], k.ps[:, 0, :]).then_inc(order, 1)

        @block.scalar
        def _(act):
            act.wait_ge(var_ready, 1)
            nc.scalar.activation(dev[:], var[:], ACT.Sqrt).then_inc(dev_ready, 1)
            act.wait_ge(turned, 2)
            nc.scalar.copy(k.hT[:, BANK:T], k.ps[:, 1, :]).then_inc(dev_ready, 1)

        @block.tensor
        def _(pe):
            pe.wait_ge(h_ready, 1)
            for b in range(2):
                for j in range(4):
                    last = nc.tensor.transpose(k.ps[:, b, j * P:(j + 1) * P], k.h[:, 4 * b + j, :], k.ident[:])
                last.then_inc(turned, 1)


def load(k, pairs):
    nc = k.nc
    with Stage(nc) as t:
        loaded = t.sem("loaded")
        block = t.block()

        @block.sync
        def _(sp):
            with nc.allow_non_contiguous_dma("a few small vectors lie by partition"):
                for dst, src in pairs:
                    sp.dma_start(dst, src).then_inc(loaded, 16)
            sp.wait_ge(loaded, 16 * len(pairs))


def row(k, name, n, at=0):
    return k.dram[name][at:at + n].partition_broadcast(P)


def project(k, srcT, tiles, w, n, dst, bias=None, act=None):
    nc = k.nc
    per = BANK // n
    groups = [range(a, min(a + per, tiles)) for a in range(0, tiles, per)]
    with Stage(nc) as s:
        product = s.sem("product")
        kept = s.sem("kept")
        block = s.block()

        @block.tensor
        def _(pe):
            for g, ts in enumerate(groups):
                if g >= NBANK:
                    pe.wait_ge(kept, g - NBANK + 1)
                for j, t in enumerate(ts):
                    last = nc.tensor.matmul(k.ps[:, g % NBANK, j * n:(j + 1) * n], srcT[:, t * P:(t + 1) * P], w,
                                            start=True, stop=True)
                last.then_inc(product, 1)

        @block.vector
        def _(dve):
            for g, ts in enumerate(groups):
                dve.wait_ge(product, g + 1)
                src = k.ps[:, g % NBANK, 0:len(ts) * n].rearrange("p (t n) -> p t n", n=n)
                out = dst[:, ts[0]:ts[0] + len(ts), :]
                if bias is None:
                    nc.vector.tensor_copy(out, src).then_inc(kept, 1)
                else:
                    nc.vector.tensor_tensor(out, src, mid(bias, len(ts)), ALU.add).then_inc(kept, 1)


def turn(k, src, dstT):
    nc = k.nc
    with Stage(nc) as s:
        turned = s.sem("turned")
        kept = s.sem("kept")
        block = s.block()

        @block.tensor
        def _(pe):
            for b in range(2):
                for j in range(4):
                    last = nc.tensor.transpose(k.ps[:, b, j * P:(j + 1) * P], src[:, 4 * b + j, :], k.ident[:])
                last.then_inc(turned, 1)

        @block.vector
        def _(dve):
            for b in range(2):
                dve.wait_ge(turned, b + 1)
                nc.vector.tensor_copy(dstT[:, b * BANK:(b + 1) * BANK], k.ps[:, b, :]).then_inc(kept, 1)


def project_add(k, srcT, w, bias=None):
    nc = k.nc
    with Stage(nc) as s:
        product = s.sem("product")
        order = s.sem("order")
        block = s.block()

        @block.tensor
        def _(pe):
            for b in range(2):
                for j in range(4):
                    t = 4 * b + j
                    last = nc.tensor.matmul(k.ps[:, b, j * P:(j + 1) * P], srcT[:, t * P:(t + 1) * P], w,
                                            start=True, stop=True)
                last.then_inc(product, 1)

        @block.vector
        def _(dve):
            o = InOrder(dve, order)
            for b in range(2):
                part = k.x[:, 4 * b:4 * b + 4, :]
                dve.wait_ge(product, b + 1)
                o.step(nc.vector.tensor_tensor(part, part, k.ps[:, b, :].rearrange("p (t d) -> p t d", d=D), ALU.add))
                if bias is not None:
                    o.step(nc.vector.tensor_tensor(part, part, mid(bias, 4), ALU.add))


def experts(k, E, F, w1, w2, func, gate=None, b1=None, b2=None):
    nc = k.nc
    FC = F // P
    with Stage(nc) as s:
        hid = s.sb("hid", [P, 2, FC, T])
        up = s.sem("up")
        hid_ready = s.sem("hid_ready")
        down = s.sem("down")
        added = s.sem("added")
        block = s.block()

        @block.tensor
        def _(pe):
            def up_product(e):
                for c in range(FC):
                    n = e * FC + c
                    if n >= 2:
                        pe.wait_ge(hid_ready, n - 1)
                    for b in range(2):
                        last = nc.tensor.matmul(k.ps[:, 2 * (n % 2) + b, :], w1(e)[:, c * P:(c + 1) * P],
                                                k.hT[:, b * BANK:(b + 1) * BANK], start=True, stop=True)
                    last.then_inc(up, 1)

            def down_product(e):
                pe.wait_ge(hid_ready, FC * (e + 1))
                if e >= 2:
                    pe.wait_ge(added, NT * (e - 1))
                for t in range(NT):
                    out = k.ps[:, 4 + 2 * (e % 2) + t // 4, (t % 4) * P:(t % 4 + 1) * P]
                    if b2 is not None:
                        nc.tensor.matmul(out, k.ones[0:1, :], b2(e), start=True, stop=False)
                    for c in range(FC):
                        last = nc.tensor.matmul(out, hid[:, e % 2, c, t * P:(t + 1) * P], w2(e, c),
                                                start=(c == 0 and b2 is None), stop=(c == FC - 1))
                    if t % 4 == 3:
                        last.then_inc(down, 1)

            for e in range(E):
                up_product(e)
                if e >= 1:
                    down_product(e - 1)
            down_product(E - 1)

        @block.scalar
        def _(act):
            for n in range(E * FC):
                e, c = divmod(n, FC)
                act.wait_ge(up, n + 1)
                if e >= 2:
                    act.wait_ge(down, 2 * (e - 1))
                bias = b1(e, c) if b1 is not None else 0.0
                nc.scalar.activation(hid[:, e % 2, c, :],
                                     k.ps[:, 2 * (n % 2):2 * (n % 2) + 2, :].rearrange("p a b -> p (a b)"),
                                     func, bias=bias).then_inc(hid_ready, 1)

        @block.vector
        def _(dve):
            for e in range(E):
                for t in range(NT):
                    out = k.ps[:, 4 + 2 * (e % 2) + t // 4, (t % 4) * P:(t % 4 + 1) * P]
                    dve.wait_ge(down, 2 * e + t // 4 + 1)
                    if e >= 1:
                        dve.wait_ge(added, NT * (e - 1) + t + 1)
                    if gate is None:
                        nc.vector.tensor_tensor(k.x[:, t, :], out, k.x[:, t, :], ALU.add).then_inc(added, 1)
                    else:
                        nc.vector.scalar_tensor_tensor(out=k.x[:, t, :], in0=out, scalar=gate[:, t, e:e + 1],
                                                       in1=k.x[:, t, :], op0=ALU.mult, op1=ALU.add).then_inc(added, 1)


def relu_ffn(k):
    dr = k.dram
    F = 512
    FC = F // P
    with Stage(k.nc) as s:
        w1 = s.sb("w1", [P, F])
        w2 = s.sb("w2", [P, FC, D])
        b1 = s.sb("b1", [P, FC])
        b2 = s.sb("b2", [1, D])
        normalise(k, loads=[(w1[:], dr["L1_ffn_W1"]),
                 (w2[:], dr["L1_ffn_W2"].rearrange("(c p) d -> p c d", p=P)),
                 (b1[:], dr["L1_ffn_b1"].rearrange("(c p) -> p c", p=P)),
                 (b2[:], dr["L1_ffn_b2"].rearrange("(a d) -> a d", a=1))])
        experts(k, 1, F, lambda e: w1[:], lambda e, c: w2[:, c, :], ACT.Relu,
                b1=lambda e, c: b1[:, c:c + 1], b2=lambda e: b2[:])


def hash_ffn(k):
    nc, dr = k.nc, k.dram
    E, F = 8, 512
    FC = F // P
    with Stage(nc) as s:
        gate = s.sb("gate", [P, NT, E])
        w1 = s.sb("w1", [P, E, F])
        w2 = s.sb("w2", [P, E, FC, D])
        b1 = s.sb("b1", [P, E, FC])
        b2 = s.sb("b2", [1, E, D])
        normalise(k, loads=[(w1[:], dr["L3_ffn_W1"].rearrange("e d f -> d e f")),
                 (w2[:], dr["L3_ffn_W2"].rearrange("e (c p) d -> p e c d", p=P)),
                 (b1[:], dr["L3_ffn_b1"].rearrange("e (c p) -> p e c", p=P)),
                 (b2[:], dr["L3_ffn_b2"].rearrange("(a e) d -> a e d", a=1))])
        with Stage(nc) as g:
            a = g.sb("a", [P, NT])
            b = g.sb("b", [P, NT])
            c = g.sb("c", [P, NT])
            sign = g.sb("sign", [P, NT])
            eq = g.sb("eq", [P, NT, E])
            order = g.sem("order")
            block = g.block()

            @block.vector
            def _(dve):
                o = InOrder(dve, order)
                o.step(nc.vector.tensor_tensor(a[:], k.h[:, :, 0], k.h[:, :, 1], ALU.add))
                o.step(nc.vector.tensor_scalar(sign[:], a[:], 0.0, None, ALU.is_ge))
                o.step(nc.vector.tensor_scalar(sign[:], sign[:], 2.0, -1.0, ALU.mult, ALU.add))
                o.step(nc.vector.tensor_tensor(a[:], a[:], sign[:], ALU.mult))
                floor(o, nc, b, a, c)
                o.step(nc.vector.tensor_tensor(a[:], b[:], sign[:], ALU.mult))
                for first in (True, False):
                    o.step(nc.vector.tensor_scalar(sign[:], a[:], 1.0 / E, None, ALU.mult))
                    floor(o, nc, b, sign, c)
                    o.step(nc.vector.scalar_tensor_tensor(out=a[:], in0=b[:], scalar=-float(E), in1=a[:],
                                                          op0=ALU.mult, op1=ALU.add))
                    if first:
                        o.step(nc.vector.tensor_tensor(gate[:], mid(k.iota[:, 0:E], NT), bc(a[:], [P, NT, E]), ALU.is_equal))
                        o.step(nc.vector.tensor_scalar(a[:], a[:], 1.0, None, ALU.add))
                o.step(nc.vector.tensor_tensor(eq[:], mid(k.iota[:, 0:E], NT), bc(a[:], [P, NT, E]), ALU.is_equal))
                o.step(nc.vector.tensor_tensor(gate[:], gate[:], eq[:], ALU.add))
                o.step(nc.vector.tensor_scalar(gate[:], gate[:], 0.5, None, ALU.mult))
        experts(k, E, F, lambda e: w1[:, e, :], lambda e, c: w2[:, e, c, :], ACT.Relu, gate,
                b1=lambda e, c: b1[:, e, c:c + 1], b2=lambda e: b2[:, e, :])


def floor(o, nc, out, a, tmp):
    o.step(nc.vector.tensor_scalar(out[:], a[:], ROUND, -ROUND, ALU.add, ALU.add))
    o.step(nc.vector.tensor_tensor(tmp[:], out[:], a[:], ALU.is_gt))
    o.step(nc.vector.tensor_tensor(out[:], out[:], tmp[:], ALU.subtract))


def choice_ffn(k):
    nc, dr = k.nc, k.dram
    E, F = 8, 256
    FC = F // P
    CAP = T // E
    with Stage(nc) as s:
        gate = s.sb("gate", [P, NT, E])
        wg = s.sb("wg", [P, E])
        w1 = s.sb("w1", [P, E, F])
        w2 = s.sb("w2", [P, E, FC, D])
        normalise(k, loads=[(wg[:], dr["L0_ffn_Wg"]),
                 (w1[:], dr["L0_ffn_W1"].rearrange("e d f -> d e f")),
                 (w2[:], dr["L0_ffn_W2"].rearrange("e (c p) d -> p e c d", p=P))])
        with Stage(nc) as g:
            probs = g.sb("probs", [P, NT, E])
            red = g.sb("red", [P, NT])
            by_expert = g.sb("by_expert", [E, 2, T])
            top8 = g.sb("top8", [E, 8])
            sel = g.sb("sel", [P, NT, E])
            cand = g.sb("cand", [P, NT, E])
            order = g.sem("order")
            logits = g.sem("logits")
            shifted = g.sem("shifted")
            powers = g.sem("powers")
            probs_ready = g.sem("probs_ready")
            turned = g.sem("turned")
            chosen = g.sem("chosen")
            back = g.sem("back")
            block = g.block()

            @block.tensor
            def _(pe):
                for t in range(NT):
                    last = nc.tensor.matmul(k.ps[:, 0, t * E:(t + 1) * E], k.hT[:, t * P:(t + 1) * P], wg[:],
                                            start=True, stop=True)
                last.then_inc(logits, 1)
                pe.wait_ge(probs_ready, 1)
                for t in range(NT):
                    last = nc.tensor.transpose(k.ps[0:E, 2 + t // 4, (t % 4) * P:(t % 4 + 1) * P], probs[:, t, :], k.ident[:])
                last.then_inc(turned, 1)
                pe.wait_ge(chosen, 1)
                for t in range(NT):
                    last = nc.tensor.transpose(k.ps[:, 1, t * E:(t + 1) * E], by_expert[:, 1, t * P:(t + 1) * P],
                                               k.ident[0:E, 0:E])
                last.then_inc(back, 1)

            @block.scalar
            def _(act):
                act.wait_ge(shifted, 1)
                nc.scalar.activation(probs[:], cand[:], ACT.Exp).then_inc(powers, 1)

            @block.vector
            def _(dve):
                o = InOrder(dve, order)
                lg = k.ps[:, 0, 0:NT * E].rearrange("p (t e) -> p t e", e=E)
                dve.wait_ge(logits, 1)
                o.step(nc.vector.tensor_reduce(red[:], lg, AX.X, ALU.max))
                nc.vector.tensor_tensor(cand[:], lg, bc(red[:], [P, NT, E]), ALU.subtract).then_inc(shifted, 1)
                dve.wait_ge(powers, 1)
                o.step(nc.vector.tensor_reduce(red[:], probs[:], AX.X, ALU.add))
                o.step(nc.vector.reciprocal(red[:], red[:]))
                nc.vector.tensor_tensor(probs[:], probs[:], bc(red[:], [P, NT, E]), ALU.mult).then_inc(probs_ready, 1)
                dve.wait_ge(turned, 1)
                o.step(nc.vector.tensor_copy(by_expert[:, 0, :], k.ps[0:E, 2:4, :].rearrange("p a b -> p (a b)")))
                for r in range(CAP // 8):
                    o.step(nc.vector.max(top8[:], by_expert[:, r % 2, :]))
                    o.step(nc.vector.match_replace(by_expert[:, (r + 1) % 2, :], top8[:], by_expert[:, r % 2, :], -1.0))
                nc.vector.tensor_scalar(by_expert[:, 1, :], by_expert[:, 0, :], 0.0, None, ALU.is_lt).then_inc(chosen, 1)
                dve.wait_ge(back, 1)
                o.step(nc.vector.tensor_copy(sel[:], k.ps[:, 1, 0:NT * E].rearrange("p (t e) -> p t e", e=E)))
                o.step(nc.vector.tensor_reduce(red[:], sel[:], AX.X, ALU.max))
                o.step(nc.vector.tensor_scalar(red[:], red[:], -1.0, 1.0, ALU.mult, ALU.add))
                o.step(nc.vector.tensor_tensor(sel[:], sel[:], bc(red[:], [P, NT, E]), ALU.max))
                o.step(nc.vector.tensor_tensor(cand[:], probs[:], sel[:], ALU.mult))
                o.step(nc.vector.scalar_tensor_tensor(out=cand[:], in0=sel[:], scalar=-1.0, in1=cand[:],
                                                      op0=ALU.add, op1=ALU.add))
                o.step(nc.vector.tensor_reduce(red[:], cand[:], AX.X, ALU.max))
                o.step(nc.vector.tensor_tensor(cand[:], cand[:], bc(red[:], [P, NT, E]), ALU.is_equal))
                o.step(nc.vector.scalar_tensor_tensor(out=cand[:], in0=cand[:], scalar=-100.0, in1=mid(k.iota[:, 0:E], NT),
                                                      op0=ALU.mult, op1=ALU.add))
                o.step(nc.vector.tensor_reduce(red[:], cand[:], AX.X, ALU.min))
                o.step(nc.vector.tensor_tensor(cand[:], cand[:], bc(red[:], [P, NT, E]), ALU.is_equal))
                o.step(nc.vector.tensor_tensor(gate[:], cand[:], probs[:], ALU.mult))
        experts(k, E, F, lambda e: w1[:, e, :], lambda e, c: w2[:, e, c, :], ACT.Gelu, gate)


def time_mix(k):
    nc, dr = k.nc, k.dram
    with Stage(nc) as outer:
        mixed = outer.sb("mixed", [P, 3, T])
        time_mix_average(k, mixed)
        project_add(k, mixed[:, 0, :], k.wT["L1_attn_W_output"][:])


def time_mix_average(k, mixed):
    nc, dr = k.nc, k.dram
    with Stage(nc) as s:
        col = s.sb("col", [P, 8])
        normalise(k, loads=[(col[:, 0:1], dr["L1_attn_time_decay"].rearrange("(p a) -> p a", a=1)),
                 (col[:, 1:2], dr["L1_attn_time_first"].rearrange("(p a) -> p a", a=1))] +
                [(col[:, 2 + i:3 + i], dr["L1_attn_time_mix_" + n].rearrange("a b (p c) -> p (a b c)", c=1))
                 for i, n in enumerate("kvr")])
        rest = s.sb("rest", [P, 3])
        decay = s.sb("decay", [P, 2])
        hs = s.sb("hs", [P, T + 1])
        kvr = s.sb("kvr", [P, 3, T])
        fall = s.sb("fall", [P, T])
        m = s.sb("m", [P, T + 1])
        keep = s.sb("keep", [P, T])
        new = s.sb("new", [P, T])
        newv = s.sb("newv", [P, T])
        num = s.sb("num", [P, T + 1])
        den = s.sb("den", [P, T + 1])
        c1 = s.sb("c1", [P, T])
        c2 = s.sb("c2", [P, T])
        top = s.sb("top", [P, T])
        uk = s.sb("uk", [P, T])
        order = s.sem("order")
        mixed_ready = s.sem("mixed_ready")
        product = s.sem("product")
        w_ready = s.sem("w_ready")
        to_power = s.sem("to_power")
        powers = s.sem("powers")
        block = s.block()

        @block.tensor
        def _(pe):
            for i, n in enumerate(("key", "value", "receptance")):
                pe.wait_ge(mixed_ready, i + 1)
                for b in range(2):
                    last = nc.tensor.matmul(k.ps[:, 2 * i + b, :], k.wT["L1_attn_W_" + n][:],
                                            mixed[:, i, b * BANK:(b + 1) * BANK], start=True, stop=True)
                last.then_inc(product, 1)

        @block.scalar
        def _(act):
            nc.scalar.activation(decay[:, 0:1], col[:, 0:1], ACT.Exp).then_inc(w_ready, 1)
            act.wait_ge(to_power, 1)
            nc.scalar.activation(keep[:], keep[:], ACT.Exp).then_inc(powers, 1)
            nc.scalar.activation(new[:], new[:], ACT.Exp).then_inc(powers, 1)
            act.wait_ge(to_power, 2)
            nc.scalar.activation(c1[:], c1[:], ACT.Exp).then_inc(powers, 1)
            nc.scalar.activation(c2[:], c2[:], ACT.Exp).then_inc(powers, 1)
            act.wait_ge(product, 3)
            nc.scalar.activation(kvr[:, 2, :], k.ps[:, 4:6, :].rearrange("p a b -> p (a b)"), ACT.Sigmoid).then_inc(powers, 1)

        @block.vector
        def _(dve):
            o = InOrder(dve, order)
            o.step(nc.vector.memset(hs[:, 0:1], 0.0))
            o.step(nc.vector.memset(m[:, 0:1], -1.0e38))
            o.step(nc.vector.memset(num[:, 0:1], 0.0))
            o.step(nc.vector.memset(den[:, 0:1], 0.0))
            o.step(nc.vector.tensor_copy(hs[:, 1:T + 1], k.hT[:]))
            o.step(nc.vector.tensor_scalar(rest[:], col[:, 2:5], -1.0, 1.0, ALU.mult, ALU.add))
            for i in range(3):
                o.step(nc.vector.tensor_scalar(mixed[:, i, :], hs[:, 0:T], rest[:, i:i + 1], None, ALU.mult))
                nc.vector.scalar_tensor_tensor(out=mixed[:, i, :], in0=k.hT[:], scalar=col[:, 2 + i:3 + i],
                                               in1=mixed[:, i, :], op0=ALU.mult, op1=ALU.add).then_inc(mixed_ready, 1)
            dve.wait_ge(w_ready, 1)
            o.step(nc.vector.tensor_scalar(decay[:, 1:2], decay[:, 0:1], -1.0, None, ALU.mult))
            o.step(nc.vector.memset(fall[:], 0.0))
            o.step(nc.vector.tensor_scalar(fall[:], fall[:], decay[:, 1:2], None, ALU.add))
            for i in range(2):
                dve.wait_ge(product, i + 1)
                o.step(nc.vector.tensor_copy(kvr[:, i, :], k.ps[:, 2 * i:2 * i + 2, :].rearrange("p a b -> p (a b)")))
            kk, vv = kvr[:, 0, :], kvr[:, 1, :]
            o.step(nc.vector.tensor_tensor_scan(m[:, 1:T + 1], fall[:], kk, -1.0e38, ALU.add, ALU.max))
            o.step(nc.vector.scalar_tensor_tensor(out=keep[:], in0=m[:, 0:T], scalar=decay[:, 1:2], in1=m[:, 1:T + 1],
                                                  op0=ALU.add, op1=ALU.subtract))
            nc.vector.tensor_tensor(new[:], kk, m[:, 1:T + 1], ALU.subtract).then_inc(to_power, 1)
            o.step(nc.vector.tensor_scalar(uk[:], kk, col[:, 1:2], None, ALU.add))
            o.step(nc.vector.tensor_tensor(top[:], uk[:], m[:, 0:T], ALU.max))
            o.step(nc.vector.tensor_tensor(c1[:], m[:, 0:T], top[:], ALU.subtract))
            nc.vector.tensor_tensor(c2[:], uk[:], top[:], ALU.subtract).then_inc(to_power, 1)
            dve.wait_ge(powers, 2)
            o.step(nc.vector.tensor_tensor(newv[:], new[:], vv, ALU.mult))
            o.step(nc.vector.tensor_tensor_scan(den[:, 1:T + 1], keep[:], new[:], 0.0, ALU.mult, ALU.add))
            o.step(nc.vector.tensor_tensor_scan(num[:, 1:T + 1], keep[:], newv[:], 0.0, ALU.mult, ALU.add))
            dve.wait_ge(powers, 4)
            o.step(nc.vector.tensor_tensor(num[:, 0:T], num[:, 0:T], c1[:], ALU.mult))
            o.step(nc.vector.tensor_tensor(den[:, 0:T], den[:, 0:T], c1[:], ALU.mult))
            o.step(nc.vector.tensor_tensor(newv[:], c2[:], vv, ALU.mult))
            o.step(nc.vector.tensor_tensor(num[:, 0:T], num[:, 0:T], newv[:], ALU.add))
            o.step(nc.vector.tensor_tensor(den[:, 0:T], den[:, 0:T], c2[:], ALU.add))
            o.step(nc.vector.reciprocal(den[:, 0:T], den[:, 0:T]))
            o.step(nc.vector.tensor_tensor(num[:, 0:T], num[:, 0:T], den[:, 0:T], ALU.mult))
            dve.wait_ge(powers, 5)
            o.step(nc.vector.tensor_tensor(mixed[:, 0, :], num[:, 0:T], kvr[:, 2, :], ALU.mult))


def linear_attention(k):
    nc, dr = k.nc, k.dram
    HH, HW = 8, 16
    with Stage(nc) as s:
        wrows = s.sb("wrows", [HW, 2 * HH, D])
        proj = s.sb("proj", [HW, HH, D])
        vrows = s.sb("vrows", [P, D])
        vT = s.sb("vT", [P, D])
        same = s.sb("same", [P, P])
        b_out = s.sb("b_out", [P, D])
        normalise(k, loads=[(wrows[:], dr["L2_attn_w_qkv"][0:2 * D].rearrange("(h j) i -> j h i", j=HW)),
                 (vrows[:], dr["L2_attn_w_qkv"][2 * D:3 * D]),
                 (proj[:], dr["L2_attn_proj"].rearrange("h j f -> j h f")),
                 (same[:], dr["c_same32"]), (b_out[:], row(k, "L2_attn_b_out", D))])
        folded = s.sb("folded", [P, 2 * HH, D])
        with Stage(nc) as g:
            product = g.sem("product")
            kept = g.sem("kept")
            block = g.block()

            @block.tensor
            def _(pe):
                for i in range(2 * HH):
                    last = nc.tensor.matmul(k.ps[:, i // 4, (i % 4) * P:(i % 4 + 1) * P], wrows[:, i, :],
                                            proj[:, i % HH, :], start=True, stop=True)
                    if i % 4 == 3:
                        last.then_inc(product, 1)
                nc.tensor.transpose(k.ps[:, 4, 0:P], vrows[:], k.ident[:]).then_inc(product, 1)

            @block.vector
            def _(dve):
                for b in range(4):
                    dve.wait_ge(product, b + 1)
                    nc.vector.tensor_copy(folded[:, 4 * b:4 * b + 4, :],
                                          k.ps[:, b, :].rearrange("p (i f) -> p i f", f=D)).then_inc(kept, 1)
                dve.wait_ge(product, 5)
                nc.vector.tensor_copy(vT[:], k.ps[:, 4, 0:P]).then_inc(kept, 1)
        v = s.sb("v", [P, NT, D])
        project(k, k.hT, NT, vT[:], D, v)
        out = s.sb("out", [P, NT, D])
        outT = s.sb("outT", [P, T])
        with Stage(nc) as g:
            v1 = g.sb("v1", [P, NT, HH, HW + 1])
            low = g.sb("low", [P, 2 * T])
            feat = g.sb("feat", [P, 2 * T])
            prod = g.sb("prod", [P, NT, P])
            z = g.sb("z", [P, NT])
            order = g.sem("order")
            qk = g.sem("qk")
            low_ready = g.sem("low_ready")
            powers = g.sem("powers")
            feat_ready = g.sem("feat_ready")
            scores = g.sem("scores")
            prod_ready = g.sem("prod_ready")
            sums = g.sem("sums")
            done = g.sem("done")
            block = g.block()

            @block.tensor
            def _(pe):
                for h in range(HH):
                    if h >= 1:
                        pe.wait_ge(feat_ready, h)
                    for i in range(2):
                        for b in range(2):
                            last = nc.tensor.matmul(k.ps[:, 2 * i + b, :], folded[:, i * HH + h, :],
                                                    k.hT[:, b * BANK:(b + 1) * BANK], start=True, stop=True)
                    last.then_inc(qk, 1)
                    pe.wait_ge(feat_ready, h + 1)
                    if h >= 1:
                        pe.wait_ge(prod_ready, h)
                    for t in range(NT):
                        last = nc.tensor.matmul(k.ps[:, 4 + t // 4, (t % 4) * P:(t % 4 + 1) * P],
                                                feat[:, T + t * P:T + (t + 1) * P], feat[:, t * P:(t + 1) * P],
                                                start=True, stop=True)
                    last.then_inc(scores, 1)
                    pe.wait_ge(prod_ready, h + 1)
                    if h >= 1:
                        pe.wait_ge(done, h)
                    for t in range(NT):
                        last = nc.tensor.matmul(k.ps[:, 6, t * 32:t * 32 + HW + 1], prod[:, t, :], v1[:, t, h, :],
                                                start=True, stop=True)
                    last.then_inc(sums, 1)

            @block.scalar
            def _(act):
                for h in range(HH):
                    act.wait_ge(low_ready, h + 1)
                    nc.scalar.activation(low[:], low[:], ACT.Exp).then_inc(powers, 1)

            @block.vector
            def _(dve):
                o = InOrder(dve, order)
                o.step(nc.vector.memset(v1[:], 1.0))
                o.step(nc.vector.tensor_copy(v1[:, :, :, 0:HW], v[:].rearrange("p t (h d) -> p t h d", h=HH)))
                for h in range(HH):
                    both = k.ps[:, 0:4, :].rearrange("p a b -> p (a b)")
                    dve.wait_ge(qk, h + 1)
                    nc.vector.tensor_scalar(low[:], both, 0.0, None, ALU.min).then_inc(low_ready, 1)
                    dve.wait_ge(powers, h + 1)
                    if h >= 1:
                        dve.wait_ge(scores, h)
                    nc.vector.scalar_tensor_tensor(out=feat[:], in0=both, scalar=0.0, in1=low[:],
                                                   op0=ALU.max, op1=ALU.add).then_inc(feat_ready, 1)
                    dve.wait_ge(scores, h + 1)
                    if h >= 1:
                        dve.wait_ge(sums, h)
                    for b in range(2):
                        last = nc.vector.tensor_tensor(prod[:, 4 * b:4 * b + 4, :],
                                                       k.ps[:, 4 + b, :].rearrange("p (t n) -> p t n", n=P),
                                                       mid(same[:], 4), ALU.mult)
                        if b == 0:
                            o.step(last)
                    last.then_inc(prod_ready, 1)
                    dve.wait_ge(sums, h + 1)
                    acc = k.ps[:, 6, 0:NT * 32].rearrange("p (t n) -> p t n", n=32)
                    o.step(nc.vector.tensor_scalar(z[:], acc[:, :, HW], 1e-8, None, ALU.add))
                    o.step(nc.vector.reciprocal(z[:], z[:]))
                    nc.vector.tensor_tensor(out[:, :, h * HW:(h + 1) * HW], acc[:, :, 0:HW], bc(z[:], [P, NT, HW]),
                                            ALU.mult).then_inc(done, 1)
                    dve.wait_ge(done, h + 1)
        turn(k, out, outT)
        project_add(k, outT, k.wT["L2_attn_w_out"][:], b_out[:])


def retention(k):
    nc, dr = k.nc, k.dram
    L, F, HH, HW = 4, 256, 8, 16
    with Stage(nc) as s:
        X = s.sb("X", [P, NT, D])
        table = s.sb("table", [P, 2, NT, 8])
        within = s.sb("within", [P, HH, P])
        powers_in = s.sb("powers_in", [P, 2, HH])
        blocks = s.sb("blocks", [P, P + 1])
        head_of = s.sb("head_of", [P, HH])
        ln = s.sb("ln", [P, 2, D])
        wide = s.sb("wide", [P, L, 4, D])
        wo = s.sb("wo", [P, L, D])
        gn = s.sb("gn", [P, 2, L * D])
        w1 = s.sb("w1", [P, L, F])
        w2 = s.sb("w2", [P, L, F // P, D])
        normalise(k, loads=[(table[:], dr["c_rot16"]), (within[:], dr["c_within"]), (powers_in[:], dr["c_powers"]),
                 (blocks[:], dr["c_blocks"]), (head_of[:], dr["c_head_of"]),
                 (ln[:, 0, :], row(k, "L3_attn_ln_scale", D)), (ln[:, 1, :], row(k, "L3_attn_ln_bias", D)),
                 (wo[:], dr["L3_attn_Wo"].rearrange("l p d -> p l d")),
                 (gn[:, 0, :], dr["L3_attn_gn_scale"].rearrange("l d -> (l d)").partition_broadcast(P)),
                 (gn[:, 1, :], dr["L3_attn_gn_bias"].rearrange("l d -> (l d)").partition_broadcast(P)),
                 (w1[:], dr["L3_attn_W1"].rearrange("l p f -> p l f"))] +
                [(w2[:, i], dr["L3_attn_W2"][i].rearrange("(c p) d -> p c d", p=P)) for i in range(L)] +
                [(wide[:, :, j, :], dr["L3_attn_W" + n].rearrange("l p d -> p l d")) for j, n in enumerate("qkvg")])
        with Stage(nc) as g:
            done = g.sem("done")
            block = g.block()

            @block.vector
            def _(dve):
                nc.vector.tensor_copy(X[:], k.h[:]).then_inc(done, 1)
        outer, k.x = k.x, X
        for i in range(L):
            normalise(k, (ln[:, 0, :], ln[:, 1, :]))
            retention_layer(k, wide[:, i], wo[:, i, :], gn[:, :, i * D:(i + 1) * D], table, within, powers_in, blocks, head_of)
            normalise(k, (ln[:, 0, :], ln[:, 1, :]))
            experts(k, 1, F, lambda e: w1[:, i, :], lambda e, c: w2[:, i, c, :], ACT.Gelu_apprx_tanh)
        k.x = outer
        with Stage(nc) as g:
            done = g.sem("done")
            block = g.block()

            @block.vector
            def _(dve):
                nc.vector.tensor_tensor(k.x[:], k.x[:], X[:], ALU.add).then_inc(done, 1)


def retention_layer(k, w, wo, gn, table, within, powers_in, blocks, head_of):
    nc, dr = k.nc, k.dram
    HH, HW = 8, 16
    with Stage(nc) as s:
        qkvg = s.sb("qkvg", [P, NT, 4 * D])
        project(k, k.hT, NT, w.rearrange("p a b -> p (a b)"), 4 * D, qkvg)
        rot = s.sb("rot", [P, 4, NT, D])
        out = s.sb("out", [P, NT, D])
        with Stage(nc) as g:
            t1 = g.sb("t1", [P, NT, 8 * 8])
            t2 = g.sb("t2", [P, NT, 8 * 8])
            turnedT = g.sb("turnedT", [P, 3, T])
            wide_q = g.sb("wide_q", [P, NT, HH, P])
            state = g.sb("state", [P, NT, D])
            prod = g.sb("prod", [P, 2, HH, P])
            kv = g.sb("kv", [P, NT, D])
            order = g.sem("order")
            rot_ready = g.sem("rot_ready")
            turned = g.sem("turned")
            turned_kept = g.sem("turned_kept")
            kv_product = g.sem("kv_product")
            state_ready = g.sem("state_ready")
            scores = g.sem("scores")
            prod_ready = g.sem("prod_ready")
            sums = g.sem("sums")
            taken = g.sem("taken")
            block = g.block()

            def half(ap, odd):
                return ap.rearrange("p t (h f two) -> p t h f two", h=HH, two=2)[:, :, :, :, odd]

            def four(ap):
                return ap[:].rearrange("p t (h f) -> p t h f", h=HH)

            @block.vector
            def _(dve):
                o = InOrder(dve, order)
                cos, sin = (table[:, a].unsqueeze(2).to_broadcast([P, NT, HH, 8]) for a in range(2))
                for j in range(2):
                    src = qkvg[:, :, j * D:(j + 1) * D]
                    x1, x2 = half(src, 0), half(src, 1)
                    o.step(nc.vector.tensor_tensor(four(t1), x1, cos, ALU.mult))
                    o.step(nc.vector.tensor_tensor(four(t2), x2, sin, ALU.mult))
                    o.step(nc.vector.tensor_tensor(half(rot[:, j], 0), four(t1), four(t2), ALU.subtract if j == 0 else ALU.add))
                    o.step(nc.vector.tensor_tensor(four(t1), x1, sin, ALU.mult))
                    o.step(nc.vector.tensor_tensor(four(t2), x2, cos, ALU.mult))
                    if j == 0:
                        o.step(nc.vector.tensor_tensor(half(rot[:, j], 1), four(t1), four(t2), ALU.add))
                    else:
                        o.step(nc.vector.tensor_tensor(half(rot[:, j], 1), four(t2), four(t1), ALU.subtract))
                for j in range(2):
                    wide = powers_in[:, j, :].unsqueeze(1).unsqueeze(3).to_broadcast([P, NT, HH, HW])
                    o.step(nc.vector.tensor_tensor(rot[:, 2 + j].rearrange("p t (h d) -> p t h d", h=HH),
                                                   rot[:, j].rearrange("p t (h d) -> p t h d", h=HH), wide, ALU.mult))
                nc.vector.memset(state[:, 0, :], 0.0).then_inc(rot_ready, 1)
                for a in range(3):
                    dve.wait_ge(turned, a + 1)
                    nc.vector.tensor_copy(turnedT[:, a, :], k.ps[:, 2 * a:2 * a + 2, :].rearrange("p a b -> p (a b)")).then_inc(turned_kept, 1)
                dve.wait_ge(turned_kept, 3)
                for h in range(HH):
                    nc.vector.tensor_scalar(wide_q[:, :, h, :], turnedT[:, 0, :].rearrange("p (t n) -> p t n", n=P),
                                            head_of[:, h:h + 1], None, ALU.mult).then_inc(turned_kept, 1)
                dve.wait_ge(kv_product, 1)
                for b in range(2):
                    o.step(nc.vector.tensor_tensor(kv[:, 4 * b:4 * b + 4, :],
                                                   k.ps[:, 6 + b, :].rearrange("p (t n) -> p t n", n=P),
                                                   mid(blocks[:, 0:P], 4), ALU.mult))
                for t in range(1, NT):
                    nc.vector.scalar_tensor_tensor(out=state[:, t, :], in0=state[:, t - 1, :], scalar=blocks[:, P:P + 1],
                                                   in1=kv[:, t - 1, :], op0=ALU.mult, op1=ALU.add).then_inc(state_ready, 1)
                    dve.wait_ge(state_ready, t)
                for t in range(NT):
                    dve.wait_ge(scores, t + 1)
                    if t >= 2:
                        dve.wait_ge(sums, t - 1)
                    nc.vector.tensor_tensor(prod[:, t % 2], k.ps[:, 2 * (t % 2):2 * (t % 2) + 2, :].rearrange("p a (h n) -> p (a h) n", n=P),
                                            within[:], ALU.mult).then_inc(prod_ready, 1)
                for b in range(2):
                    dve.wait_ge(sums, 4 * b + 4)
                    nc.vector.tensor_copy(out[:, 4 * b:4 * b + 4, :],
                                          k.ps[:, 4 + b, :].rearrange("p (t n) -> p t n", n=P)).then_inc(taken, 1)

            @block.tensor
            def _(pe):
                pe.wait_ge(rot_ready, 1)
                for a in range(3):
                    for t in range(NT):
                        last = nc.tensor.transpose(k.ps[:, 2 * a + t // 4, (t % 4) * P:(t % 4 + 1) * P], rot[:, a, t, :], k.ident[:])
                    last.then_inc(turned, 1)
                for t in range(NT):
                    last = nc.tensor.matmul(k.ps[:, 6 + t // 4, (t % 4) * P:(t % 4 + 1) * P], rot[:, 3, t, :],
                                            qkvg[:, t, 2 * D:3 * D], start=True, stop=True)
                last.then_inc(kv_product, 1)
                pe.wait_ge(turned_kept, 3 + HH)
                pe.wait_ge(state_ready, NT - 1)

                def weigh(t):
                    if t >= 2:
                        pe.wait_ge(prod_ready, t - 1)
                    for b in range(2):
                        last = nc.tensor.matmul(k.ps[:, 2 * (t % 2) + b, :], turnedT[:, 1, t * P:(t + 1) * P],
                                                wide_q[:, t, 4 * b:4 * b + 4, :], start=True, stop=True)
                    last.then_inc(scores, 1)

                def add_up(t):
                    acc = k.ps[:, 4 + t // 4, (t % 4) * P:(t % 4 + 1) * P]
                    nc.tensor.matmul(acc, turnedT[:, 2, t * P:(t + 1) * P], state[:, t, :], start=True, stop=False,
                                     skip_group_check=True)
                    pe.wait_ge(prod_ready, t + 1)
                    for h in range(HH):
                        last = nc.tensor.matmul(acc[:, h * HW:(h + 1) * HW], prod[:, t % 2, h, :],
                                                qkvg[:, t, 2 * D + h * HW:2 * D + (h + 1) * HW],
                                                start=False, stop=True, skip_group_check=True)
                    last.then_inc(sums, 1)

                for t in range(NT):
                    weigh(t)
                    if t >= 1:
                        add_up(t - 1)
                add_up(NT - 1)
        with Stage(nc) as g:
            red = g.sb("red", [P, NT * HH])
            sq = g.sb("sq", [P, NT * HH, HW])
            var = g.sb("var", [P, NT * HH])
            silu = g.sb("silu", [P, NT, D])
            order = g.sem("order")
            var_ready = g.sem("var_ready")
            roots = g.sem("roots")
            gated = g.sem("gated")
            block = g.block()
            y = out[:].rearrange("p t (h d) -> p (t h) d", d=HW)

            @block.scalar
            def _(act):
                nc.scalar.activation(silu[:], qkvg[:, :, 3 * D:4 * D], ACT.Silu).then_inc(gated, 1)
                act.wait_ge(var_ready, 1)
                nc.scalar.activation(var[:], var[:], ACT.Sqrt).then_inc(roots, 1)

            @block.vector
            def _(dve):
                o = InOrder(dve, order)
                o.step(nc.vector.tensor_reduce(red[:], y, AX.X, ALU.add))
                o.step(nc.vector.tensor_scalar(red[:], red[:], 1.0 / HW, None, ALU.mult))
                o.step(nc.vector.tensor_tensor(y, y, bc(red[:], [P, NT * HH, HW]), ALU.subtract))
                o.step(nc.vector.tensor_tensor(sq[:], y, y, ALU.mult))
                o.step(nc.vector.tensor_reduce(red[:], sq[:], AX.X, ALU.add))
                nc.vector.tensor_scalar(var[:], red[:], 1.0 / HW, 1e-5, ALU.mult, ALU.add).then_inc(var_ready, 1)
                dve.wait_ge(roots, 1)
                o.step(nc.vector.reciprocal(red[:], var[:]))
                o.step(nc.vector.tensor_tensor(y, y, bc(red[:], [P, NT * HH, HW]), ALU.mult))
                o.step(nc.vector.tensor_tensor(out[:], out[:], mid(gn[:, 0, :], NT), ALU.mult))
                o.step(nc.vector.tensor_tensor(out[:], out[:], mid(gn[:, 1, :], NT), ALU.add))
                dve.wait_ge(gated, 1)
                o.step(nc.vector.tensor_tensor(out[:], out[:], silu[:], ALU.mult))
        outT = s.sb("outT", [P, T])
        turn(k, out, outT)
        project_add(k, outT, wo)


def routed_ffn(k):
    nc, dr = k.nc, k.dram
    E, F, TOP = 32, 64, 4
    PLACES = 2 * (2 * 256) * TOP // E
    PAIRS = E // 2
    with Stage(nc) as s:
        gateT = s.sb("gateT", [E, T])
        spread = s.sb("spread", [E, PAIRS, P])
        wa = s.sb("wa", [P, E, F])
        wb = s.sb("wb", [P, E, F])
        wc = s.sb("wc", [P, PAIRS, D])
        with Stage(nc) as g:
            raw = g.sb("raw", [P, 3, E * F], BF16)
            before = g.sb("before", [P, P])
            bias = g.sb("bias", [P, E])
            normalise(k, loads=[(raw[:, 0, :].rearrange("p (e f) -> p e f", e=E), dr["L2_ffn_W1"].rearrange("e d f -> d e f")),
                     (raw[:, 1, :].rearrange("p (e f) -> p e f", e=E), dr["L2_ffn_W3"].rearrange("e d f -> d e f")),
                     (raw[:, 2, :].rearrange("p (e d) -> p e d", d=D), dr["L2_ffn_W2"].rearrange("(q b) i d -> (b i) q d", b=2)),
                     (before[:], dr["c_before"]), (bias[:], row(k, "L2_ffn_bias", E)), (spread[:], dr["c_spread"])])
            scores = g.sb("scores", [P, NT, E])
            keys = g.sb("keys", [P, NT, E])
            top8 = g.sb("top8", [P, NT, 8])
            place = g.sb("place", [P, NT, 8], U32)
            placef = g.sb("placef", [P, NT, 8])
            sel = g.sb("sel", [P, NT, E])
            eq = g.sb("eq", [P, NT, E])
            red = g.sb("red", [P, NT])
            order = g.sem("order")
            wide = g.sem("wide")
            logits = g.sem("logits")
            sig = g.sem("sig")
            sel_ready = g.sem("sel_ready")
            counts = g.sem("counts")
            gate_ready = g.sem("gate_ready")
            turned = g.sem("turned")
            block = g.block()

            @block.gpsimd
            def _(pool):
                nc.gpsimd.tensor_copy(wa[:].rearrange("p e f -> p (e f)"), raw[:, 0, :]).then_inc(wide, 1)
                nc.gpsimd.tensor_copy(wb[:].rearrange("p e f -> p (e f)"), raw[:, 1, :]).then_inc(wide, 1)
                nc.gpsimd.tensor_copy(wc[:].rearrange("p e f -> p (e f)"), raw[:, 2, :]).then_inc(wide, 1)

            @block.tensor
            def _(pe):
                for t in range(NT):
                    last = nc.tensor.matmul(k.ps[:, 0, t * E:(t + 1) * E], k.hT[:, t * P:(t + 1) * P],
                                            k.wT["L2_ffn_gate_w"][:], start=True, stop=True)
                last.then_inc(logits, 1)
                pe.wait_ge(sel_ready, 1)
                nc.tensor.matmul(k.ps[:, 1, 0:NT * E], before[:], sel[:].rearrange("p t e -> p (t e)"), start=True,
                                 stop=False, skip_group_check=True)
                for a in range(1, NT):
                    last = nc.tensor.matmul(k.ps[:, 1, a * E:NT * E], k.ones[:],
                                            sel[:, 0:NT - a, :].rearrange("p t e -> p (t e)"), start=False,
                                            stop=(a == NT - 1), skip_group_check=True)
                last.then_inc(counts, 1)
                pe.wait_ge(gate_ready, 1)
                for t in range(NT):
                    last = nc.tensor.transpose(k.ps[0:E, 2 + t // 4, (t % 4) * P:(t % 4 + 1) * P], sel[:, t, :], k.ident[:])
                last.then_inc(turned, 1)

            @block.scalar
            def _(act):
                act.wait_ge(logits, 1)
                nc.scalar.activation(scores[:].rearrange("p t e -> p (t e)"), k.ps[:, 0, 0:NT * E], ACT.Sigmoid).then_inc(sig, 1)

            @block.vector
            def _(dve):
                o = InOrder(dve, order)
                dve.wait_ge(sig, 1)
                o.step(nc.vector.tensor_tensor(keys[:], scores[:], mid(bias[:], NT), ALU.add))
                for t in range(NT):
                    o.step(nc.vector.max(top8[:, t, :], keys[:, t, :]))
                    o.step(nc.vector.max_index(place[:, t, :], top8[:, t, :], keys[:, t, :]))
                o.step(nc.vector.tensor_copy(placef[:], place[:]))
                for j in range(TOP):
                    dst = sel if j == 0 else eq
                    o.step(nc.vector.tensor_tensor(dst[:], mid(k.iota[:, 0:E], NT), bc(placef[:, :, j], [P, NT, E]), ALU.is_equal))
                    if j:
                        last = nc.vector.tensor_tensor(sel[:], sel[:], eq[:], ALU.add)
                        if j < TOP - 1:
                            o.step(last)
                last.then_inc(sel_ready, 1)
                dve.wait_ge(sel_ready, 1)
                o.step(nc.vector.tensor_tensor(scores[:], scores[:], sel[:], ALU.mult))
                o.step(nc.vector.tensor_reduce(red[:], scores[:], AX.X, ALU.add))
                o.step(nc.vector.tensor_scalar(red[:], red[:], 1e-12, None, ALU.max))
                o.step(nc.vector.reciprocal(red[:], red[:]))
                o.step(nc.vector.tensor_tensor(scores[:], scores[:], bc(red[:], [P, NT, E]), ALU.mult))
                dve.wait_ge(counts, 1)
                o.step(nc.vector.tensor_scalar(eq[:].rearrange("p t e -> p (t e)"), k.ps[:, 1, 0:NT * E], float(PLACES), None, ALU.is_lt))
                nc.vector.tensor_tensor(sel[:], scores[:], eq[:], ALU.mult).then_inc(gate_ready, 1)
                dve.wait_ge(turned, 1)
                o.step(nc.vector.tensor_copy(gateT[:], k.ps[0:E, 2:4, :].rearrange("p a b -> p (a b)")))
        with Stage(nc) as g:
            act_a = g.sb("act_a", [P, 2, T])
            hid = g.sb("hid", [P, 2, T])
            order = g.sem("order")
            up = g.sem("up")
            silu = g.sem("silu")
            product = g.sem("product")
            hid_ready = g.sem("hid_ready")
            used = g.sem("used")
            block = g.block()
            flat = [k.ps[:, 2 * a:2 * a + 2, :].rearrange("p a b -> p (a b)") for a in range(3)]

            @block.tensor
            def _(pe):
                def up_products(q):
                    if q >= 1:
                        pe.wait_ge(hid_ready, q)
                    m = P if q < PAIRS else F
                    for b in range(2):
                        ht = k.hT[:, b * BANK:(b + 1) * BANK]
                        a1 = wa[:, 2 * q:2 * q + 2, :] if q < PAIRS else k.wT["L2_ffn_sw1"][:]
                        a3 = wb[:, 2 * q:2 * q + 2, :] if q < PAIRS else k.wT["L2_ffn_sw3"][:]
                        nc.tensor.matmul(k.ps[0:m, b, :], a1, ht, start=True, stop=True)
                        last = nc.tensor.matmul(k.ps[0:m, 2 + b, :], a3, ht, start=True, stop=True)
                        if q < PAIRS:
                            last = nc.tensor.matmul(k.ps[:, 4 + b, :], spread[:, q, :], gateT[:, b * BANK:(b + 1) * BANK],
                                                    start=True, stop=True)
                    last.then_inc(up, 1)

                def down_product(q):
                    pe.wait_ge(hid_ready, q + 1)
                    for t in range(NT):
                        m = P if q < PAIRS else F
                        w = wc[:, q, :] if q < PAIRS else k.wT["L2_ffn_sw2"][:]
                        last = nc.tensor.matmul(k.ps[:, 6 + t // 4, (t % 4) * P:(t % 4 + 1) * P],
                                                hid[0:m, q % 2, t * P:(t + 1) * P], w, start=(q == 0 and t % 4 == 0), stop=(q == PAIRS),
                                                skip_group_check=True)
                    last.then_inc(used, 1)

                for q in range(PAIRS + 1):
                    up_products(q)
                    if q >= 1:
                        down_product(q - 1)
                down_product(PAIRS)

            @block.scalar
            def _(act):
                for q in range(PAIRS + 1):
                    m = P if q < PAIRS else F
                    act.wait_ge(up, q + 1)
                    if q >= 2:
                        act.wait_ge(hid_ready, q - 1)
                    nc.scalar.activation(act_a[0:m, q % 2, :], flat[0][0:m], ACT.Silu).then_inc(silu, 1)

            @block.vector
            def _(dve):
                for q in range(PAIRS + 1):
                    m = P if q < PAIRS else F
                    dve.wait_ge(silu, q + 1)
                    dve.wait_ge(up, q + 1)
                    if q >= 2:
                        dve.wait_ge(used, q - 1)
                    one = nc.vector.tensor_tensor(hid[0:m, q % 2, :], flat[1][0:m], act_a[0:m, q % 2, :], ALU.mult)
                    if q < PAIRS:
                        one.then_inc(product, 1)
                        dve.wait_ge(product, q + 1)
                        one = nc.vector.tensor_tensor(hid[:, q % 2, :], flat[2], hid[:, q % 2, :], ALU.mult)
                    one.then_inc(hid_ready, 1)
                o = InOrder(dve, order)
                for b in range(2):
                    part = k.x[:, 4 * b:4 * b + 4, :]
                    dve.wait_ge(used, PAIRS + 1)
                    o.step(nc.vector.tensor_tensor(part, part, k.ps[:, 6 + b, :].rearrange("p (t d) -> p t d", d=D), ALU.add))


PARTS = 6
ONE = PARTS * HD
SHIFT = ONE + 1
ROWS = SHIFT + 3
SLOT = 64
LOW8 = -57344.0
LOWER = 2.0 ** 14
BYTE8 = 251.0
STEP8 = 2.0 ** -8
PAIRS = H // 2


def attend(k, tiles, q, keys, values, out, key_mask=None, mask8=None, causal=False):
    nc = k.nc
    n_keys = tiles * P
    kgroups = [range(a, min(a + 8, tiles)) for a in range(0, tiles, 8)]
    chunks = [(a, min(a + BANK, n_keys)) for a in range(0, n_keys, BANK)]
    NC, NG = len(chunks), len(kgroups)

    def span(t, c):
        lo, hi = chunks[c]
        return lo, min(hi, (t + 1) * P) if causal else hi

    def first_query(t):
        return t * P if causal else 0

    prepare = ([("keys", g) for g in range(NG)] + [("queries", 0)] +
               [("chunk", a, t, c) for a in range(2) for t in range(NT) for c in range(NC) if span(t, c)[1] > span(t, c)[0]] +
               [("queries", 1)])
    G = len(prepare)
    FILL = 3 * (tiles - (4 if tiles > 2 * NT else 1))
    STEPS = 6 + (4 if mask8 is not None else 0)

    def before(p, a, b):
        if isinstance(p, int) and p == 0:
            return a
        return 2 * a + (p - 1) * (a + b)

    def items_of(p, par):
        first, last = isinstance(p, int) and p == 0, isinstance(p, int) and p == PAIRS - 1
        items = [] if last else [(item, p + 1, 1 - par) for item in prepare]
        return items if first else items[:NG] + [(("sums",), p - 1, 1 - par)] + items[NG:]

    def sums_place(p):
        return 0 if isinstance(p, int) and p == PAIRS - 1 else NG

    def phases(eng, phase, straight=False):
        phase(0, 0)
        if straight:
            for p in range(1, PAIRS):
                phase(p, p % 2)
            return
        with eng.Fori(0, PAIRS // 2 - 1) as i:
            phase(2 * i + 1, 1)
            phase(2 * i + 2, 0)
        phase(PAIRS - 1, 1)

    with Stage(nc) as s:
        kstack = s.sb("kstack", [P, tiles, 2, SLOT], BF16)
        qstack = s.sb("qstack", [P, 2, NT, 2, SLOT], BF16)
        kturned = s.sb("kturned", [P, 2, n_keys], BF16)
        qturned = s.sb("qturned", [P, 2, T], BF16)
        vstack = s.sb("vstack", [P, 2, tiles, 2, HD + 1])
        left = s.sb("left", [P, max(tiles, NT), 2, HD])
        probs = s.sb("probs", [P, 4, T])
        maxima = s.sb("maxima", [P, 2 * NT, NC])
        shift = s.sb("shift", [P, 2 * NT])
        shift_left = s.sb("shift_left", [P, 2 * NT])
        empty = s.sb("empty", [P, 2, 2 * NT])
        sums = s.sb("sums", [P, BANK])
        inverse = s.sb("inverse", [P, 2 * NT])
        junk = s.sb("junk", [P, 4, BANK], BF16)
        cleared = s.sem("cleared")
        first_order = s.sem("first_order")
        no_maxima = s.sem("no_maxima")
        pool_order = s.sem("pool_order")
        stacks_ready = s.sem("stacks_ready")
        values_ready = s.sem("values_ready")
        ring_filled = s.sem("ring_filled")
        ring_free = s.sem("ring_free")
        dve_order = s.sem("dve_order")
        shift_ready = s.sem("shift_ready")
        scores_filled = s.sem("scores_filled")
        probs_ready = s.sem("probs_ready")
        unit_done = s.sem("unit_done")
        sums_taken = s.sem("sums_taken")
        block = s.block()

        def ring(j):
            return 5 + j % 3

        def score_buffer(n):
            return k.ps[:, 2 * (n % 2):2 * (n % 2) + 2, :].rearrange("p a b -> p (a b)")

        N_CLEAR = 6 + (key_mask is not None)

        def split(e, o, src, stack, first, second, third, last_step=None):
            rest = left[:, 0:src.shape[1]]

            def slot(i):
                return stack[:, :, :, i * HD:(i + 1) * HD]
            o.step(e.tensor_copy(slot(first[0]), src))
            o.step(e.tensor_tensor(rest, src, slot(first[0]), ALU.subtract))
            o.step(e.tensor_copy(slot(second[0]), rest))
            o.step(e.tensor_tensor(rest, rest, slot(second[0]), ALU.subtract))
            o.step(e.tensor_copy(slot(third[0]), rest))
            copies = [(slot(i), slot(part[0])) for part in (first, second, third) for i in part[1:]]
            for dst, src2 in copies[:-1]:
                o.step(e.tensor_copy(dst, src2))
            return copies[-1]

        per_pair = 2 * 8 - 1

        def stacks(eng, e, o, pp, par):
            src = keys[:, :, 16 * pp:16 * pp + 16].rearrange("p t (a d) -> p t a d", a=2)
            dst, last = split(e, o, src, kstack, (0, 1, 2), (3, 4), (5,))
            o.step(e.tensor_copy(dst, last))
            src = q[:, :, 16 * pp:16 * pp + 16].rearrange("p t (a d) -> p t a d", a=2)
            dst, last = split(e, o, src, qstack[:, par], (0, 3, 5), (1, 4), (2,))
            e.tensor_copy(dst, last).then_inc(stacks_ready, 1)
            eng.wait_ge(stacks_ready, pp + 1)

        @block.gpsimd
        def _(pool):
            pool.wait_ge(cleared, N_CLEAR)

            def value_stack(pp, par):
                src = values[:, :, 16 * pp:16 * pp + 16].rearrange("p t (a d) -> p t a d", a=2)
                nc.gpsimd.tensor_copy(vstack[:, par, :, :, 0:HD], src).then_inc(values_ready, 1)

            def stacks_of(pp):
                stacks(pool, nc.gpsimd, InOrder(pool, pool_order, (pp - 1) * per_pair), pp, pp % 2)

            value_stack(0, 0)
            value_stack(1, 1)
            pool.wait_ge(ring_filled, NG)
            pool.wait_ge(stacks_ready, 1)
            stacks_of(1)
            for pp in range(2, PAIRS):
                pool.wait_ge(ring_filled, before(pp - 2, G, 1) + NG)
                stacks_of(pp)
                pool.wait_ge(unit_done, (pp - 1) * tiles)
                value_stack(pp, pp % 2)

        @block.tensor
        def _(pe):
            def ring_item(item, pp, par, base, j):
                bank = ring(j)
                pe.wait_ge(ring_free, base + max(j - 2, 0)) if not (isinstance(base, int) and base + max(j - 2, 0) == 0) else None
                turned = k.ps[:, bank, :].bitcast(BF16)
                if item[0] == "keys":
                    if item[1] == 0:
                        pe.wait_ge(stacks_ready, pp + 1)
                    for m, t in enumerate(kgroups[item[1]]):
                        last = nc.tensor.transpose(turned[:, m * P:(m + 1) * P],
                                                   kstack[:, t].rearrange("p a r -> p (a r)"), k.ident16[:])
                elif item[0] == "queries":
                    if item[1] == 1:
                        pe.wait_ge(shift_ready, pp + 1)
                    for t in range(NT):
                        last = nc.tensor.transpose(turned[:, t * P:(t + 1) * P],
                                                   qstack[:, par, t].rearrange("p a r -> p (a r)"), k.ident16[:])
                elif item[0] == "chunk":
                    _, a, t, c = item
                    if (a, t, c) == (0, 0, 0):
                        pe.wait_ge(ring_free, base + j)
                    lo, hi = span(t, c)
                    rows = slice(a * SLOT, a * SLOT + SHIFT)
                    last = nc.tensor.matmul(k.ps[:, bank, 0:hi - lo], qturned[rows, par, t * P:(t + 1) * P],
                                            kturned[rows, par, lo:hi], start=True, stop=True)
                else:
                    pe.wait_ge(sums_taken, 4 * (pp + 1))
                    for m in range(4):
                        last = nc.tensor.transpose(k.ps[:, bank, m * P:(m + 1) * P], sums[:, m * P:(m + 1) * P], k.ident[:])
                last.then_inc(ring_filled, 1)

            def scores(p, par, n):
                t, a = divmod(n, 2)
                if n >= 2 or not (isinstance(p, int) and p == 0):
                    pe.wait_ge(probs_ready, 2 * tiles * p + n - 1)
                rows = slice(a * SLOT, a * SLOT + ROWS)
                for b in range(2):
                    q0 = max(first_query(t) - b * BANK, 0)
                    if q0 >= BANK:
                        continue
                    masked = [] if mask8 is None else [t - 4 * b] if causal else range(4)
                    masked = [m for m in masked if 0 <= m < 4]
                    last = nc.tensor.matmul(k.ps[:, 2 * (n % 2) + b, q0:], kturned[rows, par, t * P:(t + 1) * P],
                                            qturned[rows, par, b * BANK + q0:(b + 1) * BANK], start=True,
                                            stop=not masked, skip_group_check=True)
                    for m in masked:
                        last = nc.tensor.matmul(k.ps[:, 2 * (n % 2) + b, m * P:(m + 1) * P],
                                                mask8[:, 4 * b + m, t * P:(t + 1) * P], k.lower[:],
                                                start=False, stop=True, skip_group_check=True)
                last.then_inc(scores_filled, 1)

            def weigh(p, par, t):
                if t == 0:
                    pe.wait_ge(values_ready, p + 1)
                    if not (isinstance(p, int) and p == 0):
                        pe.wait_ge(sums_taken, 4 * p)
                pe.wait_ge(probs_ready, 2 * tiles * p + 2 * t + 2)
                for a in range(2):
                    for b in range(2):
                        at = 32 * (2 * a + b)
                        q0 = max(first_query(t) - b * BANK, 0)
                        if q0 >= BANK:
                            continue
                        last = nc.tensor.matmul(k.ps[at:at + HD + 1, 4, q0:], vstack[:, par, t, a, :],
                                                probs[:, (2 * tiles * par + 2 * t + a) % 4, b * BANK + q0:(b + 1) * BANK],
                                                start=(t == 0), stop=(t == tiles - 1), skip_group_check=True)
                last.then_inc(unit_done, 1)

            for j, item in enumerate(prepare):
                ring_item(item, 0, 0, 0, j)

            def phase(p, par):
                base = before(p, G, 1)
                items = items_of(p, par)
                last_phase = isinstance(p, int) and p == PAIRS - 1
                spread = items if last_phase else items[:-1]
                at, third = 0, 0

                def some_items():
                    nonlocal at, third
                    third += 1
                    upto = min(len(spread), -(-len(spread) * third // FILL))
                    for j in range(at, upto):
                        ring_item(items[j][0], items[j][1], items[j][2], base, j)
                    at = upto

                for t in range(tiles):
                    more = t + 1 < tiles
                    some_items()
                    if more:
                        scores(p, par, 2 * t + 2)
                    some_items()
                    if more:
                        scores(p, par, 2 * t + 3)
                    some_items()
                    if t == tiles - 2 and not last_phase:
                        ring_item(items[-1][0], items[-1][1], items[-1][2], base, len(items) - 1)
                    if not more and not last_phase:
                        pe.wait_ge(ring_free, base + len(items))
                        scores(p + 1, 1 - par, 0)
                        scores(p + 1, 1 - par, 1)
                    weigh(p, par, t)

            pe.wait_ge(ring_free, G)
            scores(0, 0, 0)
            scores(0, 0, 1)
            phases(pe, phase)
            ring_item(("sums",), PAIRS - 1, 1, before(PAIRS - 1, G, 1) + 1, 0)

        @block.scalar
        def _(act):
            def phase(p, par):
                first = isinstance(p, int) and p == 0
                for n in range(2 * tiles):
                    act.wait_ge(scores_filled, 2 * tiles * p + n + 1)
                    if n >= 4 or not first:
                        act.wait_ge(unit_done, tiles * p + n // 2 - 1)
                    q0 = first_query(n // 2)
                    nc.scalar.activation(probs[:, (2 * tiles * par + n) % 4, q0:], score_buffer(n)[:, q0:], ACT.Exp,
                                         scale=(1.0 if mask8 is None else 1.0 / STEP8)).then_inc(probs_ready, 1)
                act.wait_ge(unit_done, tiles * (p + 1))
                if not first:
                    act.wait_ge(ring_filled, before(p, G, 1) + sums_place(p) + 1)
                for j in range(4):
                    nc.scalar.copy(sums[32 * j:32 * j + HD + 1, :], k.ps[32 * j:32 * j + HD + 1, 4, :]).then_inc(sums_taken, 1)

            phases(act, phase)

        @block.vector
        def _(dve):
            def ring_item(o, item, pp, par, base, j):
                bank = ring(j)
                dve.wait_ge(ring_filled, base + j + 1)
                turned = k.ps[:, bank, :].bitcast(BF16)
                if item[0] == "keys":
                    ts = kgroups[item[1]]
                    last = nc.vector.tensor_copy(kturned[:, par, ts[0] * P:(ts[-1] + 1) * P], turned[:, 0:len(ts) * P])
                elif item[0] == "queries":
                    last = nc.vector.tensor_copy(qturned[:, par, :], turned)
                elif item[0] == "chunk":
                    _, a, t, c = item
                    lo, hi = span(t, c)
                    dst = maxima[:, a * NT + t, c:c + 1]
                    if mask8 is None:
                        last = nc.vector.tensor_reduce(dst, k.ps[:, bank, 0:hi - lo], AX.X, ALU.max)
                    else:
                        if j >= 4:
                            dve.wait_ge(ring_free, base + j - 3)
                        last = nc.vector.tensor_tensor_reduce(junk[:, j % 4, 0:hi - lo], k.ps[:, bank, 0:hi - lo],
                                                              mask8[:, t, lo:hi].bitcast(mybir.dt.uint8), 1.0, -3.0e38,
                                                              ALU.subtract, ALU.max, dst)
                else:
                    acc = k.ps[:, bank, :].rearrange("p (m a b r) -> p a b m r", m=4, a=2, b=2)
                    inv = inverse[:].rearrange("p (a b m) -> p a b m", a=2, b=2)
                    o.step(nc.vector.reciprocal(inv, acc[:, :, :, :, HD]))
                    for a in range(2):
                        last = nc.vector.tensor_tensor(out[:, :, bass.ds(16 * pp + 8 * a, 8)].rearrange("p (b m) d -> p b m d", b=2),
                                                       acc[:, a, :, :, 0:HD], bc(inv[:, a], [P, 2, 4, HD]), ALU.mult)
                        if a == 0:
                            o.step(last)
                last.then_inc(ring_free, 1)
                if item == prepare[-2]:
                    dve.wait_ge(ring_free, base + j + 1)
                    place_shift(o, par)

            def place_shift(o, par):
                o.step(nc.vector.tensor_reduce(shift[:], maxima[:], AX.X, ALU.max, negate=True))
                if mask8 is not None:
                    o.step(nc.vector.tensor_scalar(empty[:, 0], shift[:], BYTE8 / 2, None, ALU.is_gt))
                    o.step(nc.vector.tensor_scalar(empty[:, 1], empty[:, 0], -1.0, 1.0, ALU.mult, ALU.add))
                    o.step(nc.vector.tensor_tensor(shift[:], shift[:], empty[:, 1], ALU.mult))
                    o.step(nc.vector.scalar_tensor_tensor(out=shift[:], in0=empty[:, 0], scalar=-LOW8 * LOWER, in1=shift[:],
                                                          op0=ALU.mult, op1=ALU.add))
                parts = [qstack[:, par, :, :, SHIFT + i].rearrange("p t a -> p a t") for i in range(3)]
                whole = shift[:].rearrange("p (a t) -> p a t", a=2)
                rest = shift_left[:].rearrange("p (a t) -> p a t", a=2)
                o.step(nc.vector.tensor_copy(parts[0], whole))
                o.step(nc.vector.tensor_tensor(rest, whole, parts[0], ALU.subtract))
                o.step(nc.vector.tensor_copy(parts[1], rest))
                o.step(nc.vector.tensor_tensor(rest, rest, parts[1], ALU.subtract))
                nc.vector.tensor_copy(parts[2], rest).then_inc(shift_ready, 1)

            nc.vector.memset(kstack[:], 0.0).then_inc(cleared, 1)
            nc.vector.memset(qstack[:], 0.0).then_inc(cleared, 1)
            nc.vector.memset(vstack[:], 1.0).then_inc(cleared, 1)
            nc.vector.memset(sums[:], 0.0).then_inc(cleared, 1)
            dve.wait_ge(cleared, 4)
            nc.vector.memset(kstack[:, :, :, SHIFT:ROWS], 1.0).then_inc(cleared, 1)
            nc.vector.memset(qstack[:, :, :, :, ONE:ONE + 1], 1.0).then_inc(cleared, 1)
            if key_mask is not None:
                nc.vector.tensor_copy(kstack[:, :, :, ONE], bc(key_mask, [P, tiles, 2])).then_inc(cleared, 1)
            dve.wait_ge(cleared, N_CLEAR)
            stacks(dve, nc.vector, InOrder(dve, first_order), 0, 0)
            if causal:
                nc.vector.memset(maxima[:], -3.0e38).then_inc(no_maxima, 1)
                dve.wait_ge(no_maxima, 1)
            PREP = STEPS - 1
            o = InOrder(dve, dve_order)
            for j, item in enumerate(prepare):
                ring_item(o, item, 0, 0, 0, j)
            assert o.n == PREP, o.n

            def phase(p, par):
                base = before(p, G, 1)
                o = InOrder(dve, dve_order, before(p, PREP, 2))
                items = items_of(p, par)
                for j, (item, pp, pr) in enumerate(items):
                    ring_item(o, item, pp, pr, base, j)

            phases(dve, phase, mask8 is not None)
            p = PAIRS - 1
            ring_item(InOrder(dve, dve_order, before(p, PREP, 2) + 2), ("sums",), p, 1, before(p, G, 1) + 1, 0)


def context_turned(k, s):
    nc = k.nc
    ctxT = s.sb("ctxT", [P, SP])
    full, rest = S // P, S % P
    groups = [range(a, min(a + 4, KT)) for a in range(0, KT, 4)]
    with Stage(nc) as g:
        rows = g.sb("rows", [P, KT, D])
        loaded = [g.sem(f"loaded{i}") for i in range(5)]
        zeroed = g.sem("zeroed")
        turned = g.sem("turned")
        kept = g.sem("kept")
        block = g.block()
        cuts = [0, 16, 32, full]

        @block.sync
        def _(sp):
            sp.wait_ge(zeroed, 1)
            sp.dma_start(rows[0:rest, full, :], k.dram["ctx_1024"][0, full * P:S]).then_inc(loaded[3], 16)
            for i in range(3):
                sp.dma_start(rows[:, cuts[i]:cuts[i + 1], :],
                             k.dram["ctx_1024"][0, cuts[i] * P:cuts[i + 1] * P].rearrange("(t p) d -> p t d", p=P)).then_inc(loaded[i], 16)

        @block.tensor
        def _(pe):
            for i, ts in enumerate(groups):
                for c in range(3):
                    if ts[0] == cuts[c]:
                        pe.wait_ge(loaded[c], 16)
                if ts[-1] == KT - 1:
                    pe.wait_ge(loaded[3], 16)
                if i >= NBANK:
                    pe.wait_ge(kept, i - NBANK + 1)
                for j, t in enumerate(ts):
                    last = nc.tensor.transpose(k.ps[:, i % NBANK, j * P:(j + 1) * P], rows[:, t, :], k.ident[:])
                last.then_inc(turned, 1)

        @block.vector
        def _(dve):
            nc.vector.memset(rows[:, full, :], 0.0).then_inc(zeroed, 1)
            for i, ts in enumerate(groups):
                dve.wait_ge(turned, i + 1)
                nc.vector.tensor_copy(ctxT[:, ts[0] * P:(ts[-1] + 1) * P], k.ps[:, i % NBANK, 0:len(ts) * P]).then_inc(kept, 1)
    return ctxT


def clear(k, aps):
    nc = k.nc
    with Stage(nc) as s:
        done = s.sem("done")
        block = s.block()

        @block.vector
        def _(dve):
            for ap in aps:
                nc.vector.memset(ap, 0).then_inc(done, 1)


def scale_by(k, ap, factor):
    nc = k.nc
    with Stage(nc) as s:
        done = s.sem("done")
        block = s.block()

        @block.vector
        def _(dve):
            nc.vector.tensor_scalar(ap, ap, factor, None, ALU.mult).then_inc(done, 1)


def masked_attention(k):
    nc, dr = k.nc, k.dram
    with Stage(nc) as s:
        q = k.h
        out = k.hT[:].rearrange("p (t d) -> p t d", t=NT)
        outT = k.h[:].rearrange("p t d -> p (t d)")
        bo = s.sb("bo", [P, D])
        ends = s.sb("ends", [P, KT])
        mask8 = s.sb("mask8", [P, NT, SP], FP8)
        normalise(k, loads=[(bo[:], row(k, "L1_xattn_bo", D)), (ends[:], dr["c_ends"])])
        project(k, k.hT, NT, k.wT["L1_xattn_Wq"][:], D, q)
        scale_by(k, q[:], HD ** -0.5 * STEP8)
        with Stage(nc) as g:
            raw = g.sb("raw", [P, 2, S], I32)
            loaded = [g.sem(f"loaded{i}") for i in range(2)]
            kept = g.sem("kept")
            block = g.block()

            @block.sync
            def _(sp):
                for t in range(NT):
                    if t >= 2:
                        sp.wait_ge(kept, t)
                    sp.dma_start(raw[:, t % 2, :], dr["mask_BxSxS2_if1"][0, t * P:(t + 1) * P]).then_inc(loaded[t % 2], 16)

            @block.vector
            def _(dve):
                nc.vector.memset(mask8[:, :, S:SP], 0.0).then_inc(kept, 1)
                for t in range(NT):
                    dve.wait_ge(loaded[t % 2], 16 * (t // 2 + 1))
                    nc.vector.tensor_scalar(mask8[:, t, 0:S].bitcast(mybir.dt.uint8), raw[:, t % 2, :], 0.0, BYTE8,
                                            ALU.is_equal, ALU.mult).then_inc(kept, 1)
        keys = s.sb("keys", [P, KT, D])
        values = s.sb("values", [P, KT, D])
        with Stage(nc) as g:
            ctxT = context_turned(k, g)
            project(k, ctxT, KT, k.wT["L1_xattn_Wk"][:], D, keys)
            project(k, ctxT, KT, k.wT["L1_xattn_Wv"][:], D, values)
        attend(k, KT, q, keys, values, out, ends[:], mask8)
        turn(k, out, outT)
        project_add(k, outT, k.wT["L1_xattn_Wo"][:], bo[:])


def cross_attention(k):
    nc, dr = k.nc, k.dram
    with Stage(nc) as s:
        q = s.sb("q", [P, NT, D])
        out = s.sb("out", [P, NT, D])
        wq = s.sb("wq", [P, D])
        wkv = s.sb("wkv", [P, 2 * D])
        wo = s.sb("wo", [P, D])
        bias = s.sb("bias", [P, 4, D])
        ends = s.sb("ends", [P, KT])
        maskb = s.sb("maskb", [P, KT], mybir.dt.uint8)
        full, rest = S // P, S % P
        clear(k, [maskb[:, full:full + 1]])
        normalise(k, loads=[(wq[:], dr["L2_xattn_q_w"]), (wkv[:], dr["L2_xattn_kv_w"]), (wo[:], dr["L2_xattn_proj_w"]),
                 (bias[:, 0, :], row(k, "L2_xattn_q_b", D)), (bias[:, 1, :], row(k, "L2_xattn_kv_b", D)),
                 (bias[:, 2, :], row(k, "L2_xattn_kv_b", D, D)), (bias[:, 3, :], row(k, "L2_xattn_proj_b", D)),
                 (ends[:], dr["c_ends"]), (maskb[:, 0:full], dr["mask_BxS2_bk0"][0, 0:full * P].rearrange("(t p) -> p t", p=P)),
                 (maskb[0:rest, full:full + 1], dr["mask_BxS2_bk0"][0, full * P:S].rearrange("(p a) -> p a", a=1))])
        with Stage(nc) as g:
            done = g.sem("done")
            block = g.block()

            @block.vector
            def _(dve):
                nc.vector.scalar_tensor_tensor(out=ends[:], in0=maskb[:], scalar=MINUS_INF, in1=ends[:],
                                               op0=ALU.mult, op1=ALU.min).then_inc(done, 1)
        project(k, k.hT, NT, wq[:], D, q, bias[:, 0, :])
        scale_by(k, q[:], HD ** -0.5)
        keys = s.sb("keys", [P, KT, D])
        values = s.sb("values", [P, KT, D])
        with Stage(nc) as g:
            ctxT = context_turned(k, g)
            project(k, ctxT, KT, wkv[:, 0:D], D, keys, bias[:, 1, :])
            project(k, ctxT, KT, wkv[:, D:2 * D], D, values, bias[:, 2, :])
        attend(k, KT, q, keys, values, out, ends[:])
        turn(k, out, k.hT)
        project_add(k, k.hT, wo[:], bias[:, 3, :])


def quantise(k, src, dstT, scale):
    nc = k.nc
    with Stage(nc) as s:
        inv = s.sb("inv", [P, NT])
        whole = s.sb("whole", [P, NT, D])
        order = s.sem("order")
        rounded = s.sem("rounded")
        turned = s.sem("turned")
        kept = s.sem("kept")
        block = s.block()

        @block.vector
        def _(dve):
            o = InOrder(dve, order)
            o.step(nc.vector.tensor_reduce(scale[:], src[:], AX.X, ALU.max, apply_absolute_value=True))
            o.step(nc.vector.tensor_scalar(scale[:], scale[:], 1e-8, 1.0 / 127.0, ALU.max, ALU.mult))
            o.step(nc.vector.reciprocal(inv[:], scale[:]))
            o.step(nc.vector.tensor_tensor(whole[:], src[:], bc(inv[:], [P, NT, D]), ALU.mult))
            o.step(nc.vector.tensor_scalar(whole[:], whole[:], 127.0, -128.0, ALU.min, ALU.max))
            nc.vector.tensor_scalar(whole[:], whole[:], ROUND, -ROUND, ALU.add, ALU.add).then_inc(rounded, 1)
            for b in range(2):
                dve.wait_ge(turned, b + 1)
                nc.vector.tensor_copy(dstT[:, b * BANK:(b + 1) * BANK], k.ps[:, b, :]).then_inc(kept, 1)

        @block.tensor
        def _(pe):
            pe.wait_ge(rounded, 1)
            for b in range(2):
                for j in range(4):
                    last = nc.tensor.transpose(k.ps[:, b, j * P:(j + 1) * P], whole[:, 4 * b + j, :], k.ident[:])
                last.then_inc(turned, 1)


def ternary_attention(k):
    nc, dr = k.nc, k.dram
    KVH = 4
    KVD = KVH * HD
    N = D + 2 * KVD
    names = [("Wq", D), ("Wk", KVD), ("Wv", KVD), ("Wp", D)]
    with Stage(nc) as s:
        wT = s.sb("wT", [P, N + D], BF16)
        alpha = s.sb("alpha", [P, 4])
        scale = s.sb("scale", [P, NT])
        gain = s.sb("gain", [P, H])
        table = s.sb("table", [P, 2, NT, HD // 2])
        mask8 = s.sb("mask8", [P, NT, T], FP8)
        intT = s.sb("intT", [P, T], BF16)
        q = s.sb("q", [P, NT, D])
        keys = s.sb("keys", [P, NT, D])
        values = s.sb("values", [P, NT, D])
        out = s.sb("out", [P, NT, D])
        with Stage(nc) as g:
            rows = g.sb("rows", [P, 4, D])
            later = g.sb("later", [P, P])
            total = g.sb("total", [P, 4])
            inv = g.sb("inv", [P, 4])
            normalise(k, loads=[(rows[0:r, i, :], dr["L0_attn_" + n]) for i, (n, r) in enumerate(names)] +
                      [(gain[:], row(k, "L0_attn_q_gain", H)), (table[:], dr["c_rot8"]), (later[:], dr["c_before"])])
            order = g.sem("order")
            summed = g.sem("summed")
            spread = g.sem("spread")
            rounded = g.sem("rounded")
            turned = g.sem("turned")
            kept = g.sem("kept")
            block = g.block()

            @block.vector
            def _(dve):
                o = InOrder(dve, order)
                o.step(nc.vector.memset(total[:], 0.0))
                bytes8 = mask8[:].bitcast(mybir.dt.uint8)
                for t in range(NT):
                    if t:
                        o.step(nc.vector.memset(bytes8[:, t, 0:t * P], 0))
                    o.step(nc.vector.tensor_scalar(bytes8[:, t, t * P:(t + 1) * P], later[:], BYTE8, None, ALU.mult))
                    if t < NT - 1:
                        o.step(nc.vector.memset(bytes8[:, t, (t + 1) * P:], int(BYTE8)))
                for i, (n, r) in enumerate(names):
                    last = nc.vector.tensor_reduce(total[0:r, i:i + 1], rows[0:r, i, :], AX.X, ALU.add, apply_absolute_value=True)
                    if i < 3:
                        o.step(last)
                last.then_inc(summed, 1)
                dve.wait_ge(spread, 1)
                for i, (n, r) in enumerate(names):
                    o.step(nc.vector.tensor_scalar(alpha[:, i:i + 1], k.ps[:, 0, i:i + 1], 1.0 / (r * D), 1e-8, ALU.mult, ALU.max))
                o.step(nc.vector.reciprocal(inv[:], alpha[:]))
                for i, (n, r) in enumerate(names):
                    w = rows[0:r, i, :]
                    o.step(nc.vector.tensor_scalar(w, w, inv[0:r, i:i + 1], 1.0, ALU.mult, ALU.min))
                    o.step(nc.vector.tensor_scalar(w, w, -1.0, ROUND, ALU.max, ALU.add))
                    last = nc.vector.tensor_scalar(w, w, -ROUND, None, ALU.add)
                    if i < 3:
                        o.step(last)
                last.then_inc(rounded, 1)
                dve.wait_ge(turned, 1)
                nc.vector.tensor_copy(wT[:], k.ps[:, 1, 0:N + D]).then_inc(kept, 1)

            @block.tensor
            def _(pe):
                pe.wait_ge(summed, 1)
                nc.tensor.matmul(k.ps[:, 0, 0:4], k.ones[:], total[:], start=True, stop=True).then_inc(spread, 1)
                pe.wait_ge(rounded, 1)
                at = 0
                for i, (n, r) in enumerate(names):
                    last = nc.tensor.transpose(k.ps[:, 1, at:at + r], rows[0:r, i, :], k.ident[0:r, 0:r])
                    at += r
                last.then_inc(turned, 1)
        quantise(k, k.h, intT, scale)
        with Stage(nc) as g:
            small = g.sb("small", [P, NT, 2 * KVD])
            square = g.sb("square", [P, NT, D + KVD])
            var = g.sb("var", [P, NT, H + KVH])
            turn1 = g.sb("turn1", [P, NT, D + KVD])
            t1 = g.sb("t1", [P, NT, H, HD // 2])
            t2 = g.sb("t2", [P, NT, H, HD // 2])
            order = g.sem("order")
            product = g.sem("product")
            var_ready = g.sem("var_ready")
            roots = g.sem("roots")
            block = g.block()

            @block.tensor
            def _(pe):
                for t in range(NT):
                    last = nc.tensor.matmul(k.ps[:, t // 2, (t % 2) * 256:(t % 2) * 256 + N], intT[:, t * P:(t + 1) * P],
                                            wT[:, 0:N], start=True, stop=True)
                last.then_inc(product, 1)

            @block.scalar
            def _(act):
                act.wait_ge(var_ready, 1)
                nc.scalar.activation(var[:], var[:], ACT.Sqrt).then_inc(roots, 1)

            @block.vector
            def _(dve):
                o = InOrder(dve, order)
                dve.wait_ge(product, 1)
                acc = k.ps[:, 0:4, :].rearrange("p b (j n) -> p (b j) n", j=2)
                o.step(nc.vector.tensor_tensor(q[:], acc[:, :, 0:D], bc(scale[:], [P, NT, D]), ALU.mult))
                o.step(nc.vector.tensor_tensor(small[:], acc[:, :, D:N], bc(scale[:], [P, NT, 2 * KVD]), ALU.mult))
                o.step(nc.vector.tensor_scalar(q[:], q[:], alpha[:, 0:1], None, ALU.mult))
                for i in range(2):
                    part = small[:, :, i * KVD:(i + 1) * KVD]
                    o.step(nc.vector.tensor_scalar(part, part, alpha[:, 1 + i:2 + i], None, ALU.mult))
                o.step(nc.vector.tensor_tensor(square[:, :, 0:D], q[:], q[:], ALU.mult))
                kk = small[:, :, 0:KVD]
                o.step(nc.vector.tensor_tensor(square[:, :, D:D + KVD], kk, kk, ALU.mult))
                o.step(nc.vector.tensor_reduce(var[:], square[:].rearrange("p t (h d) -> p t h d", d=HD), AX.X, ALU.add))
                nc.vector.tensor_scalar(var[:], var[:], 1.0 / HD, 1.1920929e-07, ALU.mult, ALU.add).then_inc(var_ready, 1)
                dve.wait_ge(roots, 1)
                o.step(nc.vector.reciprocal(var[:], var[:]))
                o.step(nc.vector.tensor_tensor(var[:, :, 0:H], var[:, :, 0:H], mid(gain[:], NT), ALU.mult))
                o.step(nc.vector.tensor_scalar(var[:, :, 0:H], var[:, :, 0:H], HD ** -0.5 * STEP8, None, ALU.mult))
                for src, heads, at, fac in ((q[:], H, 0, var[:, :, 0:H]), (kk, KVH, D, var[:, :, H:H + KVH])):
                    src4 = src.rearrange("p t (h d) -> p t h d", d=HD)
                    dst4 = turn1[:, :, at:at + heads * HD].rearrange("p t (h d) -> p t h d", d=HD)
                    half = HD // 2
                    cos, sin = (table[:, a].unsqueeze(2).to_broadcast([P, NT, heads, half]) for a in range(2))
                    x1, x2 = src4[:, :, :, 0:half], src4[:, :, :, half:HD]
                    u1, u2 = t1[:, :, 0:heads], t2[:, :, 0:heads]
                    o.step(nc.vector.tensor_tensor(u1, x1, cos, ALU.mult))
                    o.step(nc.vector.tensor_tensor(u2, x2, sin, ALU.mult))
                    o.step(nc.vector.tensor_tensor(dst4[:, :, :, 0:half], u1, u2, ALU.add))
                    o.step(nc.vector.tensor_tensor(u1, x1, sin, ALU.mult))
                    o.step(nc.vector.tensor_tensor(u2, x2, cos, ALU.mult))
                    o.step(nc.vector.tensor_tensor(dst4[:, :, :, half:HD], u2, u1, ALU.subtract))
                    o.step(nc.vector.tensor_tensor(dst4, dst4, fac.unsqueeze(3).to_broadcast([P, NT, heads, HD]), ALU.mult))
                o.step(nc.vector.tensor_copy(q[:], turn1[:, :, 0:D]))
                rep = H // KVH
                for h in range(KVH):
                    for dst, src in ((keys, turn1[:, :, D + h * HD:D + (h + 1) * HD]),
                                     (values, small[:, :, KVD + h * HD:KVD + (h + 1) * HD])):
                        o.step(nc.vector.tensor_copy(dst[:, :, h * rep * HD:(h + 1) * rep * HD].rearrange("p t (r d) -> p t r d", d=HD),
                                                     src.unsqueeze(2).to_broadcast([P, NT, rep, HD])))
        attend(k, NT, q, keys, values, out, None, mask8, causal=True)
        quantise(k, out, intT, scale)
        with Stage(nc) as g:
            order = g.sem("order")
            product = g.sem("product")
            block = g.block()

            @block.tensor
            def _(pe):
                for t in range(NT):
                    last = nc.tensor.matmul(k.ps[:, t // 4, (t % 4) * P:(t % 4 + 1) * P], intT[:, t * P:(t + 1) * P],
                                            wT[:, N:N + D], start=True, stop=True)
                last.then_inc(product, 1)

            @block.vector
            def _(dve):
                o = InOrder(dve, order)
                dve.wait_ge(product, 1)
                acc = k.ps[:, 0:2, :].rearrange("p b (j n) -> p (b j) n", j=4)
                o.step(nc.vector.tensor_tensor(out[:], acc, bc(scale[:], [P, NT, D]), ALU.mult))
                o.step(nc.vector.tensor_scalar(out[:], out[:], alpha[:, 3:4], None, ALU.mult))
                o.step(nc.vector.tensor_tensor(k.x[:], k.x[:], out[:], ALU.add))


def context_kernels(k, kern):
    nc, dr = k.nc, k.dram
    C, F = 2 * D, 64
    n = "L0_xattn_"
    with Stage(nc) as s:
        hist_w = s.sb("hist_w", [P, C])
        rows = s.sb("rows", [P, 3, C])
        w1 = s.sb("w1", [P, 2, F])
        b1 = s.sb("b1", [F, 1])
        w2 = s.sb("w2", [F, 1])
        b2 = s.sb("b2", [P, 1])
        kw1 = s.sb("kw1", [P, 2, D])
        kw2 = s.sb("kw2", [P, 9 * H])
        kb = s.sb("kb", [1, 3, D])
        kb2 = s.sb("kb2", [1, 9 * H])
        ends = s.sb("ends", [P, KT])
        load(k, [(hist_w[:], dr[n + "hist_W"]), (rows[:, 0, :], row(k, n + "hist_b", C)),
                 (rows[:, 1, :], row(k, n + "hist_ln_g", C)), (rows[:, 2, :], row(k, n + "hist_ln_b", C)),
                 (w1[:], dr[n + "ctx_W1"].rearrange("(c p) f -> p c f", p=P)),
                 (b1[:], dr[n + "ctx_b1"].rearrange("(p a) -> p a", a=1)), (w2[:], dr[n + "ctx_W2"]),
                 (b2[:], row(k, n + "ctx_b2", 1)), (kw1[:], dr[n + "kg_W1"].rearrange("(c p) f -> p c f", p=P)),
                 (kw2[:], dr[n + "kg_W2"])] +
                [(kb[:, i, :], dr[n + m].rearrange("(a d) -> a d", a=1)) for i, m in enumerate(("kg_b1", "kg_ln_g", "kg_ln_b"))] +
                [(kb2[:], dr[n + "kg_b2"].rearrange("(a d) -> a d", a=1)), (ends[:], dr["c_ends"])])
        eh = s.sb("eh", [P, KT, C])
        with Stage(nc) as g:
            ctxT = context_turned(k, g)
            square = g.sb("square", [P, 2, C])
            mean = g.sb("mean", [P, 2])
            red = g.sb("red", [P, KT])
            var = g.sb("var", [P, KT])
            order = g.sem("order")
            weights_ready = g.sem("weights_ready")
            product = g.sem("product")
            centred = g.sem("centred")
            squared = g.sem("squared")
            var_ready = g.sem("var_ready")
            roots = g.sem("roots")
            scaled = g.sem("scaled")
            shifted = g.sem("shifted")
            gelu = g.sem("gelu")
            block = g.block()
            pairs = [range(a, min(a + 2, KT)) for a in range(0, KT, 2)]
            parts = [range(a, min(a + 8, KT)) for a in range(0, KT, 8)]

            @block.tensor
            def _(pe):
                pe.wait_ge(weights_ready, 1)
                for i, ts in enumerate(pairs):
                    if i >= NBANK:
                        pe.wait_ge(centred, i - NBANK + 1)
                    for j, t in enumerate(ts):
                        last = nc.tensor.matmul(k.ps[:, i % NBANK, j * C:(j + 1) * C], ctxT[:, t * P:(t + 1) * P], hist_w[:],
                                                start=True, stop=True)
                    last.then_inc(product, 1)

            @block.vector
            def _(dve):
                o = InOrder(dve, order)
                o.step(nc.vector.tensor_reduce(mean[:, 0:1], hist_w[:], AX.X, ALU.add))
                o.step(nc.vector.tensor_reduce(mean[:, 1:2], rows[:, 0, :], AX.X, ALU.add))
                o.step(nc.vector.tensor_scalar(mean[:], mean[:], 1.0 / C, None, ALU.mult))
                o.step(nc.vector.tensor_scalar(rows[:, 0, :], rows[:, 0, :], mean[:, 1:2], None, ALU.subtract))
                nc.vector.tensor_scalar(hist_w[:], hist_w[:], mean[:, 0:1], None, ALU.subtract).then_inc(weights_ready, 1)
                for i, ts in enumerate(pairs):
                    dve.wait_ge(product, i + 1)
                    n = len(ts)
                    nc.vector.tensor_tensor(eh[:, ts[0]:ts[0] + n, :], k.ps[:, i % NBANK, 0:n * C].rearrange("p (t c) -> p t c", c=C),
                                            mid(rows[:, 0, :], n), ALU.add).then_inc(centred, 1)
                dve.wait_ge(squared, KT)
                nc.vector.tensor_scalar(var[:], red[:], 1.0 / C, 1e-5, ALU.mult, ALU.add).then_inc(var_ready, 1)
                dve.wait_ge(roots, 1)
                o.step(nc.vector.reciprocal(red[:], var[:]))
                for i, ts in enumerate(parts):
                    for t in ts:
                        nc.vector.scalar_tensor_tensor(out=eh[:, t, :], in0=eh[:, t, :], scalar=red[:, t:t + 1], in1=rows[:, 1, :],
                                                       op0=ALU.mult, op1=ALU.mult).then_inc(scaled, 1)
                    dve.wait_ge(scaled, ts[-1] + 1)
                    part = eh[:, ts[0]:ts[-1] + 1, :]
                    nc.vector.tensor_tensor(part, part, mid(rows[:, 2, :], len(ts)), ALU.add).then_inc(shifted, 1)

            @block.scalar
            def _(act):
                for t in range(KT):
                    act.wait_ge(centred, t // 2 + 1)
                    if t >= 2:
                        act.wait_ge(squared, t - 1)
                    nc.scalar.activation(square[:, t % 2, :], eh[:, t, :], ACT.Square, accum_out=red[:, t:t + 1]).then_inc(squared, 1)
                act.wait_ge(var_ready, 1)
                nc.scalar.activation(var[:], var[:], ACT.Sqrt).then_inc(roots, 1)
                for i, ts in enumerate(parts):
                    act.wait_ge(shifted, i + 1)
                    part = eh[:, ts[0]:ts[-1] + 1, :]
                    nc.scalar.activation(part, part, ACT.Gelu).then_inc(gelu, 1)
        weight = s.sb("weight", [P, KT])
        with Stage(nc) as g:
            ehT = g.sb("ehT", [P, 2, SP])
            hid = g.sb("hid", [F, SP])
            turned = g.sem("turned")
            turned_kept = g.sem("turned_kept")
            up = g.sem("up")
            hid_ready = g.sem("hid_ready")
            down = g.sem("down")
            order = g.sem("order")
            chunks = [(a, min(a + BANK, SP)) for a in range(0, SP, BANK)]
            groups = [(c, range(a, min(a + 4, KT))) for c in range(2) for a in range(0, KT, 4)]
            block = g.block()

            @block.tensor
            def _(pe):
                for i, (c, ts) in enumerate(groups):
                    if i >= 4:
                        pe.wait_ge(turned_kept, i - 3)
                    for j, t in enumerate(ts):
                        last = nc.tensor.transpose(k.ps[:, i % 4, j * P:(j + 1) * P], eh[:, t, c * P:(c + 1) * P], k.ident[:])
                    last.then_inc(turned, 1)
                pe.wait_ge(turned_kept, len(groups))
                for i, (lo, hi) in enumerate(chunks):
                    if i >= 3:
                        pe.wait_ge(hid_ready, i - 2)
                    for c in range(2):
                        last = nc.tensor.matmul(k.ps[0:F, 4 + i % 3, 0:hi - lo], w1[:, c, :], ehT[:, c, lo:hi],
                                                start=(c == 0), stop=(c == 1))
                    last.then_inc(up, 1)
                pe.wait_ge(hid_ready, len(chunks))
                for t in range(KT):
                    last = nc.tensor.matmul(k.ps[:, 7, t:t + 1], hid[:, t * P:(t + 1) * P], w2[:], start=True, stop=True)
                last.then_inc(down, 1)

            @block.scalar
            def _(act):
                for i, (lo, hi) in enumerate(chunks):
                    act.wait_ge(up, i + 1)
                    nc.scalar.activation(hid[:, lo:hi], k.ps[0:F, 4 + i % 3, 0:hi - lo], ACT.Gelu, bias=b1[:, 0:1]).then_inc(hid_ready, 1)

            @block.vector
            def _(dve):
                for i, (c, ts) in enumerate(groups):
                    dve.wait_ge(turned, i + 1)
                    nc.vector.tensor_copy(ehT[:, c, ts[0] * P:(ts[-1] + 1) * P], k.ps[:, i % 4, 0:len(ts) * P]).then_inc(turned_kept, 1)
                o = InOrder(dve, order)
                dve.wait_ge(down, 1)
                o.step(nc.vector.tensor_scalar(weight[:], k.ps[:, 7, 0:KT], b2[:, 0:1], None, ALU.add))
                o.step(nc.vector.tensor_tensor(weight[:], weight[:], ends[:], ALU.add))
        with Stage(nc) as g:
            top = g.sb("top", [P, 4])
            lane = g.sb("lane", [1, 2])
            acc = g.sb("acc", [P, 1])
            cc = g.sb("cc", [1, C])
            ccT = g.sb("ccT", [P, 2])
            z = g.sb("z", [1, D])
            zz = g.sb("zz", [1, D])
            st = g.sb("st", [1, 8])
            zT = g.sb("zT", [P, 1])
            ker = g.sb("ker", [1, 9 * H])
            red = g.sb("red", [1, H])
            order = g.sem("order")
            to_pe = g.sem("to_pe")
            from_pe = g.sem("from_pe")
            to_act = g.sem("to_act")
            from_act = g.sem("from_act")
            block = g.block()

            @block.vector
            def _(dve):
                o = InOrder(dve, order)
                nc.vector.tensor_reduce(top[:, 0:1], weight[:], AX.X, ALU.max).then_inc(to_pe, 1)
                dve.wait_ge(from_pe, 1)
                nc.vector.tensor_reduce(lane[:, 0:1], k.ps[0:1, 0, 0:P], AX.X, ALU.max, negate=True).then_inc(to_pe, 1)
                dve.wait_ge(from_pe, 2)
                nc.vector.tensor_copy(top[:, 1:2], k.ps[:, 1, 0:1]).then_inc(to_act, 1)
                dve.wait_ge(from_pe, 3)
                o.step(nc.vector.reciprocal(lane[:, 1:2], k.ps[0:1, 2, C:C + 1]))
                nc.vector.tensor_scalar(cc[:], k.ps[0:1, 2, 0:C], lane[:, 1:2], None, ALU.mult).then_inc(to_pe, 1)
                dve.wait_ge(from_pe, 4)
                nc.vector.tensor_copy(ccT[:], k.ps[:, 3, 0:2]).then_inc(to_pe, 1)
                dve.wait_ge(from_pe, 5)
                o.step(nc.vector.tensor_tensor(z[:], k.ps[0:1, 4, 0:D], kb[:, 0, :], ALU.add))
                o.step(nc.vector.tensor_reduce(st[:, 0:1], z[:], AX.X, ALU.add))
                o.step(nc.vector.tensor_scalar(st[:, 1:2], st[:, 0:1], 1.0 / D, None, ALU.mult))
                o.step(nc.vector.tensor_scalar(z[:], z[:], st[:, 1:2], None, ALU.subtract))
                o.step(nc.vector.tensor_tensor(zz[:], z[:], z[:], ALU.mult))
                o.step(nc.vector.tensor_reduce(st[:, 2:3], zz[:], AX.X, ALU.add))
                nc.vector.tensor_scalar(st[:, 3:4], st[:, 2:3], 1.0 / D, 1e-5, ALU.mult, ALU.add).then_inc(to_act, 1)
                dve.wait_ge(from_act, 2)
                o.step(nc.vector.reciprocal(st[:, 5:6], st[:, 4:5]))
                o.step(nc.vector.tensor_scalar(z[:], z[:], st[:, 5:6], None, ALU.mult))
                o.step(nc.vector.tensor_tensor(z[:], z[:], kb[:, 1, :], ALU.mult))
                nc.vector.tensor_tensor(z[:], z[:], kb[:, 2, :], ALU.add).then_inc(to_act, 1)
                dve.wait_ge(from_pe, 6)
                nc.vector.tensor_copy(zT[:], k.ps[:, 5, 0:1]).then_inc(to_pe, 1)
                dve.wait_ge(from_pe, 7)
                o.step(nc.vector.tensor_tensor(ker[:], k.ps[0:1, 6, 0:9 * H], kb2[:], ALU.add))
                by_head = ker[:].rearrange("p (h j) -> p h j", h=H)
                o.step(nc.vector.tensor_reduce(red[:], by_head, AX.X, ALU.max))
                nc.vector.tensor_tensor(by_head, by_head, bc(red[:], [1, H, 9]), ALU.subtract).then_inc(to_act, 1)
                dve.wait_ge(from_act, 4)
                o.step(nc.vector.tensor_reduce(red[:], by_head, AX.X, ALU.add))
                o.step(nc.vector.reciprocal(red[:], red[:]))
                nc.vector.tensor_tensor(by_head, by_head, bc(red[:], [1, H, 9]), ALU.mult).then_inc(to_pe, 1)
                dve.wait_ge(from_pe, 8)
                nc.vector.tensor_copy(kern[:], k.ps[:, 7, 0:9 * H]).then_inc(to_act, 1)

            @block.scalar
            def _(act):
                act.wait_ge(to_act, 1)
                nc.scalar.activation(weight[:], weight[:], ACT.Exp, bias=top[:, 1:2], accum_out=top[:, 2:3]).then_inc(from_act, 1)
                act.wait_ge(to_act, 2)
                nc.scalar.activation(st[:, 4:5], st[:, 3:4], ACT.Sqrt).then_inc(from_act, 1)
                act.wait_ge(to_act, 3)
                nc.scalar.activation(z[:], z[:], ACT.Gelu).then_inc(from_act, 1)
                act.wait_ge(to_act, 4)
                nc.scalar.activation(ker[:], ker[:], ACT.Exp).then_inc(from_act, 1)

            @block.tensor
            def _(pe):
                pe.wait_ge(to_pe, 1)
                nc.tensor.transpose(k.ps[0:1, 0, 0:P], top[:, 0:1], k.ident[:]).then_inc(from_pe, 1)
                pe.wait_ge(to_pe, 2)
                nc.tensor.matmul(k.ps[:, 1, 0:1], k.ones[0:1, :], lane[:, 0:1], start=True, stop=True).then_inc(from_pe, 1)
                pe.wait_ge(from_act, 1)
                for t in range(KT):
                    nc.tensor.matmul(k.ps[0:1, 2, 0:C], weight[:, t:t + 1], eh[:, t, :], start=(t == 0), stop=(t == KT - 1))
                nc.tensor.matmul(k.ps[0:1, 2, C:C + 1], top[:, 2:3], k.ones[:, 0:1], start=True, stop=True).then_inc(from_pe, 1)
                pe.wait_ge(to_pe, 3)
                for c in range(2):
                    last = nc.tensor.transpose(k.ps[:, 3, c:c + 1], cc[:, c * P:(c + 1) * P], k.ident[0:1, 0:1])
                last.then_inc(from_pe, 1)
                pe.wait_ge(to_pe, 4)
                for c in range(2):
                    last = nc.tensor.matmul(k.ps[0:1, 4, 0:D], ccT[:, c:c + 1], kw1[:, c, :], start=(c == 0), stop=(c == 1))
                last.then_inc(from_pe, 1)
                pe.wait_ge(from_act, 3)
                nc.tensor.transpose(k.ps[:, 5, 0:1], z[:], k.ident[0:1, 0:1]).then_inc(from_pe, 1)
                pe.wait_ge(to_pe, 5)
                nc.tensor.matmul(k.ps[0:1, 6, 0:9 * H], zT[:], kw2[:], start=True, stop=True).then_inc(from_pe, 1)
                pe.wait_ge(to_pe, 6)
                nc.tensor.matmul(k.ps[:, 7, 0:9 * H], k.ones[0:1, :], ker[:], start=True, stop=True).then_inc(from_pe, 1)


def convolved_attention(k):
    nc, dr = k.nc, k.dram
    WIN = P - 2
    NW = (T + WIN - 1) // WIN
    last_out = T - (NW - 1) * WIN
    n = "L0_xattn_"
    with Stage(nc) as s:
        kern = s.sb("kern", [P, 9 * H])
        context_kernels(k, kern)
        w = s.sb("w", [P, 4, D])
        proj_b = s.sb("proj_b", [P, D])
        shifts = s.sb("shifts", [P, 3, WIN])
        sum4 = s.sb("sum4", [P, HD])
        keep = s.sb("keep", [P, NW, T], BF16)
        lose = s.sb("lose", [WIN, NW, T], BF16)
        QW = NW * WIN + 2
        qstack = s.sb("qstack", [ONE, H, QW], BF16)
        kstack = s.sb("kstack", [ONE, H, T], BF16)
        v = s.sb("v", [P, NT, H, 32])
        out = s.sb("out", [WIN, NW, D])
        with Stage(nc) as narrow:
            keep8 = narrow.sb("keep8", [P, NW, T], mybir.dt.uint8)
            lose8 = narrow.sb("lose8", [WIN, NW, T], mybir.dt.uint8)
            clear(k, [keep8[:, 0, :], keep8[:, NW - 1, :], lose8[:, NW - 1, :]])
            mask = dr["mask_SxS_bc0"]
            inner = mask[WIN - 1:WIN - 1 + (NW - 2) * WIN]
            loads = [(keep8[1:P, 0, :], mask[0:P - 1]), (keep8[0:last_out + 1, NW - 1, :], mask[T - last_out - 1:T]),
                     (lose8[0:last_out, NW - 1, :], mask[T - last_out:T]),
                     (lose8[:, 0:NW - 1, :], mask[0:(NW - 1) * WIN].rearrange("(w p) n -> p w n", p=WIN))]
            loads += [(keep8[:, i, :], mask[i * WIN - 1:i * WIN - 1 + P]) for i in range(1, NW - 1)]
            loads += [(w[:, i, :], dr[n + m]) for i, m in enumerate(("Wq", "Wk", "Wv", "proj_W"))]
            loads += [(proj_b[:], row(k, n + "proj_b", D)), (shifts[:], dr["c_shifts"]), (sum4[:], dr["c_sum4"])]
            normalise(k, loads=loads)
            with Stage(nc) as g:
                qT = g.sb("qT", [P, T])
                kT = g.sb("kT", [P, T])
                partsT = g.sb("partsT", [P, 2, 3, T], BF16)
                order = g.sem("order")
                product = g.sem("product")
                kept = g.sem("kept")
                zeroed = g.sem("zeroed")
                split = g.sem("split")
                stored = [g.sem(f"stored{i}") for i in range(2)]
                loaded = g.sem("loaded")
                block = g.block()

                @block.tensor
                def _(pe):
                    for i in range(2):
                        for b in range(2):
                            last = nc.tensor.matmul(k.ps[:, 2 * i + b, :], w[:, i, :], k.hT[:, b * BANK:(b + 1) * BANK],
                                                    start=True, stop=True)
                        last.then_inc(product, 1)
                    for t in range(NT):
                        last = nc.tensor.matmul(k.ps[:, 4 + t // 4, (t % 4) * P:(t % 4 + 1) * P], k.hT[:, t * P:(t + 1) * P],
                                                w[:, 2, :], start=True, stop=True)
                    last.then_inc(product, 1)

                @block.gpsimd
                def _(pool):
                    nc.gpsimd.memset(qstack[:, :, 0:1], 0.0).then_inc(zeroed, 1)
                    nc.gpsimd.memset(qstack[:, :, T + 1:QW], 0.0).then_inc(zeroed, 1)

                @block.vector
                def _(dve):
                    o = InOrder(dve, order)
                    for i, (src, factor) in enumerate(((qT, HD ** -0.5), (kT, 1.0))):
                        dve.wait_ge(product, i + 1)
                        o.step(nc.vector.tensor_scalar(src[:], k.ps[:, 2 * i:2 * i + 2, :].rearrange("p a b -> p (a b)"), factor, None,
                                                       ALU.mult))
                        o.step(nc.vector.tensor_copy(partsT[:, i, 0, :], src[:]))
                        o.step(nc.vector.tensor_tensor(src[:], src[:], partsT[:, i, 0, :], ALU.subtract))
                        o.step(nc.vector.tensor_copy(partsT[:, i, 1, :], src[:]))
                        o.step(nc.vector.tensor_tensor(src[:], src[:], partsT[:, i, 1, :], ALU.subtract))
                        nc.vector.tensor_copy(partsT[:, i, 2, :], src[:]).then_inc(split, 1)
                    o.step(nc.vector.memset(v[:], 0.0))
                    dve.wait_ge(product, 3)
                    for b in range(2):
                        nc.vector.tensor_copy(v[:, 4 * b:4 * b + 4, :, 0:HD],
                                              k.ps[:, 4 + b, :].rearrange("p (t h d) -> p t h d", t=4, h=H)).then_inc(kept, 1)
                    nc.vector.tensor_scalar(keep[:], keep8[:], -1.0, 1.0, ALU.mult, ALU.add).then_inc(kept, 1)
                    nc.vector.tensor_scalar(lose[:], lose8[:], MINUS_INF, None, ALU.mult).then_inc(kept, 1)

                @block.sync
                def _(sp):
                    for i in range(2):
                        sp.wait_ge(split, i + 1)
                        sp.dma_start(k.parts_dram[i].rearrange("j p t -> p j t"), partsT[:, i]).then_inc(stored[i], 16)
                    sp.wait_ge(zeroed, 2)
                    for i, (stack, at, use) in enumerate(((qstack, 1, (0, 1, 2, 0, 1, 0)), (kstack, 0, (0, 0, 0, 1, 1, 2)))):
                        sp.wait_ge(stored[i], 16)
                        for slot, part in enumerate(use):
                            sp.dma_start(stack[slot * HD:(slot + 1) * HD, :, at:at + T],
                                         k.parts_dram[i, part].rearrange("(h d) t -> d h t", h=H)).then_inc(loaded, 16)
                    sp.wait_ge(loaded, 16 * 2 * PARTS)
        planes(k, qstack, kstack, v, kern, shifts, sum4, keep, lose, out, WIN, NW)
        outT = s.sb("outT", [P, T])
        with Stage(nc) as g:
            turned = g.sem("turned")
            kept = g.sem("kept")
            block = g.block()

            @block.tensor
            def _(pe):
                for i in range(NW):
                    no = WIN if i < NW - 1 else last_out
                    last = nc.tensor.transpose(k.ps[:, i // 4, (i % 4) * P:(i % 4) * P + no], out[0:no, i, :], k.ident[0:no, 0:no])
                last.then_inc(turned, 1)

            @block.vector
            def _(dve):
                dve.wait_ge(turned, 1)
                for i in range(NW):
                    no = WIN if i < NW - 1 else last_out
                    nc.vector.tensor_copy(outT[:, i * WIN:i * WIN + no], k.ps[:, i // 4, (i % 4) * P:(i % 4) * P + no]).then_inc(kept, 1)
        project_add(k, outT, w[:, 3, :], proj_b[:])


def planes(k, qstack, kstack, v, kern, shifts, sum4, keep, lose, out, WIN, NW):
    nc = k.nc
    with Stage(nc) as s:
        shares = s.sb("shares", [P, 2, WIN])
        bands = s.sb("bands", [P, 2, 3, WIN])
        plane = s.sb("plane", [P, 3, T + 2])
        power = s.sb("power", [WIN, 3, T])
        top = s.sb("top", [WIN, 3, 2])
        total = s.sb("total", [WIN, 5, 2])
        powerT = s.sb("powerT", [P, 3, NT, P])
        cleared = s.sem("cleared")
        order = s.sem("order")
        head_order = s.sem("head_order")
        head_ready = s.sem("head_ready")
        scores = s.sem("scores")
        masked = s.sem("masked")
        mixed = s.sem("mixed")
        mixed_kept = s.sem("mixed_kept")
        top_ready = s.sem("top_ready")
        powers = s.sem("powers")
        turned = s.sem("turned")
        turned_kept = s.sem("turned_kept")
        shares_ready = s.sem("shares_ready")
        shares_kept = s.sem("shares_kept")
        sums = s.sem("sums")
        done = s.sem("done")
        block = s.block()

        def two(b):
            return k.ps[:, b:b + 2, :].rearrange("p a b -> p (a b)")

        def back(h, w, n):
            return (w - n) % NW, -1 if w < n else 0, not (isinstance(h, int) and h == 0 and w < n)

        @block.tensor
        def _(pe):
            def score(h, par, w, u):
                if not (isinstance(u, int) and u == 0):
                    pe.wait_ge(masked, u)
                for b in range(2):
                    last = nc.tensor.matmul(k.ps[:, b, :], qstack[:, h, w * WIN:w * WIN + P], kstack[:, h, b * BANK:(b + 1) * BANK],
                                            start=True, stop=True)
                last.then_inc(scores, 1)

            def mix(h, par, w, u):
                if w == 0:
                    pe.wait_ge(head_ready, h + 1)
                pe.wait_ge(masked, u + 1)
                if not (isinstance(u, int) and u == 0):
                    pe.wait_ge(mixed_kept, u)
                for b in range(2):
                    for c in range(3):
                        last = nc.tensor.matmul(k.ps[0:WIN, 2 + b, :], bands[:, par, c, :],
                                                plane[:, w % 3, b * BANK + c:b * BANK + c + BANK],
                                                start=(c == 0), stop=(c == 2))
                last.then_inc(mixed, 1)

            def turn_powers(w, u):
                pe.wait_ge(powers, u + 1)
                if not (isinstance(u, int) and u == 0):
                    pe.wait_ge(turned_kept, u)
                for t in range(NT):
                    last = nc.tensor.transpose(k.ps[:, 4 + t // 4, (t % 4) * P:(t % 4) * P + WIN],
                                               power[:, w % 3, t * P:(t + 1) * P], k.ident[0:WIN, 0:WIN])
                last.then_inc(turned, 1)

            def weigh(h, w, u):
                pe.wait_ge(turned_kept, u + 1)
                if u > 0:
                    pe.wait_ge(shares_kept, u)
                for t in range(NT):
                    last = nc.tensor.matmul(k.ps[32 * (t % 4):32 * (t % 4) + 32, 6, 0:WIN], v[:, t, h, :], powerT[:, w % 3, t, 0:WIN],
                                            start=(t < 4), stop=(t >= 4), skip_group_check=True)
                last.then_inc(shares_ready, 1)

            def add_up(u):
                pe.wait_ge(shares_kept, u + 1)
                if u > 0:
                    pe.wait_ge(done, u)
                nc.tensor.matmul(k.ps[0:WIN, 7, 0:HD], shares[:, u % 2, :], sum4[:], start=True, stop=True).then_inc(sums, 1)

            score(0, 0, 0, 0)

            def head(h, par):
                for w in range(NW):
                    u = h * NW + w
                    if w < NW - 1:
                        score(h, par, w + 1, u + 1)
                    elif not (isinstance(h, int) and h == H - 1):
                        score(h + 1, 1 - par, 0, u + 1)
                    mix(h, par, w, u)
                    pw, dh, there = back(h, w, 1)
                    if there:
                        turn_powers(pw, u - 1)
                    pw, dh, there = back(h, w, 2)
                    if there:
                        weigh(h + dh, pw, u - 2)
                    if u >= 3:
                        add_up(u - 3)

            for h in range(H):
                head(h, h % 2)
            U = H * NW
            turn_powers(NW - 1, U - 1)
            weigh(H - 1, NW - 2, U - 2)
            add_up(U - 3)
            add_up(U - 2)
            weigh(H - 1, NW - 1, U - 1)
            add_up(U - 1)

        @block.scalar
        def _(act):
            def keep_shares(u):
                act.wait_ge(shares_ready, u + 1)
                if u >= 2:
                    act.wait_ge(sums, u - 1)
                nc.scalar.copy(shares[:, u % 2, :], k.ps[:, 6, 0:WIN]).then_inc(shares_kept, 1)

            for u in range(H * NW):
                w = u % NW
                act.wait_ge(top_ready, u + 1)
                if u >= 5:
                    act.wait_ge(done, u - 4)
                nc.scalar.activation(power[:, w % 3, :], power[:, w % 3, :], ACT.Exp, bias=top[:, w % 3, 1:2],
                                     accum_out=total[:, u % 5, 0:1]).then_inc(powers, 1)
                if u >= 2:
                    keep_shares(u - 2)
            keep_shares(H * NW - 2)
            keep_shares(H * NW - 1)

        @block.vector
        def _(dve):
            def prepare(h, par):
                o = InOrder(dve, head_order, h * 8)
                for a in range(3):
                    for c in range(3):
                        weight = kern[:, 9 * h + 3 * a + c:9 * h + 3 * a + c + 1]
                        if a == 0:
                            ins = nc.vector.tensor_scalar(bands[:, par, c, :], shifts[:, a, :], weight, None, ALU.mult)
                        else:
                            ins = nc.vector.scalar_tensor_tensor(out=bands[:, par, c, :], in0=shifts[:, a, :], scalar=weight,
                                                                 in1=bands[:, par, c, :], op0=ALU.mult, op1=ALU.add)
                        if (a, c) == (2, 2):
                            ins.then_inc(head_ready, 1)
                        else:
                            o.step(ins)

            def mask_out(w, u):
                dve.wait_ge(mixed, u + 1)
                if not (isinstance(u, int) and u < 3):
                    dve.wait_ge(turned, u - 2)
                nc.vector.tensor_tensor_reduce(power[:, w % 3, :], two(2)[0:WIN], lose[:, w, :], 1.0, -3.0e38,
                                               ALU.add, ALU.max, top[:, w % 3, 0:1]).then_inc(mixed_kept, 1)
                dve.wait_ge(mixed_kept, u + 1)
                nc.vector.tensor_scalar(top[:, w % 3, 1:2], top[:, w % 3, 0:1], -1.0, None, ALU.mult).then_inc(top_ready, 1)

            def keep_turned(w, u):
                dve.wait_ge(turned, u + 1)
                if not (isinstance(u, int) and u < 3):
                    dve.wait_ge(shares_ready, u - 2)
                nc.vector.tensor_copy(powerT[:, w % 3, :, 0:WIN], two(4).rearrange("p (t n) -> p t n", n=P)[:, :, 0:WIN]).then_inc(turned_kept, 1)

            def finish(h, w, u):
                dve.wait_ge(sums, u + 1)
                nc.vector.reciprocal(total[:, u % 5, 1:2], total[:, u % 5, 0:1]).then_inc(order, 1)
                dve.wait_ge(order, u + 1)
                nc.vector.tensor_scalar(out[:, w, h * HD:(h + 1) * HD], k.ps[0:WIN, 7, 0:HD], total[:, u % 5, 1:2], None,
                                        ALU.mult).then_inc(done, 1)

            nc.vector.memset(plane[:, :, 0:1], 0.0).then_inc(cleared, 1)
            nc.vector.memset(plane[:, :, T + 1:T + 2], 0.0).then_inc(cleared, 1)
            dve.wait_ge(cleared, 2)
            prepare(0, 0)

            def head(h, par):
                for w in range(NW):
                    u = h * NW + w
                    dve.wait_ge(scores, u + 1)
                    if not (isinstance(u, int) and u < 3):
                        dve.wait_ge(mixed, u - 2)
                    nc.vector.tensor_tensor(plane[:, w % 3, 1:T + 1], two(0), keep[:, w, :], ALU.mult).then_inc(masked, 1)
                    pw, dh, there = back(h, w, 1)
                    if there:
                        mask_out(pw, u - 1)
                    if w == 4 and not (isinstance(h, int) and h == H - 1):
                        prepare(h + 1, 1 - par)
                    pw, dh, there = back(h, w, 2)
                    if there:
                        keep_turned(pw, u - 2)
                    pw, dh, there = back(h, w, 4)
                    if there:
                        finish(h + dh, pw, u - 4)

            for h in range(H):
                head(h, h % 2)
            U = H * NW
            mask_out(NW - 1, U - 1)
            for n in (2, 1):
                keep_turned(NW - n, U - n)
            for n in (4, 3, 2, 1):
                finish(H - 1, NW - n, U - n)


def deformable_attention(k):
    nc, dr = k.nc, k.dram
    NK = 5
    HK = H * NK
    LINE = 4 * HD
    n = "L3_xattn_"
    table = k.table_dram
    with Stage(nc) as s:
        qp = s.sb("qp", [P, NT, D])
        index = s.sb("index", [P, NT, HK], U32)
        frac = s.sb("frac", [P, 2, NT, HK])
        bo = s.sb("bo", [P, D])
        normalise(k, loads=[(bo[:], row(k, n + "bo", D))])
        with Stage(nc) as g:
            bias = g.sb("bias", [P, 2, D])
            wkv = g.sb("wkv", [P, 2 * D])
            zero = g.sb("zero", [1, H * LINE])
            lines = g.sb("lines", [P, 3, H, 2, 2, HD])
            ctxz = g.sb("ctxz", [P, SP + P])
            load(k, [(bias[:, 0, :], row(k, n + "bk", D)), (bias[:, 1, :], row(k, n + "bv", D))])
            with Stage(nc) as f:
                ctxT = context_turned(k, f)
                with Stage(nc) as e:
                    done = e.sem("done")
                    block = e.block()

                    @block.vector
                    def _(dve):
                        nc.vector.memset(ctxz[:, 0:2], 0.0).then_inc(done, 1)
                        nc.vector.memset(ctxz[:, S + 2:SP + P], 0.0).then_inc(done, 1)
                        nc.vector.memset(zero[:], 0.0).then_inc(done, 1)
                        nc.vector.tensor_copy(wkv[:, 0:D], k.wT[n + "Wk"][:]).then_inc(done, 1)
                        nc.vector.tensor_copy(wkv[:, D:2 * D], k.wT[n + "Wv"][:]).then_inc(done, 1)
                        nc.vector.tensor_copy(ctxz[:, 2:S + 2], ctxT[:, 0:S]).then_inc(done, 1)
            with Stage(nc) as f:
                product = f.sem("product")
                line_ready = f.sem("line_ready")
                stored = [f.sem(f"stored{i}") for i in range(3)]
                block = f.block()

                @block.tensor
                def _(pe):
                    for t in range(KT):
                        if t >= 4:
                            pe.wait_ge(line_ready, 2 * (t - 3))
                        for nb in range(2):
                            last = nc.tensor.matmul(k.ps[:, 2 * (t % 4) + nb, 0:2 * D], ctxz[:, t * P + nb:t * P + nb + P], wkv[:],
                                                    start=True, stop=True)
                        last.then_inc(product, 1)

                @block.vector
                def _(dve):
                    both = bias[:].rearrange("p c (h d) -> p h c d", h=H)
                    for t in range(KT):
                        dve.wait_ge(product, t + 1)
                        if t >= 3:
                            dve.wait_ge(stored[t % 3], 16 * (t // 3))
                        for nb in range(2):
                            src = k.ps[:, 2 * (t % 4) + nb, 0:2 * D].rearrange("p (c h d) -> p h c d", c=2, h=H)
                            nc.vector.tensor_tensor(lines[:, t % 3, :, nb], src, both, ALU.add).then_inc(line_ready, 1)

                @block.sync
                def _(sp):
                    for t in range(KT):
                        sp.wait_ge(line_ready, 2 * t + 2)
                        sp.dma_start(table[t * P:(t + 1) * P, :],
                                     lines[:, t % 3].rearrange("p h a c d -> p (h a c d)")).then_inc(stored[t % 3], 16)
                    for i in range(3):
                        sp.wait_ge(stored[i], 16 * ((KT - i + 2) // 3))
                    half = zero[:, 0:H * LINE // 2].rearrange("p (h r) -> p h r", h=H)
                    def part(r, a):
                        return table[r:r + 1, :].rearrange("p (h a r) -> p h a r", h=H, a=2)[:, :, a, :]
                    for dst, src in ((table[0:1, :], zero[:]), (table[S + 2:S + 3, :], zero[:]), (part(1, 0), half), (part(S + 1, 1), half)):
                        sp.dma_start(dst, src).then_inc(stored[0], 16)
                    sp.wait_ge(stored[0], 16 * ((KT + 2) // 3 + 4))
        with Stage(nc) as g:
            bq = g.sb("bq", [P, D])
            boff = g.sb("boff", [P, HK])
            where = g.sb("where", [P, NT, HK])
            head_row = g.sb("head_row", [P, HK])
            mask = g.sb("mask", [P, KT], I32)
            qpT = g.sb("qpT", [P, T])
            pos = g.sb("pos", [P, NT, HK])
            a = g.sb("a", [P, NT, HK])
            b = g.sb("b", [P, NT, HK])
            c = g.sb("c", [P, NT, HK])
            full, rest = S // P, S % P
            load(k, [(bq[:], row(k, n + "bq", D)), (boff[:], row(k, n + "boff", HK)), (where[:], dr["c_where"]),
                     (head_row[:], dr["c_head_row"]), (mask[:, full:full + 1], dr["c_one32"])])
            load(k, [(mask[:, 0:full], dr["mask_BxS2_if0"][0, 0:full * P].rearrange("(t p) -> p t", p=P)),
                     (mask[0:rest, full:full + 1], dr["mask_BxS2_if0"][0, full * P:S].rearrange("(p a) -> p a", a=1))])
            project(k, k.hT, NT, k.wT[n + "Wq"][:], D, qp, bq[:])
            turn(k, qp, qpT)
            project(k, qpT, NT, k.wT[n + "Woff"][:], HK, pos, boff[:])
            with Stage(nc) as f:
                free = f.sb("free", [P, KT])
                few = f.sb("few", [P, 4])
                order = f.sem("order")
                counted = f.sem("counted")
                spread = f.sem("spread")
                block = f.block()

                @block.tensor
                def _(pe):
                    pe.wait_ge(counted, 1)
                    nc.tensor.matmul(k.ps[:, 0, 0:1], k.ones[:], few[:, 0:1], start=True, stop=True).then_inc(spread, 1)

                @block.vector
                def _(dve):
                    o = InOrder(dve, order)
                    o.step(nc.vector.tensor_scalar(free[:], mask[:], -1.0, 1.0, ALU.mult, ALU.add))
                    nc.vector.tensor_reduce(few[:, 0:1], free[:], AX.X, ALU.add).then_inc(counted, 1)
                    dve.wait_ge(spread, 1)
                    o.step(nc.vector.tensor_scalar(few[:, 1:2], k.ps[:, 0, 0:1], -1.0, None, ALU.add))
                    o.step(nc.vector.reciprocal(few[:, 2:3], few[:, 1:2]))
                    o.step(nc.vector.tensor_scalar(few[:, 3:4], few[:, 1:2], -1.0, None, ALU.mult))
                    o.step(nc.vector.tensor_tensor(pos[:], pos[:], where[:], ALU.add))
                    o.step(nc.vector.tensor_scalar(a[:], pos[:], few[:, 2:3], None, ALU.mult))
                    floor(o, nc, b, a, c)
                    o.step(nc.vector.scalar_tensor_tensor(out=pos[:], in0=b[:], scalar=few[:, 3:4], in1=pos[:], op0=ALU.mult, op1=ALU.add))
                    o.step(nc.vector.tensor_scalar(a[:], pos[:], few[:, 1:2], 0.0, ALU.mult, ALU.is_lt))
                    o.step(nc.vector.scalar_tensor_tensor(out=pos[:], in0=a[:], scalar=few[:, 1:2], in1=pos[:], op0=ALU.mult, op1=ALU.add))
                    o.step(nc.vector.tensor_scalar(pos[:], pos[:], 1.0 / (S - 1), 2.0, ALU.mult, ALU.mult))
                    o.step(nc.vector.tensor_scalar(pos[:], pos[:], -1.0, 1.0, ALU.add, ALU.add))
                    o.step(nc.vector.tensor_scalar(pos[:], pos[:], float(S), -1.0, ALU.mult, ALU.add))
                    o.step(nc.vector.tensor_scalar(pos[:], pos[:], 0.5, None, ALU.mult))
                    floor(o, nc, b, pos, c)
                    o.step(nc.vector.tensor_tensor(frac[:, 1], pos[:], b[:], ALU.subtract))
                    o.step(nc.vector.tensor_scalar(frac[:, 0], frac[:, 1], -1.0, 1.0, ALU.mult, ALU.add))
                    o.step(nc.vector.tensor_scalar(b[:], b[:], -2.0, float(S), ALU.max, ALU.min))
                    o.step(nc.vector.tensor_scalar(b[:], b[:], 2.0, float(H), ALU.add, ALU.mult))
                    o.step(nc.vector.tensor_tensor(b[:], b[:], mid(head_row[:], NT), ALU.add))
                    o.step(nc.vector.tensor_copy(index[:], b[:]))
        sampled_attention(k, qp, index, frac, table, NK, LINE)
        turn(k, qp, k.hT)
        project_add(k, k.hT, k.wT[n + "Wo"][:], bo[:])


def sampled_attention(k, qp, index, frac, table, NK, LINE):
    nc = k.nc
    HK = H * NK
    lines_of = table.rearrange("r (h c) -> (r h) c", h=H)
    with Stage(nc) as s:
        line = s.sb("line", [P, 2, HK, LINE])
        near = s.sb("near", [P, HK, 2 * HD])
        far = s.sb("far", [P, HK, 2 * HD])
        prod = s.sb("prod", [P, HK, HD])
        score = s.sb("score", [P, HK])
        red = s.sb("red", [P, H])
        gathered = [s.sem(f"gathered{i}") for i in range(2)]
        order = s.sem("order")
        used = s.sem("used")
        shifted = s.sem("shifted")
        powers = s.sem("powers")
        done = s.sem("done")
        block = s.block()

        @block.gpsimd
        def _(pool):
            for t in range(NT):
                if t >= 2:
                    pool.wait_ge(used, t - 1)
                for j in range(HK):
                    nc.gpsimd.indirect_dma_start(line[:, t % 2, j, :], None, lines_of,
                                                 bass.IndirectOffsetOnAxis(ap=index[:, t, j:j + 1], axis=0)).then_inc(gathered[t % 2], 16)

        @block.scalar
        def _(act):
            for t in range(NT):
                act.wait_ge(shifted, t + 1)
                nc.scalar.activation(score[:], score[:], ACT.Exp).then_inc(powers, 1)

        @block.vector
        def _(dve):
            o = InOrder(dve, order)
            by_head = score[:].rearrange("p (h j) -> p h j", h=H)
            for t in range(NT):
                dve.wait_ge(gathered[t % 2], 16 * HK * (t // 2 + 1))
                full = [P, HK, 2 * HD]
                o.step(nc.vector.tensor_tensor(near[:], line[:, t % 2, :, 0:2 * HD], bc(frac[:, 0, t, :], full), ALU.mult))
                nc.vector.tensor_tensor(far[:], line[:, t % 2, :, 2 * HD:LINE], bc(frac[:, 1, t, :], full), ALU.mult).then_inc(used, 1)
                dve.wait_ge(used, t + 1)
                o.step(nc.vector.tensor_tensor(near[:], near[:], far[:], ALU.add))
                q = qp[:, t, :].rearrange("p (h d) -> p h d", h=H).unsqueeze(2).to_broadcast([P, H, NK, HD])
                o.step(nc.vector.tensor_tensor(prod[:].rearrange("p (h j) d -> p h j d", h=H),
                                               near[:, :, 0:HD].rearrange("p (h j) d -> p h j d", h=H), q, ALU.mult))
                o.step(nc.vector.tensor_reduce(score[:], prod[:], AX.X, ALU.add))
                o.step(nc.vector.tensor_scalar(score[:], score[:], 0.5 * HD ** -0.5, None, ALU.mult))
                o.step(nc.vector.tensor_reduce(red[:], by_head, AX.X, ALU.max))
                nc.vector.tensor_tensor(by_head, by_head, bc(red[:], [P, H, NK]), ALU.subtract).then_inc(shifted, 1)
                dve.wait_ge(powers, t + 1)
                o.step(nc.vector.tensor_reduce(red[:], by_head, AX.X, ALU.add))
                o.step(nc.vector.reciprocal(red[:], red[:]))
                o.step(nc.vector.tensor_scalar(red[:], red[:], 0.5, None, ALU.mult))
                o.step(nc.vector.tensor_tensor(by_head, by_head, bc(red[:], [P, H, NK]), ALU.mult))
                o.step(nc.vector.tensor_tensor(prod[:], near[:, :, HD:2 * HD], bc(score[:], [P, HK, HD]), ALU.mult))
                o.step(nc.vector.tensor_reduce(qp[:, t, :].rearrange("p (h d) -> p h d", h=H),
                                               prod[:].rearrange("p (h j) d -> p h d j", h=H), AX.X, ALU.add))


SUBLAYERS = ["L0_attn", "L0_xattn", "L0_ffn", "L1_attn", "L1_xattn", "L1_ffn",
             "L2_attn", "L2_xattn", "L2_ffn", "L3_attn", "L3_xattn", "L3_ffn"]


def build(nc, dram, out, need=SUBLAYERS):
    k = Core(nc, dram)
    Stage.names = {}
    with k.ctx:
        k.x = k.sb("x_sb", [P, NT, D])
        k.h = k.sb("h", [P, NT, D])
        k.hT = k.sb("hT", [P, T])
        k.ident = k.sb("ident", [P, P])
        k.ident16 = k.sb("ident16", [P, P], BF16)
        k.lower = k.sb("lower", [P, P], BF16)
        k.iota = k.sb("iota", [P, P])
        k.ones = k.sb("ones", [P, P])
        k.ps = k.ctx.enter_context(nc.psum_tensor("ps", [P, NBANK, BANK], F32))
        k.table_dram = nc.dram_tensor("table", (SP, H * 4 * HD), F32, kind="Internal").ap()
        k.parts_dram = nc.dram_tensor("parts", (2, 3, P, T), BF16, kind="Internal").ap()
        setup(k, need)
        give_back(nc)
        for n in SUBLAYERS:
            if n in need:
                DO[n](k)
                give_back(nc)
        with Stage(nc) as s:
            stored = s.sem("stored")
            block = s.block()

            @block.sync
            def _(sp):
                sp.dma_start(out[0].rearrange("(t p) d -> p t d", p=P), k.x[:]).then_inc(stored, 16)
                sp.wait_ge(stored, 16)


DO = {"L0_attn": ternary_attention, "L0_xattn": convolved_attention, "L3_xattn": deformable_attention, "L1_xattn": masked_attention, "L2_xattn": cross_attention,
      "L0_ffn": choice_ffn, "L1_attn": time_mix, "L1_ffn": relu_ffn, "L2_attn": linear_attention,
      "L2_ffn": routed_ffn, "L3_attn": retention, "L3_ffn": hash_ffn}


def constants():
    import numpy as np
    f = np.float32
    c = {"c_ident": np.eye(P, dtype=f)}
    c["c_iota"] = np.tile(np.arange(P, dtype=f), (P, 1))
    i = np.arange(P)
    c["c_same32"] = (i[:, None] // 32 == i[None, :] // 32).astype(f)
    c["c_before"] = (i[:, None] < i[None, :]).astype(f)
    c["c_spread"] = (np.arange(32)[:, None, None] == 2 * np.arange(16)[None, :, None] + i[None, None, :] // 64).astype(f)
    pos = np.arange(T, dtype=f)

    def rotation(width):
        inv = (1.0 / f(10000.0) ** (np.arange(0, width, 2, dtype=f) / f(width))).astype(f)
        ang = pos[:, None] * inv[None, :]
        both = np.stack([np.cos(ang), np.sin(ang)]).astype(f)
        return np.ascontiguousarray(both.reshape(2, NT, P, width // 2).transpose(2, 0, 1, 3))

    c["c_rot16"] = rotation(16)
    c["c_rot8"] = rotation(HD)
    gammas = (1.0 - np.exp(np.linspace(np.log(1 / 32), np.log(1 / 64), 8)).astype(f)).astype(np.float64)
    diff = i[None, None, :] - i[:, None, None]
    c["c_within"] = np.where(diff >= 0, gammas[None, :, None] ** np.maximum(diff, 0), 0.0).astype(f)
    c["c_powers"] = np.stack([gammas[None, :] ** (i[:, None] + 1), gammas[None, :] ** (127 - i[:, None])], 1).astype(f)
    blocks = (i[:, None] // 16 == i[None, :] // 16).astype(f)
    c["c_blocks"] = np.concatenate([blocks, (gammas[i // 16] ** 128)[:, None].astype(f)], 1)
    c["c_head_of"] = (i[:, None] // 16 == np.arange(8)[None, :]).astype(f)
    c["c_sum4"] = (i[:, None] % 32 == np.arange(HD)[None, :]).astype(f)
    c["c_ends"] = np.where(np.arange(KT)[None, :] * P + i[:, None] < S, 0.0, MINUS_INF).astype(f)
    c["c_shifts"] = (i[:, None, None] == np.arange(P - 2)[None, None, :] + np.arange(3)[None, :, None]).astype(f)
    c["c_one32"] = np.ones((P, 1), np.int32)
    where = (np.arange(NT)[None, :, None] * P + i[:, None, None] + np.tile(np.arange(-3, 2), H)[None, None, :]).astype(f)
    c["c_where"] = where
    c["c_head_row"] = np.tile(np.repeat(np.arange(H), 5).astype(f), (P, 1))
    return c


def kernel(**inputs):
    import numpy as np
    import concourse.bacc as bacc
    from concourse.bass_utils import run_bass_kernel_spmd

    nc = bacc.Bacc("TRN2", target_bir_lowering=False, num_devices=1)
    arrays = {n: np.ascontiguousarray(a) for n, a in inputs.items()}
    arrays.update(constants())
    dram = {n: nc.dram_tensor("in_" + n, a.shape, mybir.dt.from_np(a.dtype), kind="ExternalInput").ap()
            for n, a in arrays.items()}
    out = nc.dram_tensor("out", (1, T, D), F32, kind="ExternalOutput").ap()
    build(nc, dram, out)
    r = run_bass_kernel_spmd(nc, [{"in_" + n: a for n, a in arrays.items()}], core_ids=[0])
    return r.results[0]["out"]
```
